# Optimizing a Trainium2 kernel written in Bass

```python
import numpy as np
import jax
import jax.numpy as jnp

def _softmax(x, axis=-1):
    return jax.nn.softmax(x, axis=axis)

def _gelu(x):
    return jax.nn.gelu(x, approximate=True)

def _silu(x):
    return jax.nn.silu(x)

def _sigmoid(x):
    return jax.nn.sigmoid(x)

def _layernorm(x, axis=-1, eps=1e-05):
    m = jnp.mean(x, axis=axis, keepdims=True)
    v = jnp.var(x, axis=axis, keepdims=True)
    return (x - m) / jnp.sqrt(v + eps)

def _scatter_add(tgt, idx, src, axis=0):
    return tgt.at[idx].add(src)

def _segment_sum(src, seg, n):
    return jax.ops.segment_sum(src, seg, n)
kernel_name = 'mk_macaron_d4_jaxref_r8_d0d5e8'

def setup_inputs(seed: int=0):
    np.random.seed(seed)
    _w = jnp.asarray

    def _L0_attn_setup():
        import jax, jax.numpy as jnp
        import numpy as np
        HEAD = 8
        BLOCK = 64
        D_MODEL = 128
        key = jax.random.key(seed)
        ks = jax.random.split(key, 9)
        d = D_MODEL
        s = 0.02
        return {'src': jax.random.normal(ks[0], (4, 512, d), dtype=jnp.float32), 'Wq': jax.random.normal(ks[1], (d, d), dtype=jnp.float32) * s, 'bq': jax.random.normal(ks[2], (d,), dtype=jnp.float32) * s, 'Wk': jax.random.normal(ks[3], (d, d), dtype=jnp.float32) * s, 'bk': jax.random.normal(ks[4], (d,), dtype=jnp.float32) * s, 'Wv': jax.random.normal(ks[5], (d, d), dtype=jnp.float32) * s, 'bv': jax.random.normal(ks[6], (d,), dtype=jnp.float32) * s, 'Wo': jax.random.normal(ks[7], (d, d), dtype=jnp.float32) * s, 'bo': jax.random.normal(ks[8], (d,), dtype=jnp.float32) * s}
    _L0_attn_in = _L0_attn_setup()

    def _L0_ffn_setup():
        import jax, jax.numpy as jnp
        import numpy as np
        TOPK = 8
        NUM_EXPERTS = 64
        FFN = 384
        CAPACITY = 160

        def _swiglu(x, w1, w2):
            h = x @ w1.T
            x1, x2 = jnp.split(h, 2, axis=-1)
            return x1 * jax.nn.silu(x2) @ w2.T
        key = jax.random.key(seed)
        ks = jax.random.split(key, 6)
        B, S, H = (1, 64, 128)
        scale = 0.02
        return {'hidden_states': jax.random.normal(ks[0], (B, S, H), jnp.float32), 'wg': jax.random.normal(ks[1], (NUM_EXPERTS, H), jnp.float32) * scale, 'shared_w1': jax.random.normal(ks[2], (2 * FFN, H), jnp.float32) * scale, 'shared_w2': jax.random.normal(ks[3], (H, FFN), jnp.float32) * scale, 'expert_w1': jax.random.normal(ks[4], (NUM_EXPERTS, 2 * FFN, H), jnp.float32) * scale, 'expert_w2': jax.random.normal(ks[5], (NUM_EXPERTS, H, FFN), jnp.float32) * scale}
    _L0_ffn_in = _L0_ffn_setup()

    def _L1_attn_setup():
        import jax, jax.numpy as jnp
        import numpy as np
        B, L, D, N = (8, 128, 128, 32)
        DT_MIN, DT_MAX = (0.001, 0.1)
        key = jax.random.key(seed)
        ks = jax.random.split(key, 12)
        s = 1.0 / np.sqrt(D)
        inp = {'x': jax.random.normal(ks[0], (B, L, D), jnp.float32), 'in_W': jax.random.uniform(ks[1], (D, D), jnp.float32, -s, s), 'in_b': jax.random.uniform(ks[2], (D,), jnp.float32, -s, s), 'log_dt': (np.log(DT_MIN) + jax.random.uniform(ks[3], (D,), jnp.float32) * (np.log(DT_MAX) - np.log(DT_MIN))).astype(jnp.float32), 'C': jax.random.normal(ks[4], (D, N, 2), jnp.float32), 'log_A_real': jnp.log(0.5 * jnp.ones((D, N), jnp.float32)), 'A_imag': jnp.tile((np.pi * jnp.arange(N, dtype=np.float32))[None, :], (D, 1)), 'D_skip': jax.random.normal(ks[5], (D,), jnp.float32), 'glu_W': jax.random.uniform(ks[6], (2 * D, D), jnp.float32, -s, s), 'glu_b': jax.random.uniform(ks[7], (2 * D,), jnp.float32, -s, s), 'out_W': jax.random.uniform(ks[8], (D, D), jnp.float32, -s, s), 'out_b': jax.random.uniform(ks[9], (D,), jnp.float32, -s, s)}
        return inp
    _L1_attn_in = _L1_attn_setup()

    def _L1_ffn_setup():
        import jax, jax.numpy as jnp
        import numpy as np
        D_MODEL, D_FF, RANK = (128, 512, 32)
        B, S = (4, 512)
        key = jax.random.key(seed)
        ks = jax.random.split(key, 7)
        return {'x': jax.random.normal(ks[0], (B, S, D_MODEL), dtype=jnp.float32), 'U1': jax.random.normal(ks[1], (D_MODEL, RANK), dtype=jnp.float32) * 0.02, 'V1': jax.random.normal(ks[2], (RANK, D_FF), dtype=jnp.float32) * 0.02, 'b1': jnp.zeros((D_FF,), dtype=jnp.float32), 'U2': jax.random.normal(ks[3], (D_FF, RANK), dtype=jnp.float32) * 0.02, 'V2': jax.random.normal(ks[4], (RANK, D_MODEL), dtype=jnp.float32) * 0.02, 'b2': jnp.zeros((D_MODEL,), dtype=jnp.float32)}
    _L1_ffn_in = _L1_ffn_setup()

    def _L2_attn_setup():
        import jax, jax.numpy as jnp
        import numpy as np
        D_MODEL = 128
        NUM_HEADS = 16
        HEAD_DIM = D_MODEL // NUM_HEADS
        WINDOW_SIZE = 64
        SEQ_LEN = 512
        BATCH = 1
        NUM_GLOBAL = 16

        def _sliding_window_mask(seq_len, global_idx):
            half_window = WINDOW_SIZE // 2
            pos = jnp.arange(seq_len)
            dist = pos[:, None] - pos[None, :]
            mask = jnp.abs(dist) <= half_window
            is_global = jnp.zeros((seq_len,), dtype=bool).at[global_idx].set(True)
            mask = mask | is_global[:, None] | is_global[None, :]
            return mask
        key = jax.random.key(seed)
        ks = jax.random.split(key, 6)
        hidden_states = jax.random.normal(ks[0], (BATCH, SEQ_LEN, D_MODEL), dtype=jnp.float32)
        s = 1.0 / np.sqrt(D_MODEL)
        Wq = jax.random.normal(ks[1], (D_MODEL, D_MODEL), dtype=jnp.float32) * s
        Wk = jax.random.normal(ks[2], (D_MODEL, D_MODEL), dtype=jnp.float32) * s
        Wv = jax.random.normal(ks[3], (D_MODEL, D_MODEL), dtype=jnp.float32) * s
        Wo = jax.random.normal(ks[4], (D_MODEL, D_MODEL), dtype=jnp.float32) * s
        global_token_indices = jax.random.randint(ks[5], (NUM_GLOBAL,), 0, SEQ_LEN, dtype=jnp.int64)
        return {'hidden_states': hidden_states, 'Wq': Wq, 'Wk': Wk, 'Wv': Wv, 'Wo': Wo, 'global_token_indices': global_token_indices}
    _L2_attn_in = _L2_attn_setup()

    def _L2_ffn_setup():
        import jax, jax.numpy as jnp
        import numpy as np
        EMB = 128
        FF = 4 * EMB

        def _ternary(w):
            scale = jnp.maximum(jnp.mean(jnp.abs(w)), 1e-08)
            w_t = jnp.clip(jnp.round(w / scale), -1.0, 1.0)
            return w + jax.lax.stop_gradient(w_t - w)
        key = jax.random.key(seed)
        kx, k1, k2, kb1, kb2 = jax.random.split(key, 5)
        x = jax.random.normal(kx, (4, 256, EMB), dtype=jnp.float32)
        lim1 = 1.0 / np.sqrt(EMB)
        lim2 = 1.0 / np.sqrt(FF)
        W1 = jax.random.uniform(k1, (FF, EMB), jnp.float32, -lim1, lim1)
        b1 = jax.random.uniform(kb1, (FF,), jnp.float32, -lim1, lim1)
        W2 = jax.random.uniform(k2, (EMB, FF), jnp.float32, -lim2, lim2)
        b2 = jax.random.uniform(kb2, (EMB,), jnp.float32, -lim2, lim2)
        return {'x': x, 'W1': W1, 'b1': b1, 'W2': W2, 'b2': b2}
    _L2_ffn_in = _L2_ffn_setup()

    def _L3_attn_setup():
        import jax, jax.numpy as jnp
        import numpy as np
        DIM = 128
        DI = 2 * DIM
        DSTATE = 16
        DCONV = 4
        DTRANK = DIM // 16
        B_, L = (2, 256)

        def _layernorm(x, w, b, eps=1e-05):
            mu = x.mean(-1, keepdims=True)
            var = ((x - mu) ** 2).mean(-1, keepdims=True)
            return (x - mu) * jax.lax.rsqrt(var + eps) * w + b

        def _silu(x):
            return x * jax.nn.sigmoid(x)

        def _mamba(x, in_proj_w, conv_w, conv_b, x_proj_w, dt_proj_w, dt_proj_b, A_log, D, out_proj_w):
            b, l, _ = x.shape
            xz = x @ in_proj_w.T
            xc, z = jnp.split(xz, 2, axis=-1)
            xt = jnp.pad(xc.transpose(0, 2, 1), ((0, 0), (0, 0), (DCONV - 1, 0)))
            xt = jax.lax.conv_general_dilated(xt, conv_w, (1,), 'VALID', dimension_numbers=('NCH', 'OIH', 'NCH'), feature_group_count=DI)
            xc = _silu(xt + conv_b[None, :, None]).transpose(0, 2, 1)
            dbc = xc @ x_proj_w.T
            dt = dbc[..., :DTRANK]
            Bm = dbc[..., DTRANK:DTRANK + DSTATE]
            Cm = dbc[..., DTRANK + DSTATE:]
            delta = jax.nn.softplus(dt @ dt_proj_w.T + dt_proj_b)
            A = -jnp.exp(A_log)
            dA = jnp.exp(delta[..., None] * A)
            dBu = (delta * xc)[..., None] * Bm[:, :, None, :]

            def step(h, inp):
                dA_t, dBu_t, C_t = inp
                h = dA_t * h + dBu_t
                return (h, jnp.einsum('bdn,bn->bd', h, C_t))
            h0 = jnp.zeros((b, DI, DSTATE), x.dtype)
            _, ys = jax.lax.scan(step, h0, (dA.transpose(1, 0, 2, 3), dBu.transpose(1, 0, 2, 3), Cm.transpose(1, 0, 2)))
            y = ys.transpose(1, 0, 2) + xc * D
            y = y * _silu(z)
            return y @ out_proj_w.T
        key = jax.random.key(seed)
        ks = jax.random.split(key, 8)
        s = lambda k, shape, sc=0.02: jax.random.normal(k, shape, jnp.float32) * sc
        return {'x': jax.random.normal(ks[0], (B_, L, DIM), jnp.float32), 'ln_w': jnp.ones((DIM,), jnp.float32), 'ln_b': jnp.zeros((DIM,), jnp.float32), 'in_proj_w': s(ks[1], (2 * DI, DIM)), 'conv_w': s(ks[2], (DI, 1, DCONV), 0.1), 'conv_b': jnp.zeros((DI,), jnp.float32), 'x_proj_w': s(ks[3], (DTRANK + 2 * DSTATE, DI)), 'dt_proj_w': s(ks[4], (DI, DTRANK), 0.1), 'dt_proj_b': jnp.log(jnp.expm1(jnp.full((DI,), 0.01, jnp.float32))), 'A_log': jnp.log(jnp.broadcast_to(jnp.arange(1, DSTATE + 1, dtype=jnp.float32), (DI, DSTATE))), 'D': jnp.ones((DI,), jnp.float32), 'out_proj_w': s(ks[5], (DIM, DI))}
    _L3_attn_in = _L3_attn_setup()

    def _L3_ffn_setup():
        import jax, jax.numpy as jnp
        import numpy as np
        D_MODEL = 128
        N_HEADS = 16
        N_KV = 4
        NUM_REP = N_HEADS // N_KV
        HEAD_DIM = D_MODEL // N_HEADS
        N_EXPERTS = 8
        TOP_K = 2
        CAP_FACTOR = 1.25
        EPS_NORM = 1e-06

        def _rmsnorm(x, w):
            var = jnp.mean(x * x, axis=-1, keepdims=True)
            return w * (x * jax.lax.rsqrt(var + EPS_NORM))

        def _gqa(x, qw, qb, kw, kb, vw, vb, ow, ob):
            B, S, D = x.shape
            q = (x @ qw + qb).reshape(B, S, N_HEADS, HEAD_DIM).transpose(0, 2, 1, 3)
            k = (x @ kw + kb).reshape(B, S, N_KV, HEAD_DIM).transpose(0, 2, 1, 3)
            v = (x @ vw + vb).reshape(B, S, N_KV, HEAD_DIM).transpose(0, 2, 1, 3)
            k = jnp.repeat(k, NUM_REP, axis=1)
            v = jnp.repeat(v, NUM_REP, axis=1)
            scores = jnp.einsum('bhqd,bhkd->bhqk', q, k) / np.sqrt(HEAD_DIM).astype(np.float32)
            attn = jax.nn.softmax(scores, axis=-1)
            out = jnp.einsum('bhqk,bhkd->bhqd', attn, v)
            out = out.transpose(0, 2, 1, 3).reshape(B, S, D)
            return out @ ow + ob

        def _moe(x, gate_w, w1, w2):
            B, S, D = x.shape
            T = B * S
            x_flat = x.reshape(T, D)
            capacity = int(CAP_FACTOR * T * TOP_K / N_EXPERTS)
            logits = x_flat @ gate_w
            probs = jax.nn.sigmoid(logits)
            _, sel = jax.lax.top_k(probs, TOP_K)
            w_topk = jnp.take_along_axis(probs, sel, axis=1)
            w_topk = w_topk / (jnp.sum(w_topk, axis=-1, keepdims=True) + 1e-06)
            flat_sel = sel.reshape(-1)
            em = jax.nn.one_hot(flat_sel, N_EXPERTS, dtype=jnp.int32)
            ranks = jnp.take_along_axis(jnp.cumsum(em, axis=0), flat_sel[:, None], axis=1)[:, 0] - 1
            valid = ranks < capacity
            slot = flat_sel * capacity + ranks
            scatter_idx = jnp.where(valid, slot, N_EXPERTS * capacity)
            x_rep = jnp.repeat(x_flat, TOP_K, axis=0)
            padded = jnp.zeros((N_EXPERTS * capacity + 1, D), x.dtype).at[scatter_idx].set(x_rep)
            padded_x = padded[:N_EXPERTS * capacity].reshape(N_EXPERTS, capacity, D)
            h = jax.nn.gelu(jnp.einsum('ecd,edf->ecf', padded_x, w1), approximate=False)
            out_padded = jnp.einsum('ecf,efd->ecd', h, w2).reshape(N_EXPERTS * capacity, D)
            gather_idx = jnp.where(valid, slot, 0)
            out_rep = jnp.where(valid[:, None], out_padded[gather_idx], 0.0)
            out_w = out_rep * w_topk.reshape(-1)[:, None]
            return out_w.reshape(T, TOP_K, D).sum(axis=1).reshape(B, S, D)
        key = jax.random.key(seed)
        ks = jax.random.split(key, 12)
        s = 0.02
        return {'x': jax.random.normal(ks[0], (4, 128, D_MODEL), jnp.float32), 'qw': jax.random.normal(ks[1], (D_MODEL, D_MODEL), jnp.float32) * s, 'qb': jnp.zeros((D_MODEL,), jnp.float32), 'kw': jax.random.normal(ks[2], (D_MODEL, N_KV * HEAD_DIM), jnp.float32) * s, 'kb': jnp.zeros((N_KV * HEAD_DIM,), jnp.float32), 'vw': jax.random.normal(ks[3], (D_MODEL, N_KV * HEAD_DIM), jnp.float32) * s, 'vb': jnp.zeros((N_KV * HEAD_DIM,), jnp.float32), 'ow': jax.random.normal(ks[4], (D_MODEL, D_MODEL), jnp.float32) * s, 'ob': jnp.zeros((D_MODEL,), jnp.float32), 'gate_w': jax.random.normal(ks[5], (D_MODEL, N_EXPERTS), jnp.float32) * s, 'w1': jax.random.normal(ks[6], (N_EXPERTS, D_MODEL, 256), jnp.float32) * s, 'w2': jax.random.normal(ks[7], (N_EXPERTS, 256, D_MODEL), jnp.float32) * s, 'norm1_w': jnp.ones((D_MODEL,), jnp.float32), 'norm2_w': jnp.ones((D_MODEL,), jnp.float32)}
    _L3_ffn_in = _L3_ffn_setup()
    _d = {'L0_attn_src': _L0_attn_in['src'], 'L0_attn_Wq': _L0_attn_in['Wq'], 'L0_attn_bq': _L0_attn_in['bq'], 'L0_attn_Wk': _L0_attn_in['Wk'], 'L0_attn_bk': _L0_attn_in['bk'], 'L0_attn_Wv': _L0_attn_in['Wv'], 'L0_attn_bv': _L0_attn_in['bv'], 'L0_attn_Wo': _L0_attn_in['Wo'], 'L0_attn_bo': _L0_attn_in['bo'], 'L0_ffn_wg': _L0_ffn_in['wg'], 'L0_ffn_shared_w1': _L0_ffn_in['shared_w1'], 'L0_ffn_shared_w2': _L0_ffn_in['shared_w2'], 'L0_ffn_expert_w1': _L0_ffn_in['expert_w1'], 'L0_ffn_expert_w2': _L0_ffn_in['expert_w2'], 'L1_attn_in_W': _L1_attn_in['in_W'], 'L1_attn_in_b': _L1_attn_in['in_b'], 'L1_attn_log_dt': _L1_attn_in['log_dt'], 'L1_attn_C': _L1_attn_in['C'], 'L1_attn_log_A_real': _L1_attn_in['log_A_real'], 'L1_attn_A_imag': _L1_attn_in['A_imag'], 'L1_attn_D_skip': _L1_attn_in['D_skip'], 'L1_attn_glu_W': _L1_attn_in['glu_W'], 'L1_attn_glu_b': _L1_attn_in['glu_b'], 'L1_attn_out_W': _L1_attn_in['out_W'], 'L1_attn_out_b': _L1_attn_in['out_b'], 'L1_ffn_U1': _L1_ffn_in['U1'], 'L1_ffn_V1': _L1_ffn_in['V1'], 'L1_ffn_b1': _L1_ffn_in['b1'], 'L1_ffn_U2': _L1_ffn_in['U2'], 'L1_ffn_V2': _L1_ffn_in['V2'], 'L1_ffn_b2': _L1_ffn_in['b2'], 'L2_attn_Wq': _L2_attn_in['Wq'], 'L2_attn_Wk': _L2_attn_in['Wk'], 'L2_attn_Wv': _L2_attn_in['Wv'], 'L2_attn_Wo': _L2_attn_in['Wo'], 'L2_attn_global_token_indices': _L2_attn_in['global_token_indices'], 'L2_ffn_W1': _L2_ffn_in['W1'], 'L2_ffn_b1': _L2_ffn_in['b1'], 'L2_ffn_W2': _L2_ffn_in['W2'], 'L2_ffn_b2': _L2_ffn_in['b2'], 'L3_attn_ln_w': _L3_attn_in['ln_w'], 'L3_attn_ln_b': _L3_attn_in['ln_b'], 'L3_attn_in_proj_w': _L3_attn_in['in_proj_w'], 'L3_attn_conv_w': _L3_attn_in['conv_w'], 'L3_attn_conv_b': _L3_attn_in['conv_b'], 'L3_attn_x_proj_w': _L3_attn_in['x_proj_w'], 'L3_attn_dt_proj_w': _L3_attn_in['dt_proj_w'], 'L3_attn_dt_proj_b': _L3_attn_in['dt_proj_b'], 'L3_attn_A_log': _L3_attn_in['A_log'], 'L3_attn_D': _L3_attn_in['D'], 'L3_attn_out_proj_w': _L3_attn_in['out_proj_w'], 'L3_ffn_qw': _L3_ffn_in['qw'], 'L3_ffn_qb': _L3_ffn_in['qb'], 'L3_ffn_kw': _L3_ffn_in['kw'], 'L3_ffn_kb': _L3_ffn_in['kb'], 'L3_ffn_vw': _L3_ffn_in['vw'], 'L3_ffn_vb': _L3_ffn_in['vb'], 'L3_ffn_ow': _L3_ffn_in['ow'], 'L3_ffn_ob': _L3_ffn_in['ob'], 'L3_ffn_gate_w': _L3_ffn_in['gate_w'], 'L3_ffn_w1': _L3_ffn_in['w1'], 'L3_ffn_w2': _L3_ffn_in['w2'], 'L3_ffn_norm1_w': _L3_ffn_in['norm1_w'], 'L3_ffn_norm2_w': _L3_ffn_in['norm2_w']}
    _x0 = _d['L0_attn_src']
    _d['L0_attn_src'] = jax.random.normal(jax.random.fold_in(jax.random.key(seed), 1), (16, 256, 128), dtype=_x0.dtype)
    del _x0
    return _d

def reference(L0_attn_src, L0_attn_Wq, L0_attn_bq, L0_attn_Wk, L0_attn_bk, L0_attn_Wv, L0_attn_bv, L0_attn_Wo, L0_attn_bo, L0_ffn_wg, L0_ffn_shared_w1, L0_ffn_shared_w2, L0_ffn_expert_w1, L0_ffn_expert_w2, L1_attn_in_W, L1_attn_in_b, L1_attn_log_dt, L1_attn_C, L1_attn_log_A_real, L1_attn_A_imag, L1_attn_D_skip, L1_attn_glu_W, L1_attn_glu_b, L1_attn_out_W, L1_attn_out_b, L1_ffn_U1, L1_ffn_V1, L1_ffn_b1, L1_ffn_U2, L1_ffn_V2, L1_ffn_b2, L2_attn_Wq, L2_attn_Wk, L2_attn_Wv, L2_attn_Wo, L2_attn_global_token_indices, L2_ffn_W1, L2_ffn_b1, L2_ffn_W2, L2_ffn_b2, L3_attn_ln_w, L3_attn_ln_b, L3_attn_in_proj_w, L3_attn_conv_w, L3_attn_conv_b, L3_attn_x_proj_w, L3_attn_dt_proj_w, L3_attn_dt_proj_b, L3_attn_A_log, L3_attn_D, L3_attn_out_proj_w, L3_ffn_qw, L3_ffn_qb, L3_ffn_kw, L3_ffn_kb, L3_ffn_vw, L3_ffn_vb, L3_ffn_ow, L3_ffn_ob, L3_ffn_gate_w, L3_ffn_w1, L3_ffn_w2, L3_ffn_norm1_w, L3_ffn_norm2_w):

    def _L0_attn_ref(src, Wq, bq, Wk, bk, Wv, bv, Wo, bo):
        import jax, jax.numpy as jnp
        import numpy as np
        HEAD = 8
        BLOCK = 64
        D_MODEL = 128
        B, S, D = src.shape
        H, bs = (HEAD, BLOCK)
        dk = D // H
        nb = S // bs
        q = (src @ Wq + bq).reshape(B, nb, bs, H, dk)
        k = (src @ Wk + bk).reshape(B, nb, bs, H, dk)
        v = (src @ Wv + bv).reshape(B, nb, bs, H, dk)
        scores = jnp.einsum('bnqhd,bnkhd->bhnqk', q, k) * dk ** (-0.5)
        probs = jax.nn.softmax(scores, axis=-1)
        out = jnp.einsum('bhnqk,bnkhd->bnqhd', probs, v).reshape(B, S, D)
        return out @ Wo + bo

    def _L0_ffn_ref(hidden_states, wg, shared_w1, shared_w2, expert_w1, expert_w2):
        import jax, jax.numpy as jnp
        import numpy as np
        TOPK = 8
        NUM_EXPERTS = 64
        FFN = 384
        CAPACITY = 160

        def _swiglu(x, w1, w2):
            h = x @ w1.T
            x1, x2 = jnp.split(h, 2, axis=-1)
            return x1 * jax.nn.silu(x2) @ w2.T
        B, S, H = hidden_states.shape
        T = B * S
        x = hidden_states.reshape(T, H)
        shared_out = _swiglu(x, shared_w1, shared_w2)
        logits = x.astype(jnp.float32) @ wg.T
        gates = jax.nn.softmax(logits, axis=-1)
        w_topk, idx_topk = jax.lax.top_k(gates, TOPK)
        denom = jnp.maximum(w_topk.sum(-1, keepdims=True), jnp.finfo(jnp.float32).eps)
        w_topk = w_topk / denom
        A = T * TOPK
        flat_e = idx_topk.reshape(A)
        flat_w = w_topk.reshape(A)
        flat_t = jnp.repeat(jnp.arange(T), TOPK)
        order = jnp.argsort(flat_e)
        se, st, sw = (flat_e[order], flat_t[order], flat_w[order])
        counts = jnp.zeros(NUM_EXPERTS, jnp.int32).at[flat_e].add(1)
        starts = jnp.cumsum(counts) - counts
        rank = jnp.arange(A) - starts[se]
        valid = rank < CAPACITY
        buf = jnp.zeros((NUM_EXPERTS, CAPACITY, H), x.dtype).at[se, rank].set(x[st], mode='drop')
        h = jnp.einsum('ech,efh->ecf', buf, expert_w1)
        x1, x2 = jnp.split(h, 2, axis=-1)
        out = jnp.einsum('ecf,ehf->ech', x1 * jax.nn.silu(x2), expert_w2)
        y = out[se, jnp.clip(rank, 0, CAPACITY - 1)]
        y = jnp.where(valid[:, None], y * sw[:, None].astype(y.dtype), 0.0)
        combined = jnp.zeros((T, H), x.dtype).at[st].add(y)
        return (shared_out + combined).reshape(B, S, H)

    def _L1_attn_ref(x, in_W, in_b, log_dt, C, log_A_real, A_imag, D_skip, glu_W, glu_b, out_W, out_b):
        import jax, jax.numpy as jnp
        import numpy as np
        B, L, D, N = (8, 128, 128, 32)
        DT_MIN, DT_MAX = (0.001, 0.1)
        x_in = x @ in_W.T + in_b
        u = jnp.swapaxes(x_in, 1, 2)
        Lseq = u.shape[-1]
        dt = jnp.exp(log_dt)
        Cc = (C[..., 0] + 1j * C[..., 1]).astype(jnp.complex64)
        A = (-jnp.exp(log_A_real) + 1j * A_imag).astype(jnp.complex64)
        dtA = A * dt[:, None].astype(jnp.complex64)
        K = jnp.exp(dtA[:, :, None] * jnp.arange(Lseq, dtype=jnp.float32))
        Ceff = Cc * (jnp.exp(dtA) - 1.0) / A
        k = 2.0 * jnp.einsum('hn,hnl->hl', Ceff, K).real
        n = 2 * Lseq
        k_f = jnp.fft.rfft(k, n=n)
        u_f = jnp.fft.rfft(u, n=n)
        y = jnp.fft.irfft(u_f * k_f, n=n)[..., :Lseq]
        y = y + u * D_skip[:, None]
        y = jax.nn.gelu(y, approximate=False)
        z = jnp.einsum('oh,bhl->bol', glu_W, y) + glu_b[None, :, None]
        a, g = jnp.split(z, 2, axis=1)
        y = a * jax.nn.sigmoid(g)
        y = jnp.swapaxes(y, 1, 2)
        out = y @ out_W.T + out_b
        return out + x

    def _L1_ffn_ref(x, U1, V1, b1, U2, V2, b2):
        import jax, jax.numpy as jnp
        import numpy as np
        D_MODEL, D_FF, RANK = (128, 512, 32)
        B, S = (4, 512)
        P = jnp.einsum('bsd,dr->bsr', x, U1)
        H = jax.nn.gelu(jnp.einsum('bsr,rf->bsf', P, V1) + b1)
        Q = jnp.einsum('bsf,fr->bsr', H, U2)
        return jnp.einsum('bsr,rd->bsd', Q, V2) + b2

    def _L2_attn_ref(hidden_states, Wq, Wk, Wv, Wo, global_token_indices):
        import jax, jax.numpy as jnp
        import numpy as np
        D_MODEL = 128
        NUM_HEADS = 16
        HEAD_DIM = D_MODEL // NUM_HEADS
        WINDOW_SIZE = 64
        SEQ_LEN = 512
        BATCH = 1
        NUM_GLOBAL = 16

        def _sliding_window_mask(seq_len, global_idx):
            half_window = WINDOW_SIZE // 2
            pos = jnp.arange(seq_len)
            dist = pos[:, None] - pos[None, :]
            mask = jnp.abs(dist) <= half_window
            is_global = jnp.zeros((seq_len,), dtype=bool).at[global_idx].set(True)
            mask = mask | is_global[:, None] | is_global[None, :]
            return mask
        B, S, D = hidden_states.shape
        H, Hd = (NUM_HEADS, HEAD_DIM)
        scale = 1.0 / np.sqrt(Hd)

        def proj(x, W):
            y = jnp.einsum('bsd,ed->bse', x, W)
            return y.reshape(B, S, H, Hd).transpose(0, 2, 1, 3)
        q = proj(hidden_states, Wq)
        k = proj(hidden_states, Wk)
        v = proj(hidden_states, Wv)
        scores = jnp.einsum('bhqd,bhkd->bhqk', q, k) * scale
        mask = _sliding_window_mask(S, global_token_indices)
        scores = jnp.where(mask[None, None, :, :], scores, -jnp.inf)
        attn = jax.nn.softmax(scores, axis=-1)
        out = jnp.einsum('bhqk,bhkd->bhqd', attn, v)
        out = out.transpose(0, 2, 1, 3).reshape(B, S, D)
        return jnp.einsum('bsd,ed->bse', out, Wo)

    def _L2_ffn_ref(x, W1, b1, W2, b2):
        import jax, jax.numpy as jnp
        import numpy as np
        EMB = 128
        FF = 4 * EMB

        def _ternary(w):
            scale = jnp.maximum(jnp.mean(jnp.abs(w)), 1e-08)
            w_t = jnp.clip(jnp.round(w / scale), -1.0, 1.0)
            return w + jax.lax.stop_gradient(w_t - w)
        h = jnp.einsum('bsd,fd->bsf', x, _ternary(W1)) + b1
        h = jax.nn.gelu(h, approximate=False)
        out = jnp.einsum('bsf,df->bsd', h, _ternary(W2)) + b2
        return out

    def _L3_attn_ref(x, ln_w, ln_b, in_proj_w, conv_w, conv_b, x_proj_w, dt_proj_w, dt_proj_b, A_log, D, out_proj_w):
        import jax, jax.numpy as jnp
        import numpy as np
        DIM = 128
        DI = 2 * DIM
        DSTATE = 16
        DCONV = 4
        DTRANK = DIM // 16
        B_, L = (2, 256)

        def _layernorm(x, w, b, eps=1e-05):
            mu = x.mean(-1, keepdims=True)
            var = ((x - mu) ** 2).mean(-1, keepdims=True)
            return (x - mu) * jax.lax.rsqrt(var + eps) * w + b

        def _silu(x):
            return x * jax.nn.sigmoid(x)

        def _mamba(x, in_proj_w, conv_w, conv_b, x_proj_w, dt_proj_w, dt_proj_b, A_log, D, out_proj_w):
            b, l, _ = x.shape
            xz = x @ in_proj_w.T
            xc, z = jnp.split(xz, 2, axis=-1)
            xt = jnp.pad(xc.transpose(0, 2, 1), ((0, 0), (0, 0), (DCONV - 1, 0)))
            xt = jax.lax.conv_general_dilated(xt, conv_w, (1,), 'VALID', dimension_numbers=('NCH', 'OIH', 'NCH'), feature_group_count=DI)
            xc = _silu(xt + conv_b[None, :, None]).transpose(0, 2, 1)
            dbc = xc @ x_proj_w.T
            dt = dbc[..., :DTRANK]
            Bm = dbc[..., DTRANK:DTRANK + DSTATE]
            Cm = dbc[..., DTRANK + DSTATE:]
            delta = jax.nn.softplus(dt @ dt_proj_w.T + dt_proj_b)
            A = -jnp.exp(A_log)
            dA = jnp.exp(delta[..., None] * A)
            dBu = (delta * xc)[..., None] * Bm[:, :, None, :]

            def step(h, inp):
                dA_t, dBu_t, C_t = inp
                h = dA_t * h + dBu_t
                return (h, jnp.einsum('bdn,bn->bd', h, C_t))
            h0 = jnp.zeros((b, DI, DSTATE), x.dtype)
            _, ys = jax.lax.scan(step, h0, (dA.transpose(1, 0, 2, 3), dBu.transpose(1, 0, 2, 3), Cm.transpose(1, 0, 2)))
            y = ys.transpose(1, 0, 2) + xc * D
            y = y * _silu(z)
            return y @ out_proj_w.T
        return x + _mamba(_layernorm(x, ln_w, ln_b), in_proj_w, conv_w, conv_b, x_proj_w, dt_proj_w, dt_proj_b, A_log, D, out_proj_w)

    def _L3_ffn_ref(x, qw, qb, kw, kb, vw, vb, ow, ob, gate_w, w1, w2, norm1_w, norm2_w):
        import jax, jax.numpy as jnp
        import numpy as np
        D_MODEL = 128
        N_HEADS = 16
        N_KV = 4
        NUM_REP = N_HEADS // N_KV
        HEAD_DIM = D_MODEL // N_HEADS
        N_EXPERTS = 8
        TOP_K = 2
        CAP_FACTOR = 1.25
        EPS_NORM = 1e-06

        def _rmsnorm(x, w):
            var = jnp.mean(x * x, axis=-1, keepdims=True)
            return w * (x * jax.lax.rsqrt(var + EPS_NORM))

        def _gqa(x, qw, qb, kw, kb, vw, vb, ow, ob):
            B, S, D = x.shape
            q = (x @ qw + qb).reshape(B, S, N_HEADS, HEAD_DIM).transpose(0, 2, 1, 3)
            k = (x @ kw + kb).reshape(B, S, N_KV, HEAD_DIM).transpose(0, 2, 1, 3)
            v = (x @ vw + vb).reshape(B, S, N_KV, HEAD_DIM).transpose(0, 2, 1, 3)
            k = jnp.repeat(k, NUM_REP, axis=1)
            v = jnp.repeat(v, NUM_REP, axis=1)
            scores = jnp.einsum('bhqd,bhkd->bhqk', q, k) / np.sqrt(HEAD_DIM).astype(np.float32)
            attn = jax.nn.softmax(scores, axis=-1)
            out = jnp.einsum('bhqk,bhkd->bhqd', attn, v)
            out = out.transpose(0, 2, 1, 3).reshape(B, S, D)
            return out @ ow + ob

        def _moe(x, gate_w, w1, w2):
            B, S, D = x.shape
            T = B * S
            x_flat = x.reshape(T, D)
            capacity = int(CAP_FACTOR * T * TOP_K / N_EXPERTS)
            logits = x_flat @ gate_w
            probs = jax.nn.sigmoid(logits)
            _, sel = jax.lax.top_k(probs, TOP_K)
            w_topk = jnp.take_along_axis(probs, sel, axis=1)
            w_topk = w_topk / (jnp.sum(w_topk, axis=-1, keepdims=True) + 1e-06)
            flat_sel = sel.reshape(-1)
            em = jax.nn.one_hot(flat_sel, N_EXPERTS, dtype=jnp.int32)
            ranks = jnp.take_along_axis(jnp.cumsum(em, axis=0), flat_sel[:, None], axis=1)[:, 0] - 1
            valid = ranks < capacity
            slot = flat_sel * capacity + ranks
            scatter_idx = jnp.where(valid, slot, N_EXPERTS * capacity)
            x_rep = jnp.repeat(x_flat, TOP_K, axis=0)
            padded = jnp.zeros((N_EXPERTS * capacity + 1, D), x.dtype).at[scatter_idx].set(x_rep)
            padded_x = padded[:N_EXPERTS * capacity].reshape(N_EXPERTS, capacity, D)
            h = jax.nn.gelu(jnp.einsum('ecd,edf->ecf', padded_x, w1), approximate=False)
            out_padded = jnp.einsum('ecf,efd->ecd', h, w2).reshape(N_EXPERTS * capacity, D)
            gather_idx = jnp.where(valid, slot, 0)
            out_rep = jnp.where(valid[:, None], out_padded[gather_idx], 0.0)
            out_w = out_rep * w_topk.reshape(-1)[:, None]
            return out_w.reshape(T, TOP_K, D).sum(axis=1).reshape(B, S, D)
        src = x + _gqa(x, qw, qb, kw, kb, vw, vb, ow, ob)
        src = _rmsnorm(src, norm1_w)
        src = src + _moe(src, gate_w, w1, w2)
        return _rmsnorm(src, norm2_w)
    x = L0_attn_src
    x = x + 0.5 * _L0_ffn_ref(_layernorm(x, axis=-1), L0_ffn_wg, L0_ffn_shared_w1, L0_ffn_shared_w2, L0_ffn_expert_w1, L0_ffn_expert_w2)
    x = x + _L0_attn_ref(_layernorm(x, axis=-1), L0_attn_Wq, L0_attn_bq, L0_attn_Wk, L0_attn_bk, L0_attn_Wv, L0_attn_bv, L0_attn_Wo, L0_attn_bo)
    x = x + 0.5 * _L0_ffn_ref(_layernorm(x, axis=-1), L0_ffn_wg, L0_ffn_shared_w1, L0_ffn_shared_w2, L0_ffn_expert_w1, L0_ffn_expert_w2)
    x = x + 0.5 * _L1_ffn_ref(_layernorm(x, axis=-1), L1_ffn_U1, L1_ffn_V1, L1_ffn_b1, L1_ffn_U2, L1_ffn_V2, L1_ffn_b2)
    x = x + _L1_attn_ref(_layernorm(x, axis=-1), L1_attn_in_W, L1_attn_in_b, L1_attn_log_dt, L1_attn_C, L1_attn_log_A_real, L1_attn_A_imag, L1_attn_D_skip, L1_attn_glu_W, L1_attn_glu_b, L1_attn_out_W, L1_attn_out_b)
    x = x + 0.5 * _L1_ffn_ref(_layernorm(x, axis=-1), L1_ffn_U1, L1_ffn_V1, L1_ffn_b1, L1_ffn_U2, L1_ffn_V2, L1_ffn_b2)
    x = x + 0.5 * _L2_ffn_ref(_layernorm(x, axis=-1), L2_ffn_W1, L2_ffn_b1, L2_ffn_W2, L2_ffn_b2)
    x = x + _L2_attn_ref(_layernorm(x, axis=-1), L2_attn_Wq, L2_attn_Wk, L2_attn_Wv, L2_attn_Wo, L2_attn_global_token_indices)
    x = x + 0.5 * _L2_ffn_ref(_layernorm(x, axis=-1), L2_ffn_W1, L2_ffn_b1, L2_ffn_W2, L2_ffn_b2)
    x = x + 0.5 * _L3_ffn_ref(_layernorm(x, axis=-1), L3_ffn_qw, L3_ffn_qb, L3_ffn_kw, L3_ffn_kb, L3_ffn_vw, L3_ffn_vb, L3_ffn_ow, L3_ffn_ob, L3_ffn_gate_w, L3_ffn_w1, L3_ffn_w2, L3_ffn_norm1_w, L3_ffn_norm2_w)
    x = x + _L3_attn_ref(_layernorm(x, axis=-1), L3_attn_ln_w, L3_attn_ln_b, L3_attn_in_proj_w, L3_attn_conv_w, L3_attn_conv_b, L3_attn_x_proj_w, L3_attn_dt_proj_w, L3_attn_dt_proj_b, L3_attn_A_log, L3_attn_D, L3_attn_out_proj_w)
    x = x + 0.5 * _L3_ffn_ref(_layernorm(x, axis=-1), L3_ffn_qw, L3_ffn_qb, L3_ffn_kw, L3_ffn_kb, L3_ffn_vw, L3_ffn_vb, L3_ffn_ow, L3_ffn_ob, L3_ffn_gate_w, L3_ffn_w1, L3_ffn_w2, L3_ffn_norm1_w, L3_ffn_norm2_w)
    return x

_drawn_inputs = setup_inputs


def setup_inputs(seed=0):
    import zlib

    import numpy as np

    out = dict(_drawn_inputs(seed))
    spreads = {'L1_attn_log_A_real': (-0.6931471824645996, 0.2),
     'L1_ffn_b1': (0.0, 0.1),
     'L1_ffn_b2': (0.0, 0.1),
     'L3_attn_ln_w': (1.0, 0.2),
     'L3_attn_ln_b': (0.0, 0.1),
     'L3_attn_conv_b': (0.0, 0.1),
     'L3_attn_dt_proj_b': (-4.600166320800781, 0.2),
     'L3_attn_D': (1.0, 0.2),
     'L3_ffn_qb': (0.0, 0.1),
     'L3_ffn_kb': (0.0, 0.1),
     'L3_ffn_vb': (0.0, 0.1),
     'L3_ffn_ob': (0.0, 0.1),
     'L3_ffn_norm1_w': (1.0, 0.2),
     'L3_ffn_norm2_w': (1.0, 0.2)}
    factors = {}
    for name, (base, spread) in spreads.items():
        noise = np.random.default_rng([zlib.crc32(name.encode()), seed]).standard_normal(out[name].shape)
        drawn = base * np.exp(spread * noise) if base else spread * noise
        out[name] = jnp.asarray(drawn.astype(out[name].dtype))
    for name, factor in factors.items():
        out[name] = (out[name] * factor).astype(out[name].dtype)
    return out
```

```python
from contextlib import ExitStack

import concourse.bass as bass
from concourse import mybir

F32 = mybir.dt.float32
BF16 = mybir.dt.bfloat16
U32 = mybir.dt.uint32
I32 = mybir.dt.int32
ALU = mybir.AluOpType
ACT = mybir.ActivationFunctionType
AX_X = mybir.AxisListType.X

P = 128
D = 128
TOKENS = 4096
SEQ = 256
TILES = TOKENS // P
TPG = 4
GROUPS = TILES // TPG
GT = TPG * P
LN_EPS = 1e-5
RMS_EPS = 1e-6
SUB = 80
SLOTS = 10240
TABLES = 4
FAR = 65536.0


class Phase:

    def __init__(self, nc, name):
        self.nc, self.name, self.ctx, self.sems = nc, name, ExitStack(), []

    def __enter__(self):
        return self

    def __exit__(self, *e):
        self.ctx.__exit__(*e)
        self.nc.clear_and_free_semaphores(self.sems)
        self.nc.all_engine_barrier()

    def sb(self, name, shape, dt=F32):
        return self.ctx.enter_context(self.nc.sbuf_tensor(f"{self.name}_{name}", shape, dt))

    def bank(self, name, dt=F32):
        return self.ctx.enter_context(self.nc.psum_tensor(f"{self.name}_{name}", [P, 512], dt))

    def sem(self, name):
        self.sems.append(self.nc.alloc_semaphore(f"{self.name}_{name}"))
        return self.sems[-1]

    def block(self):
        return self.ctx.enter_context(self.nc.Block())


def ahead(eng, n, unroll, front, body):
    front(0, 0, 0)

    def steps(i, last):
        for u in range(unroll):
            if u + 1 < unroll:
                front(i, u + 1, unroll * i + u + 1)
            elif not last:
                front(i + 1, 0, unroll * i + unroll)
            body(i, u, unroll * i + u)

    steps(0, False)
    with eng.Fori(1, n // unroll - 1) as i:
        steps(i, False)
    steps(n // unroll - 1, True)


def stream(eng, n, unroll, step):
    def steps(i, last):
        for u in range(unroll):
            def at(d, u=u):
                if u + d < unroll:
                    return i, u + d, unroll * i + u + d
                return None if last else (i + 1, u + d - unroll, unroll * i + u + d)
            step(at)

    steps(0, False)
    with eng.Fori(1, n // unroll - 1) as i:
        steps(i, False)
    steps(n // unroll - 1, True)


def each(eng, n, unroll, body):
    for u in range(unroll):
        body(0, u, u)
    with eng.Fori(1, n // unroll) as i:
        for u in range(unroll):
            body(i, u, unroll * i + u)


def tiles4(x, g):
    return x[:, bass.ds(TPG * g, TPG), :]


def hold(eng, mark, sem, value):
    eng.wait_ge(sem, value)
    eng.sem_inc(mark, 1)


def first(k):
    return isinstance(k, int) and k == 0


class Rsqrt:

    def __init__(self, ph, c, name, n):
        self.nc, self.mark = ph.nc, c.mark_g
        self.v, self.y, self.t = (ph.sb(f"{name}_{s}", [P, n]) for s in "vyt")
        self.seeding, self.seeded, self.newton, self.solved = (
            ph.sem(f"{name}_{s}") for s in ("seeding", "seeded", "newton", "solved"))

    def dve(self, v, src, k, scale, eps):
        nc = self.nc
        nc.vector.tensor_scalar(self.v[:, :], src, scale, eps, ALU.mult, ALU.add).then_inc(self.seeding, 1)
        v.wait_ge(self.seeding, 2 * k + 1)
        nc.vector.tensor_scalar(self.t[:, :].bitcast(I32), self.v[:, :].bitcast(I32), 1, None,
                                ALU.logical_shift_right).then_inc(self.seeding, 1)
        v.wait_ge(self.seeding, 2 * k + 2)
        nc.vector.tensor_scalar(self.y[:, :].bitcast(I32), self.t[:, :].bitcast(I32), -1.0, float(0x5F3759DF),
                                ALU.mult, ALU.add).then_inc(self.seeded, 1)

    def pool(self, g, k):
        nc, v, y, t = self.nc, self.v[:, :], self.y[:, :], self.t[:, :]
        g.wait_ge(self.seeded, k + 1)
        for i in range(3):
            n = 11 * k + 4 * i
            if i:
                g.wait_ge(self.newton, n)
            nc.gpsimd.tensor_tensor(t, y, y, ALU.mult).then_inc(self.newton, 1)
            g.wait_ge(self.newton, n + 1)
            nc.gpsimd.tensor_tensor(t, t, v, ALU.mult).then_inc(self.newton, 1)
            hold(g, self.mark, self.newton, n + 2)
            nc.gpsimd.tensor_scalar(t, t, -0.5, 1.5, ALU.mult, ALU.add).then_inc(self.newton, 1)
            g.wait_ge(self.newton, n + 3)
            nc.gpsimd.tensor_tensor(y, y, t, ALU.mult).then_inc(self.newton if i < 2 else self.solved, 1)


def weave(eng, n, unroll, group):
    def steps(i, last):
        for u in range(unroll):
            k = unroll * i + u
            nxt = (i, u + 1, k + 1) if u + 1 < unroll else None if last else (i + 1, 0, k + 1)
            group((i, u, k), nxt)

    steps(0, False)
    with eng.Fori(1, n // unroll - 1) as i:
        steps(i, False)
    steps(n // unroll - 1, True)


class Front:

    def __init__(self, ph, c, x, rows=None, perm=None, norm=True, scale=None, bias=None, bank=None, at_once=False):
        nc = ph.nc
        self.n = TILES if at_once else TPG
        self.at_once = at_once
        self.nc, self.c, self.x, self.norm = nc, c, x, norm
        self.perm = perm if perm is not None else c.ident
        self.scale, self.bias = scale, bias
        self.xn = rows if rows is not None else [ph.sb(f"xn{i}", [P, TPG, D]) for i in range(2)]
        self.xnT = [ph.sb(f"xnT{i}", [P, GT]) for i in range(2)]
        self.bank = bank if bank is not None else ph.bank("front")
        if norm:
            self.st = ph.sb("st", [P, self.n, 6])
            self.mv = ph.sb("mv", [P, self.n, 2])
            self.rsqrt = Rsqrt(ph, c, "ln", self.n)
            self.rs = self.rsqrt.y
        self.stats = ph.sem("stats")
        self.moments = ph.sem("moments")
        self.rows_ready = ph.sem("rows_ready")
        self.turned = ph.sem("turned")
        self.xnT_ready = ph.sem("xnT_ready")

    def dve(self, v, k, p, free=None):
        if self.norm:
            if not self.at_once:
                self.dve_stats(v, k)
            self.dve_rows(v, k, p, free)
            return
        if not first(k):
            hold(v, self.c.mark_v, self.turned, k)
        if free:
            free()
        self.nc.vector.tensor_copy(self.xn[p][:, :, 0:D], tiles4(self.x, k)).then_inc(self.rows_ready, TPG)

    def dve_stats(self, v, k):
        nc = self.nc
        n = self.n
        for t in range(n):
            nc.vector.bn_stats(self.st[:, t:t + 1, :], self.x[:, bass.ds(n * k + t, 1), :]).then_inc(self.stats, 1)
        hold(v, self.c.mark_v, self.stats, n * (k + 1))
        for t in range(n):
            nc.vector.bn_aggr(self.mv[:, t, :], self.st[:, t, :]).then_inc(self.moments, 1)
        v.wait_ge(self.moments, n * (k + 1))
        self.rsqrt.dve(v, self.mv[:, :, 1], k, 1.0, LN_EPS)

    def dve_rows(self, v, k, p, free=None):
        nc = self.nc
        if not first(k):
            v.wait_ge(self.turned, k)
        if not self.at_once:
            v.wait_ge(self.rsqrt.solved, k + 1)
        elif first(k):
            v.wait_ge(self.rsqrt.solved, 1)
        if free:
            free()
        for t in range(TPG):
            s = bass.ds(TPG * k + t, 1) if self.at_once else slice(t, t + 1)
            nc.vector.tensor_scalar(self.xn[p][:, t:t + 1, 0:D], self.x[:, bass.ds(TPG * k + t, 1), :],
                                    self.mv[:, s, 0:1].rearrange("p t o -> p (t o)"), self.rs[:, s], ALU.subtract,
                                    ALU.mult).then_inc(self.rows_ready, 1)

    def dve_start(self, v):
        if self.norm and self.at_once:
            self.dve_stats(v, 0)

    def pool_start(self, g):
        if self.norm and self.at_once:
            self.rsqrt.pool(g, 0)

    def pool(self, g, k):
        if self.norm and not self.at_once:
            self.rsqrt.pool(g, k)

    def pe(self, pe, k, p):
        pe.wait_ge(self.rows_ready, TPG * (k + 1))
        if not first(k):
            pe.wait_ge(self.xnT_ready, k)
        for t in range(TPG):
            m = self.nc.tensor.transpose(self.bank[:, t * P:(t + 1) * P], self.xn[p][:, t, 0:D], self.perm[:, :])
        m.then_inc(self.turned, 1)

    def act(self, a, k, p):
        a.wait_ge(self.turned, k + 1)
        if self.scale is None:
            self.nc.scalar.activation(self.xnT[p][:, :], self.bank[:, :], ACT.Copy).then_inc(self.xnT_ready, 1)
        else:
            self.nc.scalar.activation(self.xnT[p][:, :], self.bank[:, :], ACT.Identity, bias=self.bias,
                                      scale=self.scale).then_inc(self.xnT_ready, 1)


class Consts:
    pass


def setup(nc, c, w):
    with Phase(nc, "setup") as ph:
        loaded, made, out = ph.sem("loaded"), ph.sem("made"), ph.sem("converted")
        ti = ph.sb("ti", [P, TILES], I32)
        ei = ph.sb("ei", [P, 64], I32)
        di = ph.sb("di", [P, 1], I32)
        blank_made = ph.sem("blank_made")
        block = ph.block()

        @block.sync
        def _(sp):
            sp.dma_start(c.x[:, :, :], w["x"].rearrange("(t p) d -> p t d", p=P)).then_inc(loaded, 16)
            sp.wait_ge(blank_made, 2)
            clear_next(c, sp)
            sp.wait_ge(loaded, 16)

        @block.gpsimd
        def _(g):
            n = 0
            for t, val in ((c.ident, 0.0), (c.mirror, 0.0), (c.ones, 1.0), (c.zero, 0.0), (c.below, 1.0)):
                nc.gpsimd.memset(t[:, :], val).then_inc(made, 1)
                n += 1
            g.wait_ge(made, n)
            for t, pat, mul, base, op in ((c.ident, -1, 1, 0, ALU.not_equal), (c.mirror, 1, 1, -(P - 1), ALU.not_equal)):
                nc.gpsimd.affine_select(out=t[:, :], in_=t[:, :], compare_op=op, fill=1.0, base=base,
                                        pattern=[[pat, P]], channel_multiplier=mul).then_inc(made, 1)
                n += 1
            nc.gpsimd.affine_select(out=c.below[:, :], in_=c.below[:, :], compare_op=ALU.is_gt, fill=0.0, base=0,
                                    pattern=[[1, P]], channel_multiplier=-1).then_inc(made, 1)
            nc.gpsimd.iota(ti[:, :], pattern=[[P, TILES]], base=0, channel_multiplier=1).then_inc(made, 1)
            nc.gpsimd.iota(ei[:, :], pattern=[[1, 64]], base=0, channel_multiplier=0).then_inc(made, 1)
            nc.gpsimd.iota(di[:, :], pattern=[[0, 1]], base=TOKENS, channel_multiplier=1).then_inc(made, 1)

        @block.vector
        def _(v):
            nc.vector.memset(c.blank[:, :], 0.0).then_inc(blank_made, 1)
            v.wait_ge(made, 11)
            v.wait_ge(blank_made, 1)
            nc.vector.tensor_copy(c.token_id[:, :], ti[:, :]).then_inc(out, 1)
            nc.vector.tensor_copy(c.expert_id[:, :], ei[:, :]).then_inc(out, 1)
            nc.vector.tensor_copy(c.blank[:, -1:], di[:, :]).then_inc(blank_made, 1)
            nc.vector.tensor_copy(c.below_b[:, :], c.below[:, :]).then_inc(out, 1)
            nc.vector.tensor_copy(c.ones_b[:, :], c.ones[:, :]).then_inc(out, 1)


def lowrank_ffn(nc, c, name, w):
    with Phase(nc, name) as ph:
        R, F = 32, 512
        u1, v1 = ph.sb("u1", [P, R]), ph.sb("v1", [R, F])
        u2, v2 = ph.sb("u2", [P, 4, R]), ph.sb("v2", [R, D])
        b1, b2 = ph.sb("b1", [P, 4]), ph.sb("b2", [1, D])
        pT, hT, qT = ph.sb("pT", [R, GT]), ph.sb("hT", [P, 4, GT]), ph.sb("qT", [R, GT])
        fr = Front(ph, c, c.x)
        pb, qb, ob = ph.bank("p"), ph.bank("q"), ph.bank("o")
        hb = [ph.bank(f"h{i}") for i in range(2)]
        weights, p_done, pT_ready, h_done, gelu_done, q_done, qT_ready, o_done, o_free = (
            ph.sem(s) for s in ("weights", "p_done", "pT_ready", "h_done", "gelu_done", "q_done", "qT_ready",
                                "o_done", "o_free"))
        block = ph.block()

        @block.sync
        def _(sp):
            for dst, src in ((u1, "L1_ffn_U1"), (v1, "L1_ffn_V1"), (u2, "L1_ffn_U2"), (v2, "L1_ffn_V2"),
                             (b1, "L1_ffn_b1"), (b2, "L1_ffn_b2")):
                sp.dma_start(dst[:], w[src]).then_inc(weights, 16)
            sp.wait_ge(weights, 96)

        @block.gpsimd
        def _(g):
            ahead(g, GROUPS, 2, lambda i, u, k: fr.pool(g, k), lambda i, u, k: None)

        @block.vector
        def _(v):
            v.sem_inc(o_free, 1)

            def body(i, u, k):
                v.wait_ge(o_done, k + 1)
                nc.vector.scalar_tensor_tensor(
                    out=tiles4(c.x, k), in0=ob[:, :].rearrange("p (t d) -> p t d", t=TPG), scalar=0.5,
                    in1=tiles4(c.x, k), op0=ALU.mult, op1=ALU.add).then_inc(o_free, 1)

            ahead(v, GROUPS, 2, lambda i, u, k: fr.dve(v, k, u), body)

        @block.scalar
        def _(a):
            a.wait_ge(weights, 96)

            def body(i, u, k):
                a.wait_ge(p_done, k + 1)
                nc.scalar.activation(pT[:, :], pb[0:R, :], ACT.Copy).then_inc(pT_ready, 1)
                for f in range(4):
                    a.wait_ge(h_done, 4 * k + f + 1)
                    nc.scalar.activation(hT[:, f, :], hb[f % 2][:, :], ACT.Gelu_apprx_tanh,
                                         bias=b1[:, f:f + 1]).then_inc(gelu_done, 1)
                a.wait_ge(q_done, k + 1)
                nc.scalar.activation(qT[:, :], qb[0:R, :], ACT.Copy).then_inc(qT_ready, 1)

            ahead(a, GROUPS, 2, lambda i, u, k: fr.act(a, k, u), body)

        @block.tensor
        def _(pe):
            pe.wait_ge(weights, 96)

            def body(i, u, k):
                pe.wait_ge(fr.xnT_ready, k + 1)
                nc.tensor.matmul(pb[0:R, :], u1[:, :], fr.xnT[u][:, :], start=True, stop=True).then_inc(p_done, 1)
                pe.wait_ge(pT_ready, k + 1)

                def h(f):
                    nc.tensor.matmul(hb[f % 2][:, :], v1[:, f * P:(f + 1) * P], pT[:, :], start=True,
                                     stop=True).then_inc(h_done, 1)

                h(0)
                h(1)
                for f in range(4):
                    pe.wait_ge(gelu_done, 4 * k + f + 1)
                    m = nc.tensor.matmul(qb[0:R, :], u2[:, f, :], hT[:, f, :], start=(f == 0), stop=(f == 3))
                    if f + 2 < 4:
                        h(f + 2)
                m.then_inc(q_done, 1)
                pe.wait_ge(qT_ready, k + 1)
                pe.wait_ge(o_free, k + 1)
                for t in range(TPG):
                    o = ob[:, t * D:(t + 1) * D]
                    nc.tensor.matmul(o, c.ones[0:1, :], b2[:, :], start=True, stop=False)
                    m = nc.tensor.matmul(o, qT[:, t * P:(t + 1) * P], v2[:, :], start=False, stop=True)
                m.then_inc(o_done, 1)

            ahead(pe, GROUPS, 2, lambda i, u, k: fr.pe(pe, k, u), body)


def ternary_ffn(nc, c, name, w):
    with Phase(nc, name) as ph:
        w1, w2 = ph.sb("w1", [P, 512]), ph.sb("w2", [P, 4, D])
        b1, b2 = ph.sb("b1", [P, 4]), ph.sb("b2", [1, D])
        tmp, part = ph.sb("tmp", [P, 512]), ph.sb("part", [P, 2])
        scale = ph.sb("scale", [P, 2])
        hT = ph.sb("hT", [P, 4, GT])
        fr = Front(ph, c, c.x)
        ob = ph.bank("o")
        hb = [ph.bank(f"h{i}") for i in range(4)]
        weights, tern, sums, h_done, gelu_done, o_done, o_free = (
            ph.sem(s) for s in ("weights", "tern", "sums", "h_done", "gelu_done", "o_done", "o_free"))
        block = ph.block()
        MAGIC = 1.5 * 2.0 ** 23
        TERN = 2 * 8

        @block.sync
        def _(sp):
            for dst, src in ((w1, "L2_ffn_W1"), (w2, "L2_ffn_W2"), (b1, "L2_ffn_b1"), (b2, "L2_ffn_b2")):
                sp.dma_start(dst[:], w[src]).then_inc(weights, 16)
            sp.wait_ge(weights, 64)

        @block.gpsimd
        def _(g):
            ahead(g, GROUPS, 2, lambda i, u, k: fr.pool(g, k), lambda i, u, k: None)

        @block.vector
        def _(v):
            v.wait_ge(weights, 64)
            n = 0
            mats = (w1[:, :], w2[:, :, :].rearrange("p c d -> p (c d)"))

            def step(ins):
                ins.then_inc(tern, 1)

            for j, m in enumerate(mats):
                step(nc.vector.tensor_reduce(part[:, j:j + 1], m, AX_X, ALU.add, apply_absolute_value=True))
            v.wait_ge(sums, 1)
            step(nc.vector.tensor_scalar(scale[:, :], ob[:, 0:2], 1.0 / (512 * D), 1e-8, ALU.mult, ALU.max))
            v.wait_ge(tern, 3)
            step(nc.vector.reciprocal(part[:, :], scale[:, :]))
            n = 4
            for j, m in enumerate(mats):
                v.wait_ge(tern, n)
                step(nc.vector.tensor_scalar(tmp[:, :], m, part[:, j:j + 1], 1.0, ALU.mult, ALU.min))
                v.wait_ge(tern, n + 1)
                step(nc.vector.tensor_scalar(tmp[:, :], tmp[:, :], -1.0, MAGIC, ALU.max, ALU.add))
                v.wait_ge(tern, n + 2)
                step(nc.vector.scalar_tensor_tensor(out=tmp[:, :], in0=tmp[:, :], scalar=-MAGIC, in1=m, op0=ALU.add,
                                                    op1=ALU.subtract))
                v.wait_ge(tern, n + 3)
                step(nc.vector.tensor_tensor(m, m, tmp[:, :], ALU.add))
                n += 4
            v.sem_inc(o_free, 1)

            def body(i, u, k):
                v.wait_ge(o_done, k + 1)
                nc.vector.scalar_tensor_tensor(
                    out=tiles4(c.x, k), in0=ob[:, :].rearrange("p (t d) -> p t d", t=TPG), scalar=0.5,
                    in1=tiles4(c.x, k), op0=ALU.mult, op1=ALU.add).then_inc(o_free, 1)

            ahead(v, GROUPS, 2, lambda i, u, k: fr.dve(v, k, u), body)

        @block.scalar
        def _(a):
            def body(i, u, k):
                for f in range(4):
                    a.wait_ge(h_done, 4 * k + f + 1)
                    nc.scalar.activation(hT[:, f, :], hb[f][:, :], ACT.Gelu,
                                         bias=b1[:, f:f + 1]).then_inc(gelu_done, 1)

            ahead(a, GROUPS, 2, lambda i, u, k: fr.act(a, k, u), body)

        @block.tensor
        def _(pe):
            pe.wait_ge(tern, 2)
            nc.tensor.matmul(ob[:, 0:2], c.ones[:, :], part[:, :], start=True, stop=True).then_inc(sums, 1)
            pe.wait_ge(tern, 12)

            def body(i, u, k):
                pe.wait_ge(fr.xnT_ready, k + 1)
                for f in range(4):
                    nc.tensor.matmul(hb[f][:, :], w1[:, f * P:(f + 1) * P], fr.xnT[u][:, :], start=True,
                                     stop=True).then_inc(h_done, 1)
                pe.wait_ge(gelu_done, 4 * k + 4)
                pe.wait_ge(o_free, k + 1)
                for t in range(TPG):
                    o = ob[:, t * D:(t + 1) * D]
                    nc.tensor.matmul(o, c.ones[0:1, :], b2[:, :], start=True, stop=False)
                    for f in range(4):
                        m = nc.tensor.matmul(o, hT[:, f, t * P:(t + 1) * P], w2[:, f, :], start=False, stop=(f == 3))
                m.then_inc(o_done, 1)

            ahead(pe, GROUPS, 2, lambda i, u, k: fr.pe(pe, k, u), body)


def head_masks(nc, ph, g, made, target, width):
    n = target.shape[-1]
    nc.gpsimd.memset(target, 1.0).then_inc(made, 1)
    g.wait_ge(made, 1)
    nc.gpsimd.affine_select(out=target, in_=target, compare_op=ALU.is_ge, fill=0.0, base=0,
                            pattern=[[-width, n]], channel_multiplier=1).then_inc(made, 1)
    g.wait_ge(made, 2)
    nc.gpsimd.affine_select(out=target, in_=target, compare_op=ALU.is_gt, fill=0.0, base=width,
                            pattern=[[width, n]], channel_multiplier=-1).then_inc(made, 1)


def block_attention(nc, c, name, w):
    with Phase(nc, name) as ph:
        H, DK, B = 8, 16, 64
        wq, wk, wv, wo = (ph.sb(s, [P, D]) for s in ("wq", "wk", "wv", "wo"))
        bq, bk = ph.sb("bq", [P, 1]), ph.sb("bk", [P, 1])
        bv, bo = ph.sb("bv", [1, D]), ph.sb("bo", [1, D])
        bqs = ph.sb("bqs", [P, 1])
        hm = ph.sb("hm", [P, H])
        sm = ph.sb("sm", [P, 2, DK])
        qT, kT, kexp = ph.sb("qT", [P, GT]), ph.sb("kT", [P, GT]), ph.sb("kexp", [P, H, GT])
        vbd = ph.sb("vbd", [P, 8, 4, 32])
        mx = ph.sb("mx", [P, 2, H])
        sc = ph.sb("sc", [P, 2, 512])
        pr = ph.sb("pr", [P, 2, 512])
        pT = ph.sb("pT", [P, 2, 512])
        rz = ph.sb("rz", [P, P])
        oT = ph.sb("oT", [P, P])
        fr = Front(ph, c, c.x)
        qk = [ph.bank(f"qk{i}") for i in range(2)]
        vb = [ph.bank(f"v{i}") for i in range(2)]
        tb, ozb, ob = ph.bank("t"), ph.bank("oz"), ph.bank("o")
        (weights, made, ready, q_done, k_done, v_done, qT_ready, kT_ready, kexp_ready, vbd_ready, s_done, mx_ready,
         sc_ready, pr_ready, t_done, pT_ready, oz_done, rz_ready, oT_ready, o_done, o_free) = (
            ph.sem(s) for s in ("weights", "made", "ready", "q_done", "k_done", "v_done", "qT_ready", "kT_ready",
                                "kexp_ready", "vbd_ready", "s_done", "mx_ready", "sc_ready", "pr_ready", "t_done",
                                "pT_ready", "oz_done", "rz_ready", "oT_ready", "o_done", "o_free"))
        block = ph.block()

        @block.sync
        def _(sp):
            for dst, src in ((wq, "Wq"), (wk, "Wk"), (wv, "Wv"), (wo, "Wo"), (bq, "bq"), (bk, "bk"), (bv, "bv"),
                             (bo, "bo")):
                sp.dma_start(dst[:], w["L0_attn_" + src]).then_inc(weights, 16)
            sp.wait_ge(weights, 128)

        @block.gpsimd
        def _(g):
            head_masks(nc, ph, g, made, hm[:, :], DK)
            nc.gpsimd.memset(sm[:, :, :], 0.0).then_inc(made, 1)
            g.wait_ge(made, 4)
            for s in range(2):
                nc.gpsimd.memset(sm[B * s:B * s + B, s, :], 1.0).then_inc(made, 1)
            ahead(g, GROUPS, 2, lambda i, u, k: fr.pool(g, k), lambda i, u, k: None)

        @block.vector
        def _(v):
            v.wait_ge(weights, 128)
            v.wait_ge(made, 6)
            nc.vector.tensor_scalar(bqs[:, :], bq[:, :], DK ** -0.5, None, ALU.mult).then_inc(ready, 1)
            v.sem_inc(o_free, 1)

            def soft(k, t):
                n = TPG * k + t
                v.wait_ge(s_done, n + 1)
                s3 = qk[t % 2][:, :].rearrange("p (h q) -> p h q", h=H)
                nc.vector.tensor_reduce(mx[:, t % 2, :], s3, AX_X, ALU.max).then_inc(mx_ready, 1)
                v.wait_ge(mx_ready, n + 1)
                nc.vector.tensor_tensor(sc[:, t % 2, :].rearrange("p (h q) -> p h q", h=H), s3,
                                        mx[:, t % 2, :].unsqueeze(2).to_broadcast([P, H, B]),
                                        ALU.subtract).then_inc(sc_ready, 1)

            def body(i, u, k):
                v.wait_ge(kT_ready, k + 1)
                for h in range(H):
                    nc.vector.tensor_scalar(kexp[:, h, :], kT[:, :], hm[:, h:h + 1], None,
                                            ALU.mult).then_inc(kexp_ready, 1)
                for j in range(8):
                    v.wait_ge(v_done, 8 * k + 4 * (j // 4) + 4)
                    nc.vector.tensor_tensor(
                        vbd[:, j, :, :], vb[j // 4][:, (j % 4) * P:(j % 4 + 1) * P].rearrange("p (h d) -> p h d", d=32),
                        sm[:, :, :].rearrange("p s d -> p (s d)").unsqueeze(1).to_broadcast([P, 4, 32]),
                        ALU.mult).then_inc(vbd_ready, 1)
                soft(k, 0)
                for t in range(TPG):
                    n = TPG * k + t
                    if t + 1 < TPG:
                        soft(k, t + 1)
                    v.wait_ge(oz_done, n + 1)
                    nc.vector.reciprocal(rz[:, :], ozb[:, P:2 * P]).then_inc(rz_ready, 1)
                    v.wait_ge(rz_ready, n + 1)
                    nc.vector.tensor_tensor(oT[:, :], ozb[:, 0:P], rz[:, :], ALU.mult).then_inc(oT_ready, 1)
                    v.wait_ge(o_done, n + 1)
                    xt = c.x[:, bass.ds(n, 1), :]
                    nc.vector.tensor_tensor(xt, ob[:, 0:D].unsqueeze(1), xt, ALU.add).then_inc(o_free, 1)

            ahead(v, GROUPS, 2, lambda i, u, k: fr.dve(v, k, u), body)

        @block.scalar
        def _(a):
            a.wait_ge(ready, 1)

            def probs(k, t):
                a.wait_ge(sc_ready, TPG * k + t + 1)
                nc.scalar.activation(pr[:, t % 2, :], sc[:, t % 2, :], ACT.Exp).then_inc(pr_ready, 1)

            def body(i, u, k):
                a.wait_ge(q_done, k + 1)
                nc.scalar.activation(qT[:, :], qk[0][:, :], ACT.Identity, bias=bqs[:, 0:1],
                                     scale=DK ** -0.5).then_inc(qT_ready, 1)
                a.wait_ge(k_done, k + 1)
                nc.scalar.activation(kT[:, :], qk[1][:, :], ACT.Identity, bias=bk[:, 0:1]).then_inc(kT_ready, 1)
                probs(k, 0)
                for t in range(TPG):
                    if t + 1 < TPG:
                        probs(k, t + 1)
                    a.wait_ge(t_done, TPG * k + t + 1)
                    nc.scalar.activation(pT[:, t % 2, :], tb[:, :], ACT.Copy).then_inc(pT_ready, 1)

            ahead(a, GROUPS, 2, lambda i, u, k: fr.act(a, k, u), body)

        @block.tensor
        def _(pe):
            pe.wait_ge(weights, 128)
            pe.wait_ge(made, 6)

            def scores(k, t):
                for b in range(2):
                    tok = slice(t * P + b * B, t * P + b * B + B)
                    m = nc.tensor.matmul(qk[t % 2][b * B:(b + 1) * B, :].rearrange("p (h q) -> p h q", h=H),
                                         qT[:, tok], kexp[:, :, tok], start=True, stop=True)
                m.then_inc(s_done, 1)

            def body(i, u, k):
                pe.wait_ge(fr.xnT_ready, k + 1)
                xT = fr.xnT[u]
                nc.tensor.matmul(qk[0][:, :], wq[:, :], xT[:, :], start=True, stop=True).then_inc(q_done, 1)
                nc.tensor.matmul(qk[1][:, :], wk[:, :], xT[:, :], start=True, stop=True).then_inc(k_done, 1)
                for j in range(8):
                    for s in range(2):
                        o = vb[j // 4][s * B:(s + 1) * B, (j % 4) * P:(j % 4 + 1) * P]
                        nc.tensor.matmul(o, c.ones[0:1, 0:B], bv[:, :], start=True, stop=False)
                        m = nc.tensor.matmul(o, xT[:, j * B:(j + 1) * B], wv[:, :], start=False, stop=True)
                    m.then_inc(v_done, 1)
                pe.wait_ge(qT_ready, k + 1)
                pe.wait_ge(kexp_ready, H * (k + 1))
                scores(k, 0)
                for t in range(TPG):
                    n = TPG * k + t
                    if t + 1 < TPG:
                        scores(k, t + 1)
                    pe.wait_ge(pr_ready, n + 1)
                    for j in range(4):
                        m = nc.tensor.transpose(tb[:, j * P:(j + 1) * P], pr[:, t % 2, j * P:(j + 1) * P],
                                                c.ident[:, :])
                    m.then_inc(t_done, 1)
                    pe.wait_ge(pT_ready, n + 1)
                    pe.wait_ge(vbd_ready, 8 * k + 2 * t + 2)
                    for b in range(2):
                        for off, src in ((0, None), (P, sm)):
                            for j in range(4):
                                lhsT = vbd[:, 2 * t + b, j, :] if src is None else sm[:, :, :].rearrange(
                                    "p s d -> p (s d)")
                                m = nc.tensor.matmul(ozb[32 * j:32 * j + 32, off + b * B:off + (b + 1) * B], lhsT,
                                                     pT[:, t % 2, j * P + b * B:j * P + (b + 1) * B],
                                                     start=True, stop=True, tile_position=(0, 32 * j))
                    m.then_inc(oz_done, 1)
                    pe.wait_ge(oT_ready, n + 1)
                    pe.wait_ge(o_free, n + 1)
                    nc.tensor.matmul(ob[:, 0:D], c.ones[0:1, :], bo[:, :], start=True, stop=False)
                    nc.tensor.matmul(ob[:, 0:D], oT[:, :], wo[:, :], start=False, stop=True).then_inc(o_done, 1)

            ahead(pe, GROUPS, 2, lambda i, u, k: fr.pe(pe, k, u), body)


class FullAttention:

    H, DK = 16, 8
    CH = 8
    STEPS = TPG * 8
    ORDER = [4 * (i % 4) + i // 4 for i in range(16)]
    BANK = [0, 1, 2, 0, 1, 2, 0, 1]

    def __init__(self, ph, c, wq, wk, wv, wo, bq=None, bk=None, bv=None, bo=None, mask=None):
        self.nc, self.c, self.ph = ph.nc, c, ph
        self.wq, self.wk, self.wv, self.wo, self.bq, self.bk, self.bv, self.bo = wq, wk, wv, wo, bq, bk, bv, bo
        self.mask = mask
        self.hm = ph.sb("hm", [P, self.H])
        self.vm = ph.sb("vm", [P, 4, 4, 8])
        self.kT = ph.sb("kT", [P, GT])
        self.qT = [ph.sb(f"qT{i}", [P, GT]) for i in range(2)]
        self.kexp = [ph.sb(f"kexp{i}", [P, self.H, GT]) for i in range(2)]
        self.vbd = [ph.sb(f"vbd{i}", [P, TPG, self.H, 32]) for i in range(2)]
        self.mx, self.zs = ph.sb("mx", [P, 2, self.H]), ph.sb("zs", [P, 2, self.H])
        self.pr = [ph.sb(f"pr{i}", [P, 512]) for i in range(4)]
        self.pT = [ph.sb(f"pT{i}", [P, 512]) for i in range(2)]
        self.rz, self.zT, self.oT = ph.sb("rz", [P, P]), ph.sb("zT", [P, P]), ph.sb("oT", [P, P])
        self.pb = ph.bank("proj")
        self.fr = Front(ph, c, c.x, bank=self.pb)
        self.sb_ = [ph.bank(f"s{i}") for i in range(3)]
        self.tb = [ph.bank(f"t{i}") for i in range(2)]
        self.ob = [ph.bank(f"o{i}") for i in range(2)]
        self.made, self.q_done, self.k_done, self.v_done, self.qT_ready, self.kT_ready = (
            ph.sem(s) for s in ("made", "q_done", "k_done", "v_done", "qT_ready", "kT_ready"))
        self.kexp_ready, self.vbd_ready, self.s_done, self.mx_ready, self.pr_ready, self.t_done = (
            ph.sem(s) for s in ("kexp_ready", "vbd_ready", "s_done", "mx_ready", "pr_ready", "t_done"))
        self.pT_ready, self.rz_ready, self.oz_done, self.oT_ready, self.o_done, self.o_free = (
            ph.sem(s) for s in ("pT_ready", "rz_ready", "oz_done", "oT_ready", "o_done", "o_free"))
        self.zT_ready = ph.sem("zT_ready")

    MADE = 8

    def pool_setup(self, g):
        nc = self.nc
        head_masks(nc, self.ph, g, self.made, self.hm[:, :], self.DK)
        nc.gpsimd.memset(self.vm[:, :, :, :], 0.0).then_inc(self.made, 1)
        g.wait_ge(self.made, 4)
        for i in range(4):
            nc.gpsimd.memset(self.vm[:, i, i, :], 1.0).then_inc(self.made, 1)

    def later(self, s, now, nxt):
        if s < self.STEPS:
            return now[1], now[2], s // self.CH, s % self.CH
        return None if nxt is None else (nxt[1], nxt[2], 0, s - self.STEPS)

    def before(self, t, now):
        u, k = now[1], now[2]
        if t:
            return u, k, t - 1, TPG * k + t - 1
        return None if first(k) else (1 - u, k - 1, TPG - 1, TPG * k - 1)


    def dve_start(self, v):
        self.fr.dve(v, 0, 0)
        for t in range(TPG):
            self.dve_values(v, 0, 0, t)
        self.dve_maxima(v, 0, 0, 0, 0)
        self.dve_maxima(v, 0, 0, 0, 1)

    def dve_maxima(self, v, u, k, t, q):
        v.wait_ge(self.s_done, self.CH * (TPG * k + t) + q + 1)
        self.nc.vector.tensor_reduce(self.mx[:, t % 2, 2 * q:2 * q + 2],
                                     self.sb_[self.BANK[q]][:, :].rearrange("p (h s) -> p h s", h=2), AX_X, ALU.max,
                                     negate=True).then_inc(self.mx_ready, 1)

    def dve_values(self, v, u, k, t):
        if t == 0:
            v.wait_ge(self.v_done, k + 1)
        for j in range(4):
            self.nc.vector.tensor_tensor(
                self.vbd[u][:, t, 4 * j:4 * j + 4, :],
                self.pb[:, t * P + 32 * j:t * P + 32 * j + 32].unsqueeze(1).to_broadcast([P, 4, 32]),
                self.vm[:, :, :, :].rearrange("p i a b -> p i (a b)"), ALU.mult).then_inc(self.vbd_ready, 1)

    def dve_inverse(self, v, tile):
        u, k, t, n = tile
        v.wait_ge(self.pr_ready, self.CH * (n + 1))
        self.nc.vector.reciprocal(
            self.rz[:, :].rearrange("p (a b d) -> p b a d", a=4, b=4),
            self.zs[:, t % 2, :].rearrange("p (b a) -> p b a", b=4).unsqueeze(3).to_broadcast([P, 4, 4, 8])
            ).then_inc(self.rz_ready, 1)

    def dve_divide(self, v, tile):
        u, k, t, n = tile
        v.wait_ge(self.oz_done, n + 1)
        self.nc.vector.tensor_copy(self.zT[:, :], self.ob[t % 2][:, P:2 * P]).then_inc(self.zT_ready, 1)
        v.wait_ge(self.zT_ready, n + 1)
        self.nc.vector.tensor_tensor(self.oT[:, :], self.ob[t % 2][:, 0:P], self.zT[:, :],
                                     ALU.mult).then_inc(self.oT_ready, 1)

    def dve_finish(self, v, tile, finish):
        v.wait_ge(self.o_done, tile[3] + 1)
        finish(tile, self.ob[tile[2] % 2][:, 2 * P:3 * P])

    def dve(self, v, now, nxt, finish, between=None):
        for s in range(self.STEPS):
            t, q = s // self.CH, s % self.CH
            n = self.CH * TPG * now[2] + s
            ahead2 = self.later(s + 2, now, nxt)
            if ahead2:
                self.dve_maxima(v, *ahead2)
            v.wait_ge(self.t_done, n + 1)
            self.nc.vector.tensor_copy(self.pT[q % 2][:, :], self.tb[q % 2][:, :]).then_inc(self.pT_ready, 1)
            tile = self.before(t, now)
            if tile and q == 0:
                self.dve_inverse(v, tile)
            if tile and q == 2:
                self.dve_divide(v, tile)
            if tile and q == 5:
                self.dve_finish(v, tile, finish)
            if nxt and s == 10:
                self.fr.dve_stats(v, nxt[2])
            if nxt and s == 14:
                self.fr.dve_rows(v, nxt[2], nxt[1])
            if nxt and 23 <= s < 27:
                self.dve_values(v, nxt[1], nxt[2], s - 23)
            if between:
                between(s)

    def last_tile(self):
        return 1, GROUPS - 1, TPG - 1, TILES - 1

    def dve_end(self, v, finish):
        tile = self.last_tile()
        self.dve_inverse(v, tile)
        self.dve_divide(v, tile)
        self.dve_finish(v, tile, finish)


    def act_queries(self, a, u, k):
        nc, s = self.nc, self.DK ** -0.5
        a.wait_ge(self.q_done, k + 1)
        if self.bq is None:
            nc.scalar.activation(self.qT[u][:, :], self.pb[:, :], ACT.Copy, scale=s).then_inc(self.qT_ready, 1)
        else:
            nc.scalar.activation(self.qT[u][:, :], self.pb[:, :], ACT.Identity, bias=self.bq[:, 0:1],
                                 scale=s).then_inc(self.qT_ready, 1)

    def act_keys(self, a, u, k):
        nc = self.nc
        a.wait_ge(self.k_done, k + 1)
        if self.bk is None:
            nc.scalar.activation(self.kT[:, :], self.pb[:, :], ACT.Copy).then_inc(self.kT_ready, 1)
        else:
            nc.scalar.activation(self.kT[:, :], self.pb[:, :], ACT.Identity,
                                 bias=self.bk[:, 0:1]).then_inc(self.kT_ready, 1)

    def act_head_keys(self, a, u, k, i):
        if i == 0:
            a.wait_ge(self.kT_ready, k + 1)
        h = self.ORDER[i]
        self.nc.scalar.activation(self.kexp[u][:, i, :], self.kT[:, :], ACT.Copy,
                                  scale=self.hm[:, h:h + 1]).then_inc(self.kexp_ready, 1)

    def act_start(self, a):
        a.wait_ge(self.made, self.MADE)
        self.fr.act(a, 0, 0)
        self.act_queries(a, 0, 0)
        self.act_keys(a, 0, 0)
        for i in range(self.H):
            self.act_head_keys(a, 0, 0, i)

    def act(self, a, now, nxt, between=None):
        for s in range(self.STEPS):
            t, q = s // self.CH, s % self.CH
            a.wait_ge(self.mx_ready, self.CH * TPG * now[2] + s + 1)
            for h in range(2):
                m = self.nc.scalar.activation(self.pr[q % 4][:, 256 * h:256 * h + 256],
                                              self.sb_[self.BANK[q]][:, 256 * h:256 * h + 256], ACT.Exp,
                                              bias=self.mx[:, t % 2, 2 * q + h:2 * q + h + 1],
                                              accum_out=self.zs[:, t % 2, 2 * q + h:2 * q + h + 1])
            m.then_inc(self.pr_ready, 1)
            if nxt:
                _, u, k = nxt
                if s == 17:
                    self.fr.act(a, k, u)
                if s == 19:
                    self.act_queries(a, u, k)
                if s == 21:
                    self.act_keys(a, u, k)
                if 22 <= s < 30:
                    self.act_head_keys(a, u, k, 2 * (s - 22))
                    self.act_head_keys(a, u, k, 2 * (s - 22) + 1)
            if between:
                between(s)


    def pe_rows(self, pe, u, k):
        if not first(k):
            pe.wait_ge(self.vbd_ready, 16 * k)
        self.fr.pe(pe, k, u)

    def pe_queries(self, pe, u, k):
        pe.wait_ge(self.fr.xnT_ready, k + 1)
        self.nc.tensor.matmul(self.pb[:, :], self.wq[:, :], self.fr.xnT[u][:, :], start=True,
                              stop=True).then_inc(self.q_done, 1)

    def pe_keys(self, pe, u, k):
        pe.wait_ge(self.qT_ready, k + 1)
        self.nc.tensor.matmul(self.pb[:, :], self.wk[:, :], self.fr.xnT[u][:, :], start=True,
                              stop=True).then_inc(self.k_done, 1)

    def pe_values(self, pe, u, k):
        pe.wait_ge(self.kT_ready, k + 1)
        for t in range(TPG):
            o = self.pb[:, t * P:(t + 1) * P]
            if self.bv is not None:
                self.nc.tensor.matmul(o, self.c.ones[0:1, :], self.bv[:, :], start=True, stop=False)
            m = self.nc.tensor.matmul(o, self.fr.xnT[u][:, t * P:(t + 1) * P], self.wv[:, :], start=self.bv is None,
                                      stop=True)
        m.then_inc(self.v_done, 1)

    def pe_scores(self, pe, u, k, t, q):
        n = self.CH * (TPG * k + t) + q
        if (t, q) == (0, 0):
            pe.wait_ge(self.kexp_ready, self.H * (k + 1))
        if q == 0 and not (first(k) and t == 0):
            pe.wait_ge(self.pr_ready, n - 1)
        if q == 1 and not (first(k) and t == 0):
            pe.wait_ge(self.pr_ready, n - 1)
        b, o = t // 2, self.sb_[self.BANK[q]][:, :].rearrange("p (h s) -> p h s", h=2)
        m = self.nc.tensor.matmul(o, self.qT[u][:, t * P:(t + 1) * P],
                                  self.kexp[u][:, 2 * q:2 * q + 2, SEQ * b:SEQ * b + SEQ], start=True,
                                  stop=self.mask is None)
        if self.mask is not None:
            m = self.nc.tensor.matmul(o, self.c.ident_b[:, :],
                                      self.mask[:, t % 2, :].unsqueeze(1).to_broadcast([P, 2, SEQ]), start=False,
                                      stop=True)
        m.then_inc(self.s_done, 1)

    def pe_heads(self, pe, u, k, t, q):
        tile = TPG * k + t
        if q == 0 and not (first(k) and t < 2):
            pe.wait_ge(self.o_free, tile - 1)
        pe.wait_ge(self.pT_ready, self.CH * tile + q + 1)
        for half in range(2):
            for j in range(2):
                h = self.ORDER[2 * q + j]
                quad, i = h // 4, h % 4
                self.nc.tensor.matmul(self.ob[t % 2][32 * quad:32 * quad + 32, 0:P],
                                      self.vbd[u][:, 2 * (t // 2) + half, h, :],
                                      self.pT[q % 2][:, 256 * j + P * half:256 * j + P * half + P],
                                      start=(i == 0 and half == 0), stop=(i == 3 and half == 1),
                                      tile_position=(0, 32 * quad), skip_group_check=True)

    def pe_sums(self, pe, tile):
        u, k, t, n = tile
        pe.wait_ge(self.rz_ready, n + 1)
        self.nc.tensor.transpose(self.ob[t % 2][:, P:2 * P], self.rz[:, :], self.c.ident[:, :]).then_inc(self.oz_done, 1)

    def pe_project(self, pe, tile):
        u, k, t, n = tile
        o = self.ob[t % 2][:, 2 * P:3 * P]
        pe.wait_ge(self.oT_ready, n + 1)
        if self.bo is not None:
            self.nc.tensor.matmul(o, self.c.ones[0:1, :], self.bo[:, :], start=True, stop=False)
        self.nc.tensor.matmul(o, self.oT[:, :], self.wo[:, :], start=self.bo is None, stop=True).then_inc(self.o_done, 1)

    def pe_start(self, pe):
        self.pe_rows(pe, 0, 0)
        self.pe_queries(pe, 0, 0)
        self.pe_keys(pe, 0, 0)
        self.pe_values(pe, 0, 0)
        self.pe_scores(pe, 0, 0, 0, 0)
        self.pe_scores(pe, 0, 0, 0, 1)

    def pe(self, pe, now, nxt):
        for s in range(self.STEPS):
            t, q = s // self.CH, s % self.CH
            ahead2 = self.later(s + 2, now, nxt)
            if ahead2:
                self.pe_scores(pe, *ahead2)
            pe.wait_ge(self.pr_ready, self.CH * TPG * now[2] + s + 1)
            for j in range(4):
                m = self.nc.tensor.transpose(self.tb[q % 2][:, j * P:(j + 1) * P], self.pr[q % 4][:, j * P:(j + 1) * P],
                                             self.c.ident[:, :])
            m.then_inc(self.t_done, 1)
            if s == 1:
                pe.wait_ge(self.vbd_ready, 16 * (now[2] + 1))
            tile = self.before(t, now)
            if s:
                self.pe_heads(pe, now[1], now[2], (s - 1) // self.CH, (s - 1) % self.CH)
            elif tile:
                self.pe_heads(pe, tile[0], tile[1], tile[2], self.CH - 1)
            if tile and q == 1:
                self.pe_sums(pe, tile)
            if tile and q == 4:
                self.pe_project(pe, tile)
            if nxt:
                _, u, k = nxt
                if s == 16:
                    self.pe_rows(pe, u, k)
                if s == 18:
                    self.pe_queries(pe, u, k)
                if s == 20:
                    self.pe_keys(pe, u, k)
                if s == 22:
                    self.pe_values(pe, u, k)

    def pe_end(self, pe):
        tile = self.last_tile()
        self.pe_heads(pe, tile[0], tile[1], tile[2], self.CH - 1)
        self.pe_sums(pe, tile)
        self.pe_project(pe, tile)


def window_attention(nc, c, name, w):
    with Phase(nc, name) as ph:
        HALF, NG = 32, 16
        wq, wk, wv, wo = (ph.sb(s, [P, D]) for s in ("wq", "wk", "wv", "wo"))
        gi, gf, gneg = ph.sb("gi", [P, NG], I32), ph.sb("gf", [P, NG]), ph.sb("gneg", [P, NG])
        posi, pos = ph.sb("posi", [P, 2], I32), ph.sb("pos", [P, 2])
        cposi, cpos = ph.sb("cposi", [P, SEQ], I32), ph.sb("cpos", [P, SEQ])
        hit, hit_q, hit_k = ph.sb("hit", [P, NG, SEQ]), ph.sb("hit_q", [P, 2]), ph.sb("hit_k", [P, SEQ])
        near, far, mask = ph.sb("near", [P, 2, SEQ]), ph.sb("far", [P, 2, SEQ]), ph.sb("mask", [P, 2, SEQ], BF16)
        at = FullAttention(ph, c, wq, wk, wv, wo, mask=mask)
        fr = at.fr
        weights, placed, step = ph.sem("weights"), ph.sem("placed"), ph.sem("step")
        block = ph.block()

        @block.sync
        def _(sp):
            for dst, src in ((wq, "Wq"), (wk, "Wk"), (wv, "Wv"), (wo, "Wo")):
                sp.dma_start(dst[:], w["L2_attn_" + src]).then_inc(weights, 16)
            sp.dma_start(gi[:, :], w["L2_attn_global_token_indices"][0, :].partition_broadcast(P)).then_inc(weights, 16)
            sp.wait_ge(weights, 80)

        @block.gpsimd
        def _(g):
            nc.gpsimd.iota(posi[:, :], pattern=[[P, 2]], base=0, channel_multiplier=1).then_inc(placed, 1)
            nc.gpsimd.iota(cposi[:, :], pattern=[[1, SEQ]], base=0, channel_multiplier=0).then_inc(placed, 1)
            at.pool_setup(g)
            ahead(g, GROUPS, 2, lambda i, u, k: fr.pool(g, k), lambda i, u, k: None)

        @block.vector
        def _(v):
            done = [0]

            def link(ins):
                done[0] += 1
                ins.then_inc(step, 1)
                v.wait_ge(step, done[0])

            v.wait_ge(weights, 80)
            v.wait_ge(placed, 2)
            link(nc.vector.tensor_copy(c.ident_b[:, :], c.ident[:, :]))
            link(nc.vector.tensor_copy(pos[:, :], posi[:, :]))
            link(nc.vector.tensor_copy(cpos[:, :], cposi[:, :]))
            link(nc.vector.tensor_copy(gf[:, :], gi[:, :]))
            link(nc.vector.tensor_scalar(gneg[:, :], gf[:, :], 0.0, float(SEQ), ALU.is_lt, ALU.mult))
            link(nc.vector.tensor_tensor(gf[:, :], gf[:, :], gneg[:, :], ALU.add))
            link(nc.vector.tensor_tensor(hit[:, :, :], cpos[:, :].unsqueeze(1).to_broadcast([P, NG, SEQ]),
                                         gf[:, :].unsqueeze(2).to_broadcast([P, NG, SEQ]), ALU.is_equal))
            link(nc.vector.tensor_reduce(hit_k[:, :], hit[:, :, :].rearrange("p g s -> p s g"), AX_X, ALU.max))
            for t in range(2):
                link(nc.vector.tensor_scalar(gneg[:, :], gf[:, :], pos[:, t:t + 1], None, ALU.is_equal))
                link(nc.vector.tensor_reduce(hit_q[:, t:t + 1], gneg[:, :], AX_X, ALU.max))
                d = near[:, t, :]
                link(nc.vector.tensor_scalar(d, cpos[:, :], pos[:, t:t + 1], None, ALU.subtract))
                link(nc.vector.tensor_scalar(far[:, t, :], d, -1.0, None, ALU.mult))
                link(nc.vector.tensor_tensor(d, d, far[:, t, :], ALU.max))
                link(nc.vector.tensor_scalar(d, d, float(HALF), hit_q[:, t:t + 1], ALU.is_le, ALU.max))
                link(nc.vector.tensor_tensor(d, d, hit_k[:, :], ALU.max))
                link(nc.vector.tensor_scalar(mask[:, t, :], d, -1.0, 1e30, ALU.add, ALU.mult))
            v.wait_ge(at.made, at.MADE)

            def finish(tile, o):
                xt = c.x[:, bass.ds(tile[3], 1), :]
                nc.vector.tensor_tensor(xt, o.unsqueeze(1), xt, ALU.add).then_inc(at.o_free, 1)

            at.dve_start(v)
            weave(v, GROUPS, 2, lambda now, nxt: at.dve(v, now, nxt, finish))
            at.dve_end(v, finish)

        @block.scalar
        def _(a):
            at.act_start(a)
            weave(a, GROUPS, 2, lambda now, nxt: at.act(a, now, nxt))

        @block.tensor
        def _(pe):
            pe.wait_ge(weights, 80)
            pe.wait_ge(step, 8 + 2 * 8)
            at.pe_start(pe)
            weave(pe, GROUPS, 2, lambda now, nxt: at.pe(pe, now, nxt))
            at.pe_end(pe)


class Mixture:

    def __init__(self, nc, ctx, name, E):
        self.R = D + E + 1
        self.rows = nc.dram_tensor(f"{name}_rows", (SLOTS, self.R), F32, kind="Internal").ap()
        self.tables = [nc.dram_tensor(f"{name}_table{i}", (TOKENS + SUB, D), F32, kind="Internal").ap()
                       for i in range(TABLES)]
        self.cleared = ctx.enter_context(nc.semaphore(f"{name}_cleared"))

    CLEARED = 16 * (1 + 2 * TABLES)


def clear_next(c, sp):
    if not c.to_clear:
        return
    m = c.to_clear.pop(0)
    sp.dma_start(m.rows.rearrange("(n p) r -> p n r", p=SUB),
                 c.blank[0:SUB, -m.R:].unsqueeze(1).to_broadcast([SUB, SLOTS // SUB, m.R])).then_inc(m.cleared, 16)
    for t in m.tables:
        sp.dma_start(t[0:TOKENS, :].rearrange("(n p) d -> p n d", p=P),
                     c.zero[:, :].unsqueeze(1).to_broadcast([P, TILES, D])).then_inc(m.cleared, 16)
        sp.dma_start(t[TOKENS:TOKENS + SUB, :], c.zero[0:SUB, :]).then_inc(m.cleared, 16)


class Shared:

    F = 3

    def __init__(self, ph, c, w1, w2):
        self.nc, self.c, self.w1, self.w2 = ph.nc, c, w1, w2
        self.hb = [[ph.bank(f"h{j}{i}") for i in range(2)] for j in range(2)]
        self.ob = ph.bank("o")
        self.sT, self.gT = ph.sb("sT", [P, 2, GT]), ph.sb("gT", [P, self.F, GT])
        self.h_done, self.silu_ready, self.gT_ready, self.o_done, self.o_free = (
            ph.sem(s) for s in ("h_done", "silu_ready", "gT_ready", "o_done", "o_free"))

    def pe_hidden(self, pe, k, xT, f):
        n = self.F * k + f
        pe.wait_ge(self.gT_ready, n + 1 if f > 1 else n + 1)
        for j in range(2):
            m = self.nc.tensor.matmul(self.hb[j][f % 2][:, :], self.w1[:, (self.F * j + f) * P:(self.F * j + f + 1) * P],
                                      xT[:, :], start=True, stop=True)
        m.then_inc(self.h_done, 1)

    def pe(self, pe, k, xT):
        for f in range(self.F):
            self.pe_hidden(pe, k, xT, f)
        pe.wait_ge(self.gT_ready, self.F * (k + 1) + 2)
        pe.wait_ge(self.o_free, k + 1)
        for t in range(TPG):
            for f in range(self.F):
                m = self.nc.tensor.matmul(self.ob[:, t * D:(t + 1) * D], self.gT[:, f, t * P:(t + 1) * P],
                                          self.w2[:, f, :], start=(f == 0), stop=(f == self.F - 1))
        m.then_inc(self.o_done, 1)

    def act(self, a, k):
        for f in range(self.F):
            n = self.F * k + f
            a.wait_ge(self.h_done, n + 1)
            a.wait_ge(self.gT_ready, n + 1)
            self.nc.scalar.activation(self.sT[:, n_par(k, f), :], self.hb[1][f % 2][:, :],
                                      ACT.Silu).then_inc(self.silu_ready, 1)

    def dve_init(self, v):
        v.sem_inc(self.gT_ready, 2)
        v.sem_inc(self.o_free, 1)

    def dve_gate(self, v, k, f):
        v.wait_ge(self.silu_ready, self.F * k + f + 1)
        self.nc.vector.tensor_tensor(self.gT[:, f, :], self.hb[0][f % 2][:, :], self.sT[:, n_par(k, f), :],
                                     ALU.mult).then_inc(self.gT_ready, 1)

    def dve_add(self, v, k):
        v.wait_ge(self.o_done, k + 1)
        xt = tiles4(self.c.x, k)
        self.nc.vector.scalar_tensor_tensor(out=xt, in0=self.ob[:, :].rearrange("p (t d) -> p t d", t=TPG), scalar=0.5,
                                            in1=xt, op0=ALU.mult, op1=ALU.add).then_inc(self.o_free, 1)


def n_par(k, f):
    return f % 2


def route(nc, c, name, w, source, m, gate, E, K, CAP, kind, shared=None):
    with Phase(nc, name) as ph:
        R = D + E + 1
        wg = ph.sb("wg", [P, E])
        row = [ph.sb(f"row{i}", [P, TPG, R]) for i in range(2)]
        rows = m.rows
        idx = [ph.sb(f"idx{i}", [P, TPG, K], U32) for i in range(2)]
        first_slot = ph.sb("first_slot", [P, E])
        lg, gates, slot, over = (ph.sb(s, [P, TPG, E]) for s in ("lg", "gates", "slot", "over"))
        top, topi, topf = ph.sb("top", [P, TPG, 8]), ph.sb("topi", [P, TPG, 8], U32), ph.sb("topf", [P, TPG * K])
        slotf, mx, total = ph.sb("slotf", [P, TPG * K]), ph.sb("mx", [P, TPG]), ph.sb("total", [P, TPG])
        hot, pick = ph.sb("hot", [P, TPG * K, E]), ph.sb("pick", [P, TPG * K, E])
        mask, cum = ph.sb("mask", [P, TPG, E], BF16), [ph.sb(f"cum{i}", [P, E], BF16) for i in range(2)]
        part = ph.sb("part", [P, E], BF16)
        if shared:
            sw1, sw2 = ph.sb("sw1", [P, 768]), ph.sb("sw2", [P, 3, D])
            sh = Shared(ph, c, sw1, sw2)
        fr = Front(ph, c, source, norm=(kind == "softmax"), at_once=True)
        lb, rb = ph.bank("logits"), ph.bank("rank")
        (weights, consts, row_ready, l_done, l_ready, e_ready, steps, masked, ranked, cum_ready, sent_ready) = (
            ph.sem(s) for s in ("weights", "consts", "row_ready", "l_done", "l_ready", "e_ready", "steps", "masked",
                                "ranked", "cum_ready", "sent_ready"))
        sent, rows_free = ph.sem("sent"), ph.sem("rows_free")
        PER = 16 * TPG * K
        block = ph.block()
        loads = [(wg, gate)] + ([(sw1, "L0_ffn_shared_w1"), (sw2, "L0_ffn_shared_w2")] if shared else [])

        @block.sync
        def _(sp):
            for dst, src in loads:
                sp.dma_start(dst[:], w[src]).then_inc(weights, 16)
            sp.wait_ge(weights, 16 * len(loads))

        @block.gpsimd
        def _(g):
            g.sem_inc(rows_free, 2)
            fr.pool_start(g)

            def body(i, u, k):
                hold(g, c.mark_g, row_ready, k + 1)
                hold(g, c.mark_g, sent_ready, k + 1)
                for t in range(TPG):
                    for j in range(K):
                        g.indirect_dma_start(out=rows, out_offset=bass.IndirectOffsetOnAxis(
                            ap=idx[u][:, t, j:j + 1], axis=0), in_=row[u][:, t, :], in_offset=None,
                            bounds_check=SLOTS - 1, oob_is_err=False).then_inc(sent, 16)
                hold(g, rows_free, sent, PER * (k + 1))

            g.wait_ge(m.cleared, m.CLEARED)
            ahead(g, GROUPS, 2, lambda i, u, k: fr.pool(g, k), body)

        @block.vector
        def _(v):
            nc.vector.tensor_scalar(first_slot[:, :], c.expert_id[:, 0:E], float(CAP), None, ALU.mult).then_inc(consts, 1)
            nc.vector.memset(cum[0][:, :], 0.0).then_inc(consts, 1)
            fr.dve_start(v)
            if shared:
                sh.dve_init(v)
            STEPS = 19 if kind == "softmax" else 16

            def front(i, u, k):
                if not isinstance(k, int) or k >= 2:
                    v.wait_ge(row_ready, k - 1)
                fr.dve(v, k, u)

            def body(i, u, k):
                done = [0]

                def link(*ins, wait=True):
                    for x in ins:
                        x.then_inc(steps, 1)
                    done[0] += 1 if len(ins) == 1 else 0
                    if wait:
                        v.wait_ge(steps, STEPS * k + done[0])

                v.wait_ge(l_done, k + 1)
                l3 = lb[:, 0:TPG * E].rearrange("p (t e) -> p t e", t=TPG)

                def spread(a):
                    return a.unsqueeze(2).to_broadcast([P, TPG, E])

                if kind == "softmax":
                    link(nc.vector.tensor_reduce(mx[:, :], l3, AX_X, ALU.max))
                    nc.vector.tensor_tensor(lg[:, :, :], l3, spread(mx[:, :]), ALU.subtract).then_inc(l_ready, 1)
                    v.wait_ge(e_ready, k + 1)
                    link(nc.vector.tensor_reduce(mx[:, :], lg[:, :, :], AX_X, ALU.add))
                    link(nc.vector.reciprocal(mx[:, :], mx[:, :]))
                    link(nc.vector.tensor_tensor(gates[:, :, :], lg[:, :, :], spread(mx[:, :]), ALU.mult), wait=False)
                else:
                    v.wait_ge(e_ready, k + 1)
                    link(nc.vector.tensor_copy(gates[:, :, :], lg[:, :, :]), wait=False)
                hold(v, c.mark_v, steps, STEPS * k + done[0])
                for t in range(TPG):
                    m = nc.vector.max(top[:, t, :], gates[:, t, :])
                link(m, wait=False)
                hold(v, c.mark_v, steps, STEPS * k + done[0])
                for t in range(TPG):
                    m = nc.vector.max_index(topi[:, t, :], top[:, t, :], gates[:, t, :])
                link(m)
                link(nc.vector.tensor_copy(topf[:, :].rearrange("p (t j) -> p t j", t=TPG), topi[:, :, 0:K]))
                link(nc.vector.tensor_tensor(hot[:, :, :],
                                             c.expert_id[:, 0:E].unsqueeze(1).to_broadcast([P, TPG * K, E]),
                                             topf[:, :].unsqueeze(2).to_broadcast([P, TPG * K, E]), ALU.is_equal))
                with nc.allow_low_precision("zeros and ones"):
                    nc.vector.tensor_reduce(mask[:, :, :], hot[:, :, :].rearrange("p (t j) e -> p t e j", t=TPG), AX_X,
                                            ALU.add).then_inc(masked, 1)
                v.wait_ge(masked, k + 1)
                with nc.allow_low_precision("counts up to 32"):
                    link(nc.vector.tensor_reduce(part[:, :], mask[:, :, :].rearrange("p t e -> p e t"), AX_X, ALU.add))
                    nc.vector.tensor_tensor(cum[1 - u][:, :], cum[u][:, :], part[:, :], ALU.add).then_inc(cum_ready, 1)
                if shared:
                    for f in range(2):
                        sh.dve_gate(v, k, f)
                link(nc.vector.tensor_reduce(total[:, :], top[:, :, 0:K], AX_X, ALU.add))
                if kind == "softmax":
                    link(nc.vector.tensor_scalar(total[:, :], total[:, :], 2.0 ** -23, None, ALU.max))
                else:
                    link(nc.vector.tensor_scalar(total[:, :], total[:, :], 1e-6, None, ALU.add))
                link(nc.vector.reciprocal(total[:, :], total[:, :]))
                v.wait_ge(rows_free, k + 1)
                link(nc.vector.tensor_tensor(row[u][:, :, D:D + E], gates[:, :, :], spread(total[:, :]), ALU.mult),
                     wait=False)
                nc.vector.tensor_copy(row[u][:, :, R - 1:R], c.token_id[:, bass.ds(TPG * k, TPG)].unsqueeze(2)
                                      ).then_inc(steps, 1)
                done[0] += 1
                v.wait_ge(ranked, k + 1)
                r3 = rb[:, 0:TPG * E].rearrange("p (t e) -> p t e", t=TPG)
                link(nc.vector.tensor_scalar(over[:, :, :], r3, float(CAP), FAR, ALU.is_ge, ALU.mult), wait=False)
                link(nc.vector.tensor_tensor(slot[:, :, :], r3,
                                             first_slot[:, :].unsqueeze(1).to_broadcast([P, TPG, E]), ALU.add))
                link(nc.vector.tensor_tensor(slot[:, :, :], slot[:, :, :], over[:, :, :], ALU.add))
                link(nc.vector.tensor_tensor(pick[:, :, :].rearrange("p (t j) e -> p t j e", t=TPG),
                                             hot[:, :, :].rearrange("p (t j) e -> p t j e", t=TPG),
                                             slot[:, :, :].unsqueeze(2).to_broadcast([P, TPG, K, E]), ALU.mult))
                link(nc.vector.tensor_reduce(slotf[:, :], pick[:, :, :], AX_X, ALU.add))
                assert done[0] == STEPS, done
                nc.vector.tensor_copy(idx[u][:, :, :].rearrange("p t j -> p (t j)"), slotf[:, :]).then_inc(sent_ready, 1)
                if shared:
                    sh.dve_gate(v, k, 2)
                    sh.dve_add(v, k)

            ahead(v, GROUPS, 2, front, body)

        @block.scalar
        def _(a):
            def body(i, u, k):
                if kind == "softmax":
                    a.wait_ge(l_ready, k + 1)
                    nc.scalar.activation(lg[:, :, :], lg[:, :, :], ACT.Exp).then_inc(e_ready, 1)
                else:
                    a.wait_ge(l_done, k + 1)
                    nc.scalar.activation(lg[:, :, :], lb[:, 0:TPG * E].rearrange("p (t e) -> p t e", t=TPG),
                                         ACT.Sigmoid).then_inc(e_ready, 1)
                a.wait_ge(rows_free, k + 1)
                nc.scalar.activation(row[u][:, :, 0:D], fr.xn[u][:, :, :], ACT.Copy).then_inc(row_ready, 1)
                if shared:
                    sh.act(a, k)

            ahead(a, GROUPS, 2, lambda i, u, k: fr.act(a, k, u), body)

        @block.tensor
        def _(pe):
            pe.wait_ge(weights, 16 * len(loads))
            pe.wait_ge(consts, 2)

            def body(i, u, k):
                pe.wait_ge(fr.xnT_ready, k + 1)
                if not first(k):
                    pe.wait_ge(e_ready, k)
                for t in range(TPG):
                    m = nc.tensor.matmul(lb[:, t * E:(t + 1) * E], fr.xnT[u][:, t * P:(t + 1) * P], wg[:, :],
                                         start=True, stop=True)
                m.then_inc(l_done, 1)
                if shared:
                    for f in range(2):
                        sh.pe_hidden(pe, k, fr.xnT[u], f)
                pe.wait_ge(masked, k + 1)
                if not first(k):
                    pe.wait_ge(cum_ready, k)
                    pe.wait_ge(sent_ready, k)
                for t in range(TPG):
                    o = rb[:, t * E:(t + 1) * E]
                    nc.tensor.matmul(o, c.ones_b[:, :], cum[u][:, :], start=True, stop=False)
                    for b in range(t):
                        nc.tensor.matmul(o, c.ones_b[:, :], mask[:, b, :], start=False, stop=False)
                    m = nc.tensor.matmul(o, c.below_b[:, :], mask[:, t, :], start=False, stop=True)
                m.then_inc(ranked, 1)
                if shared:
                    sh.pe_hidden(pe, k, fr.xnT[u], 2)
                    pe.wait_ge(sh.gT_ready, 3 * (k + 1) + 2)
                    pe.wait_ge(sh.o_free, k + 1)
                    for t in range(TPG):
                        for f in range(3):
                            m = nc.tensor.matmul(sh.ob[:, t * D:(t + 1) * D], sh.gT[:, f, t * P:(t + 1) * P],
                                                 sw2[:, f, :], start=(f == 0), stop=(f == 2))
                    m.then_inc(sh.o_done, 1)

            ahead(pe, GROUPS, 2, lambda i, u, k: fr.pe(pe, k, u), body)


def experts(nc, c, name, w, rows, tables, w1d, w2d, E, C1, KC, A, gated):
    with Phase(nc, name) as ph:
        R = D + E + 1
        S, U = A * SUB, 4
        units = SLOTS // S
        w1 = [ph.sb(f"w1_{i}", [P, C1 * P]) for i in range(U)]
        w2 = [ph.sb(f"w2_{i}", [P, KC, D]) for i in range(U)]
        row = [ph.sb(f"row{i}", [SUB, A, R]) for i in range(U)]
        xeT = [ph.sb(f"xeT{i}", [P, S]) for i in range(2)]
        sT = [ph.sb(f"sT{i}", [P, KC * S]) for i in range(2)]
        gT = [ph.sb(f"gT{i}", [P, KC * S]) for i in range(2)]
        y = [ph.sb(f"y{i}", [SUB, A, D]) for i in range(2)]
        idx = [ph.sb(f"idx{i}", [SUB, A], U32) for i in range(2)]
        xb = ph.bank("x")
        hb = [[ph.bank(f"h{i}{j}") for j in range(2)] for i in range(2)]
        ob = [ph.bank(f"o{i}") for i in range(2)]
        loaded = [ph.sem(f"loaded{i}") for i in range(U)]
        added = [ph.sem(f"added{i}") for i in range(TABLES)]
        turned, xe_ready, h_done, s_ready, g_ready, o_done, y_ready, idx_ready = (
            ph.sem(s) for s in ("turned", "xe_ready", "h_done", "s_ready", "g_ready", "o_done", "y_ready", "idx_ready"))
        block = ph.block()

        def expert(i, u):
            return U * i + u if units == E else i

        def table(p, a):
            return (a + A * p) % TABLES

        def uses(n, p, a):
            if A == TABLES:
                return n
            return n // 2 if isinstance(n, int) else (n - p) // 2

        @block.sync
        def _(sp):
            def load(i, u):
                n = U * i + u
                if not isinstance(n, int) or n >= U:
                    sp.wait_ge(y_ready, n - U + 1)
                e = expert(i, u)
                for dst, src in ((row[u][:, :, :], rows[bass.ds(S * n, S), :].rearrange("(a p) r -> p a r", p=SUB)),
                                 (w1[u][:, :], w1d[bass.ds(e, 1), :, :].rearrange("a p f -> (a p) f")),
                                 (w2[u][:, :, :], w2d[bass.ds(e, 1), :, :, :].rearrange("a p c d -> (a p) c d"))):
                    sp.dma_start(dst, src).then_inc(loaded[u], 16)

            for u in range(U):
                load(0, u)
            with sp.Fori(1, units // U) as i:
                for u in range(U):
                    load(i, u)

        @block.tensor
        def _(pe):
            def turn(i, u, n):
                pe.wait_ge(loaded[u], 48 * (i + 1))
                if not first(n):
                    pe.wait_ge(xe_ready, n)
                for a in range(A):
                    m = nc.tensor.transpose(xb[:, a * SUB:(a + 1) * SUB], row[u][:, a, 0:D], c.ident[0:SUB, 0:SUB])
                m.then_inc(turned, 1)

            def hidden(i, u, n):
                p = u % 2
                pe.wait_ge(xe_ready, n + 1)
                for f in range(C1):
                    o = hb[p][f // 3][:, (f % 3) * S:(f % 3 + 1) * S] if gated else hb[p][f][:, 0:S]
                    m = nc.tensor.matmul(o, w1[u][:, f * P:(f + 1) * P], xeT[p][:, :], start=True, stop=True)
                m.then_inc(h_done, 1)

            def output(i, u, n):
                p = u % 2
                pe.wait_ge(g_ready, n + 1)
                if not isinstance(n, int) or n >= 2:
                    pe.wait_ge(y_ready, n - 1)
                for a in range(A):
                    for f in range(KC):
                        m = nc.tensor.matmul(ob[p][0:SUB, a * D:(a + 1) * D],
                                             gT[p][:, f * S + a * SUB:f * S + (a + 1) * SUB],
                                             w2[u][:, f, :], start=(f == 0), stop=(f == KC - 1))
                m.then_inc(o_done, 1)

            def step(at):
                if at(1):
                    hidden(*at(1))
                if at(2):
                    turn(*at(2))
                output(*at(0))

            turn(0, 0, 0)
            hidden(0, 0, 0)
            turn(0, 1, 1)
            stream(pe, units, U, step)

        @block.scalar
        def _(a_):
            def copy(i, u, n):
                a_.wait_ge(turned, n + 1)
                nc.scalar.activation(xeT[u % 2][:, :], xb[:, 0:S], ACT.Copy).then_inc(xe_ready, 1)

            def bend(i, u, n):
                p = u % 2
                a_.wait_ge(h_done, n + 1)
                if gated:
                    nc.scalar.activation(sT[p][:, :], hb[p][1][:, 0:KC * S], ACT.Silu).then_inc(s_ready, 1)
                else:
                    for f in range(KC):
                        m = nc.scalar.activation(gT[p][:, f * S:(f + 1) * S], hb[p][f][:, 0:S], ACT.Gelu)
                    m.then_inc(g_ready, 1)

            def step(at):
                bend(*at(0))
                if at(2):
                    copy(*at(2))

            copy(0, 0, 0)
            copy(0, 1, 1)
            stream(a_, units, U, step)

        @block.vector
        def _(v):
            def step(at):
                i, u, n = at(0)
                p = u % 2
                if gated:
                    v.wait_ge(s_ready, n + 1)
                    nc.vector.tensor_tensor(gT[p][:, :], hb[p][0][:, 0:KC * S], sT[p][:, :], ALU.mult).then_inc(g_ready, 1)
                if not isinstance(n, int) or n >= 2:
                    for a in range(A):
                        v.wait_ge(added[table(p, a)], 16 * uses(n, p, a))
                v.wait_ge(loaded[u], 48 * (i + 1))
                nc.vector.tensor_copy(idx[p][:, :], row[u][:, :, R - 1]).then_inc(idx_ready, 1)
                v.wait_ge(o_done, n + 1)
                nc.vector.tensor_tensor(y[p][:, :, :], ob[p][0:SUB, 0:A * D].rearrange("p (a d) -> p a d", a=A),
                                        row[u][:, :, bass.ds(D + expert(i, u), 1)].to_broadcast([SUB, A, D]),
                                        ALU.mult).then_inc(y_ready, 1)

            stream(v, units, U, step)

        @block.gpsimd
        def _(g):
            def step(at):
                i, u, n = at(0)
                p = u % 2
                hold(g, c.mark_g, idx_ready, n + 1)
                hold(g, c.mark_g, y_ready, n + 1)
                for a in range(A):
                    t = table(p, a)
                    if not first(uses(n, p, a)):
                        hold(g, c.mark_g, added[t], 16 * uses(n, p, a))
                    g.indirect_dma_start(out=tables[t], out_offset=bass.IndirectOffsetOnAxis(
                        ap=idx[p][:, a:a + 1], axis=0), in_=y[p][:, a, :], in_offset=None,
                        bounds_check=TOKENS + SUB - 1, oob_is_err=True, compute_op=ALU.add).then_inc(added[t], 16)

            stream(g, units, U, step)
            for t in range(TABLES):
                g.wait_ge(added[t], 16 * (units * A // TABLES))


def combine(nc, c, name, tables, source=None, norm=None, w=None):
    with Phase(nc, name) as ph:
        acc = [ph.sb(f"acc{i}", [P, TABLES, GT]) for i in range(2)]
        s01, s23 = ph.sb("s01", [P, GT]), ph.sb("s23", [P, GT])
        loaded = [ph.sem(f"loaded{i}") for i in range(2)]
        steps, free, weights, squared = ph.sem("steps"), ph.sem("free"), ph.sem("weights"), ph.sem("squared")
        if source is not None:
            nw, sq, ss = ph.sb("nw", [P, D]), ph.sb("sq", [P, TPG, D]), ph.sb("ss", [P, TPG])
            rms = Rsqrt(ph, c, "rms", TPG)
        block = ph.block()

        @block.sync
        def _(sp):
            if source is not None:
                sp.dma_start(nw[:, :], w[norm][0, :].partition_broadcast(P)).then_inc(weights, 16)

            def load(i, u):
                k = 2 * i + u
                if not isinstance(k, int) or k >= 2:
                    sp.wait_ge(free, k - 1)
                for t in range(TABLES):
                    sp.dma_start(acc[u][:, t, :].rearrange("p (t d) -> p t d", t=TPG),
                                 tables[t][bass.ds(GT * k, GT), :].rearrange("(t p) d -> p t d", p=P)
                                 ).then_inc(loaded[u], 16)

            for u in range(2):
                load(0, u)
            with sp.Fori(1, GROUPS // 2) as i:
                for u in range(2):
                    load(i, u)
            clear_next(c, sp)

        if source is not None:
            @block.scalar
            def _(a):
                def body(i, u, k):
                    a.wait_ge(steps, 2 * k + 2)
                    for t in range(TPG):
                        m = nc.scalar.activation(sq[:, t, :], s01[:, t * D:(t + 1) * D], ACT.Square,
                                                 accum_out=ss[:, t:t + 1])
                    m.then_inc(squared, 1)

                ahead(a, GROUPS, 2, lambda i, u, k: None, body)

            @block.gpsimd
            def _(g):
                ahead(g, GROUPS, 2, lambda i, u, k: None, lambda i, u, k: rms.pool(g, k))

        @block.vector
        def _(v):
            if source is not None:
                v.wait_ge(weights, 16)

            def body(i, u, k):
                if not first(k):
                    v.wait_ge(applied, k)
                v.wait_ge(loaded[u], 16 * TABLES * (i + 1))
                nc.vector.tensor_tensor(s01[:, :], acc[u][:, 0, :], acc[u][:, 1, :], ALU.add)
                nc.vector.tensor_tensor(s23[:, :], acc[u][:, 2, :], acc[u][:, 3, :], ALU.add).then_inc(free, 1)
                v.wait_ge(free, k + 1)
                nc.vector.tensor_tensor(s01[:, :], s01[:, :], s23[:, :], ALU.add).then_inc(steps, 1)
                v.wait_ge(steps, (1 if source is None else 2) * k + 1)
                s3 = s01[:, :].rearrange("p (t d) -> p t d", t=TPG)
                xt = tiles4(c.x, k)
                if source is None:
                    nc.vector.scalar_tensor_tensor(out=xt, in0=s3, scalar=0.5, in1=xt, op0=ALU.mult, op1=ALU.add
                                                   ).then_inc(applied, 1)
                    return
                nc.vector.tensor_tensor(s3, s3, tiles4(source, k), ALU.add).then_inc(steps, 1)
                v.wait_ge(squared, k + 1)
                rms.dve(v, ss[:, :], k, 1.0 / D, RMS_EPS)
                v.wait_ge(rms.solved, k + 1)
                s23_3 = s23[:, :].rearrange("p (t d) -> p t d", t=TPG)
                for t in range(TPG):
                    m = nc.vector.scalar_tensor_tensor(out=s23_3[:, t, :], in0=s3[:, t, :], scalar=rms.y[:, t:t + 1],
                                                       in1=nw[:, :], op0=ALU.mult, op1=ALU.mult)
                m.then_inc(squared_out, 1)
                v.wait_ge(squared_out, k + 1)
                nc.vector.scalar_tensor_tensor(out=xt, in0=s23_3, scalar=0.5, in1=xt, op0=ALU.mult, op1=ALU.add
                                               ).then_inc(applied, 1)

            squared_out, applied = ph.sem("normed"), ph.sem("applied")
            each(v, GROUPS, 2, body)


def moe64(nc, c, name, w):
    m = c.mixtures[name]
    route(nc, c, name + "r", w, c.x, m, "L0_ffn_wg", 64, 8, 160, "softmax", shared=True)
    experts(nc, c, name + "e", w, m.rows, m.tables, w["L0_ffn_expert_w1"], w["L0_ffn_expert_w2"], 64, 6, 3, 2, True)
    combine(nc, c, name + "c", m.tables)


def gqa_moe(nc, c, name, w):
    m = c.mixtures[name]
    with ExitStack() as ctx:
        src = ctx.enter_context(nc.sbuf_tensor(name + "_src", [P, TILES, D], F32))
        grouped_attention(nc, c, name + "a", w, src)
        route(nc, c, name + "r", w, src, m, "L3_ffn_gate_w", 8, 2, 1280, "sigmoid")
        experts(nc, c, name + "e", w, m.rows, m.tables, w["L3_ffn_w1"], w["L3_ffn_w2"], 8, 2, 2, 4, False)
        combine(nc, c, name + "c", m.tables, source=src, norm="L3_ffn_norm2_w", w=w)


def grouped_attention(nc, c, name, w, src):
    with Phase(nc, name) as ph:
        wq, wk, wv, wo = (ph.sb(s, [P, D]) for s in ("wq", "wk", "wv", "wo"))
        bq, bqs, bk = ph.sb("bq", [P, 1]), ph.sb("bqs", [P, 1]), ph.sb("bk", [P, 1])
        bv, bo, nw = ph.sb("bv", [1, D]), ph.sb("bo", [1, D]), ph.sb("nw", [P, D])
        at = FullAttention(ph, c, wq, wk, wv, wo, bq=bqs, bk=bk, bv=bv, bo=bo)
        fr = at.fr
        sg = [ph.sb(f"sg{i}", [P, TPG, D]) for i in range(2)]
        sq, ss = ph.sb("sq", [P, TPG, D]), ph.sb("ss", [P, TPG])
        rms = Rsqrt(ph, c, "rms", TPG)
        weights, ready, sg_ready, squared = ph.sem("weights"), ph.sem("ready"), ph.sem("sg_ready"), ph.sem("squared")
        block = ph.block()

        @block.sync
        def _(sp):
            for dst, s in ((wq, "qw"), (wk, "kw"), (wv, "vw"), (wo, "ow"), (bq, "qb"), (bk, "kb"), (bv, "vb"),
                           (bo, "ob")):
                sp.dma_start(dst[:], w["L3_ffn_" + s]).then_inc(weights, 16)
            sp.dma_start(nw[:, :], w["L3_ffn_norm1_w"][0, :].partition_broadcast(P)).then_inc(weights, 16)
            sp.wait_ge(weights, 144)

        @block.gpsimd
        def _(g):
            at.pool_setup(g)
            fr.pool(g, 0)

            def group(now, nxt):
                if not first(now[2]):
                    rms.pool(g, now[2] - 1)
                if nxt:
                    fr.pool(g, nxt[2])

            weave(g, GROUPS, 2, group)
            rms.pool(g, GROUPS - 1)

        @block.vector
        def _(v):
            v.wait_ge(weights, 144)
            nc.vector.tensor_scalar(bqs[:, :], bq[:, :], at.DK ** -0.5, None, ALU.mult).then_inc(ready, 1)
            v.wait_ge(at.made, at.MADE)
            at.dve_start(v)

            def finish(tile, o):
                u, k, t, n = tile
                nc.vector.tensor_tensor(sg[u][:, t, :], o, fr.xn[u][:, t, :], ALU.add).then_inc(at.o_free, 1)

            def root(k):
                v.wait_ge(squared, k + 1)
                rms.dve(v, ss[:, :], k, 1.0 / D, RMS_EPS)

            def scale(u, k):
                v.wait_ge(rms.solved, k + 1)
                for t in range(TPG):
                    nc.vector.scalar_tensor_tensor(out=src[:, bass.ds(TPG * k + t, 1), :], in0=sg[u][:, t:t + 1, :],
                                                   scalar=rms.y[:, t:t + 1], in1=nw[:, :].unsqueeze(1),
                                                   op0=ALU.mult, op1=ALU.mult)

            def group(now, nxt):
                def between(s):
                    if not first(now[2]):
                        if s == 8:
                            root(now[2] - 1)
                        if s == 12:
                            scale(1 - now[1], now[2] - 1)

                at.dve(v, now, nxt, finish, between)

            weave(v, GROUPS, 2, group)
            at.dve_end(v, finish)
            root(GROUPS - 1)
            scale(1, GROUPS - 1)

        @block.scalar
        def _(a):
            a.wait_ge(ready, 1)
            at.act_start(a)

            def squares(u, k):
                a.wait_ge(at.o_free, TPG * (k + 1))
                for t in range(TPG):
                    m = nc.scalar.activation(sq[:, t, :], sg[u][:, t, :], ACT.Square, accum_out=ss[:, t:t + 1])
                m.then_inc(squared, 1)

            def group(now, nxt):
                at.act(a, now, nxt,
                       lambda s: squares(1 - now[1], now[2] - 1) if s == 7 and not first(now[2]) else None)

            weave(a, GROUPS, 2, group)
            squares(1, GROUPS - 1)

        @block.tensor
        def _(pe):
            pe.wait_ge(weights, 144)
            at.pe_start(pe)
            weave(pe, GROUPS, 2, lambda now, nxt: at.pe(pe, now, nxt))
            at.pe_end(pe)


def s4d(nc, c, name, w):
    W = 383
    kz = nc.dram_tensor(f"{name}_kernel", (D, W), F32, kind="Internal").ap()
    s4d_kernel(nc, c, name + "k", w, kz)
    with ExitStack() as ctx:
        u_all = ctx.enter_context(nc.sbuf_tensor(name + "_u", [P, D, TILES], F32))
        y_all = ctx.enter_context(nc.sbuf_tensor(name + "_y", [P, TILES, D], F32))
        s4d_input(nc, c, name + "i", w, u_all)
        s4d_conv(nc, c, name + "t", kz, W, u_all, y_all)
        s4d_output(nc, c, name + "o", w, y_all)


def s4d_kernel(nc, c, name, w, kz):
    with Phase(nc, name) as ph:
        N, M = 32, 32
        PI = 3.141592653589793
        C1 = 6.28125
        C2 = 4058 * 2.0 ** -21
        C3 = 2 * PI - C1 - C2
        MAGIC = 1.5 * 2.0 ** 23
        ldt, cc_, lar, ai, dsk = (ph.sb(n, s) for n, s in (
            ("ldt", [P, 1]), ("cc", [P, 2, N]), ("lar", [P, N]), ("ai", [P, N]), ("dsk", [P, 1])))
        mi, mf = ph.sb("mi", [P, M], I32), ph.sb("mf", [P, M])
        dt, ar = ph.sb("dt", [P, 1]), ph.sb("ar", [P, N])
        dr, di = ph.sb("dr", [P, N]), ph.sb("di", [P, N])
        argr, argi, turns, mag, sn, cs = (ph.sb(n, [P, N, M]) for n in ("argr", "argi", "turns", "mag", "sn", "cs"))
        nr, ni, tr, ti, den, t0, cr, ci = (ph.sb(n, [P, N]) for n in ("nr", "ni", "tr", "ti", "den", "t0", "cr", "ci"))
        pr, pi, pt = (ph.sb(n, [P, N, 16]) for n in ("pr", "pi", "pt"))
        big, big2 = ph.sb("big", [P, N, 256]), ph.sb("big2", [P, N, 256])
        kk = ph.sb("kk", [P, W_KZ])
        loaded, placed, step, to_act, from_act, stored = (
            ph.sem(s) for s in ("loaded", "placed", "step", "to_act", "from_act", "stored"))
        block = ph.block()

        @block.sync
        def _(sp):
            for dst, src in ((ldt, "log_dt"), (cc_, "C"), (lar, "log_A_real"), (ai, "A_imag"), (dsk, "D_skip")):
                sp.dma_start(dst[:], w["L1_attn_" + src]).then_inc(loaded, 16)
            sp.wait_ge(to_act, 4)
            sp.dma_start(kz, kk[:, :]).then_inc(stored, 16)
            sp.wait_ge(stored, 16)

        @block.gpsimd
        def _(g):
            nc.gpsimd.iota(mi[:, 0:16], pattern=[[1, 16]], base=0, channel_multiplier=0).then_inc(placed, 1)
            nc.gpsimd.iota(mi[:, 16:32], pattern=[[16, 16]], base=0, channel_multiplier=0).then_inc(placed, 1)

        @block.scalar
        def _(a):
            a.wait_ge(loaded, 80)
            nc.scalar.activation(dt[:, :], ldt[:, :], ACT.Exp).then_inc(from_act, 1)
            nc.scalar.activation(ar[:, :], lar[:, :], ACT.Exp).then_inc(from_act, 1)
            a.wait_ge(to_act, 1)
            nc.scalar.activation(mag[:, :, :], argr[:, :, :], ACT.Exp).then_inc(from_act, 1)
            a.wait_ge(to_act, 2)
            nc.scalar.activation(sn[:, :, :], argi[:, :, :], ACT.Sin).then_inc(from_act, 1)
            a.wait_ge(to_act, 3)
            nc.scalar.activation(cs[:, :, :], turns[:, :, :], ACT.Sin).then_inc(from_act, 1)

        @block.vector
        def _(v):
            done = [0]

            def link(ins):
                done[0] += 1
                ins.then_inc(step, 1)
                v.wait_ge(step, done[0])

            V = nc.vector

            def tt(o, a, b, op):
                link(V.tensor_tensor(o, a, b, op))

            v.wait_ge(placed, 2)
            link(V.tensor_copy(mf[:, :], mi[:, :]))
            link(V.memset(kk[:, 0:127], 0.0))
            v.wait_ge(from_act, 2)
            link(V.tensor_scalar(ar[:, :], ar[:, :], -1.0, None, ALU.mult))
            link(V.tensor_scalar(dr[:, :], ar[:, :], dt[:, 0:1], None, ALU.mult))
            link(V.tensor_scalar(di[:, :], ai[:, :], dt[:, 0:1], None, ALU.mult))
            mb = mf[:, :].unsqueeze(1).to_broadcast([P, N, M])
            V.tensor_tensor(argr[:, :, :], dr[:, :].unsqueeze(2).to_broadcast([P, N, M]), mb, ALU.mult).then_inc(to_act, 1)
            tt(argi[:, :, :], di[:, :].unsqueeze(2).to_broadcast([P, N, M]), mb, ALU.mult)
            link(V.tensor_scalar(turns[:, :, :], argi[:, :, :], 1.0 / (2 * PI), MAGIC, ALU.mult, ALU.add))
            link(V.tensor_scalar(turns[:, :, :], turns[:, :, :], -MAGIC, None, ALU.add))
            for part in (C1, C2, C3):
                link(V.scalar_tensor_tensor(out=argi[:, :, :], in0=turns[:, :, :], scalar=-part, in1=argi[:, :, :],
                                            op0=ALU.mult, op1=ALU.add))
            V.tensor_scalar(argi[:, :, :], argi[:, :, :], 3.1415925, -3.1415925, ALU.min, ALU.max).then_inc(to_act, 1)
            v.wait_ge(to_act, 2)
            link(V.scalar_tensor_tensor(out=turns[:, :, :], in0=argi[:, :, :], scalar=-1.0, in1=argi[:, :, :],
                                        op0=ALU.mult, op1=ALU.min))
            V.tensor_scalar(turns[:, :, :], turns[:, :, :], PI / 2, None, ALU.add).then_inc(to_act, 1)
            v.wait_ge(from_act, 5)
            tt(sn[:, :, :], sn[:, :, :], mag[:, :, :], ALU.mult)
            tt(cs[:, :, :], cs[:, :, :], mag[:, :, :], ALU.mult)
            link(V.tensor_scalar(nr[:, :], cs[:, :, 1], -1.0, None, ALU.add))
            link(V.tensor_copy(ni[:, :], sn[:, :, 1]))
            c_r, c_i = cc_[:, 0, :], cc_[:, 1, :]
            tt(tr[:, :], c_r, nr[:, :], ALU.mult)
            tt(t0[:, :], c_i, ni[:, :], ALU.mult)
            tt(tr[:, :], tr[:, :], t0[:, :], ALU.subtract)
            tt(ti[:, :], c_r, ni[:, :], ALU.mult)
            tt(t0[:, :], c_i, nr[:, :], ALU.mult)
            tt(ti[:, :], ti[:, :], t0[:, :], ALU.add)
            tt(den[:, :], ar[:, :], ar[:, :], ALU.mult)
            tt(t0[:, :], ai[:, :], ai[:, :], ALU.mult)
            tt(den[:, :], den[:, :], t0[:, :], ALU.add)
            link(V.reciprocal(den[:, :], den[:, :]))
            tt(cr[:, :], tr[:, :], ar[:, :], ALU.mult)
            tt(t0[:, :], ti[:, :], ai[:, :], ALU.mult)
            tt(cr[:, :], cr[:, :], t0[:, :], ALU.add)
            tt(ci[:, :], ti[:, :], ar[:, :], ALU.mult)
            tt(t0[:, :], tr[:, :], ai[:, :], ALU.mult)
            tt(ci[:, :], ci[:, :], t0[:, :], ALU.subtract)
            tt(cr[:, :], cr[:, :], den[:, :], ALU.mult)
            tt(ci[:, :], ci[:, :], den[:, :], ALU.mult)
            def b16(a):
                return a.unsqueeze(2).to_broadcast([P, N, 16])

            er, ei = cs[:, :, 16:32], sn[:, :, 16:32]
            tt(pr[:, :, :], er, b16(cr[:, :]), ALU.mult)
            tt(pt[:, :, :], ei, b16(ci[:, :]), ALU.mult)
            tt(pr[:, :, :], pr[:, :, :], pt[:, :, :], ALU.subtract)
            tt(pi[:, :, :], er, b16(ci[:, :]), ALU.mult)
            tt(pt[:, :, :], ei, b16(cr[:, :]), ALU.mult)
            tt(pi[:, :, :], pi[:, :, :], pt[:, :, :], ALU.add)

            def outer(o, p_, q_):
                tt(o[:, :, :].rearrange("p n (a b) -> p n a b", a=16),
                   p_[:, :, :].unsqueeze(3).to_broadcast([P, N, 16, 16]),
                   q_[:, :, 0:16].unsqueeze(2).to_broadcast([P, N, 16, 16]), ALU.mult)

            outer(big, pr, cs)
            outer(big2, pi, sn)
            tt(big[:, :, :], big[:, :, :], big2[:, :, :], ALU.subtract)
            link(V.tensor_reduce(kk[:, 127:W_KZ], big[:, :, :].rearrange("p n l -> p l n"), AX_X, ALU.add))
            link(V.tensor_scalar(kk[:, 127:W_KZ], kk[:, 127:W_KZ], 2.0, None, ALU.mult))
            V.tensor_tensor(kk[:, 127:128], kk[:, 127:128], dsk[:, :], ALU.add).then_inc(to_act, 1)


W_KZ = 383


def s4d_input(nc, c, name, w, u_all):
    with Phase(nc, name) as ph:
        win, bin_ = ph.sb("win", [P, D]), ph.sb("bin", [1, D])
        fr = Front(ph, c, c.x, perm=c.mirror)
        ub = ph.bank("u")
        weights, u_done, u_ready, x_ready = (ph.sem(s) for s in ("weights", "u_done", "u_ready", "x_ready"))
        block = ph.block()

        @block.sync
        def _(sp):
            sp.dma_start(win[:, :], w["L1_attn_in_W"]).then_inc(weights, 16)
            sp.dma_start(bin_[:, :], w["L1_attn_in_b"]).then_inc(weights, 16)
            sp.wait_ge(weights, 32)

        @block.gpsimd
        def _(g):
            ahead(g, GROUPS, 2, lambda i, u, k: fr.pool(g, k), lambda i, u, k: None)

        @block.vector
        def _(v):
            def body(i, u, k):
                v.wait_ge(fr.rows_ready, TPG * (k + 1))
                xt = tiles4(c.x, k)
                nc.vector.tensor_tensor(xt, xt, fr.xn[u][:, :, :], ALU.add).then_inc(x_ready, 1)
                v.wait_ge(x_ready, k + 1)

            ahead(v, GROUPS, 2, lambda i, u, k: fr.dve(v, k, u), body)

        @block.scalar
        def _(a):
            def body(i, u, k):
                hold(a, c.mark_a, u_done, k + 1)
                nc.scalar.activation(u_all[:, :, bass.ds(TPG * k, TPG)],
                                     ub[:, :].rearrange("p (t d) -> p d t", t=TPG), ACT.Copy).then_inc(u_ready, 1)

            ahead(a, GROUPS, 2, lambda i, u, k: fr.act(a, k, u), body)

        @block.tensor
        def _(pe):
            pe.wait_ge(weights, 32)

            def body(i, u, k):
                pe.wait_ge(fr.xnT_ready, k + 1)
                if not first(k):
                    pe.wait_ge(u_ready, k)
                for t in range(TPG):
                    o = ub[:, t * D:(t + 1) * D]
                    nc.tensor.matmul(o, c.ones[0:1, :], bin_[:, :], start=True, stop=False)
                    m = nc.tensor.matmul(o, fr.xnT[u][:, t * P:(t + 1) * P], win[:, :], start=False, stop=True)
                m.then_inc(u_done, 1)

            ahead(pe, GROUPS, 2, lambda i, u, k: fr.pe(pe, k, u), body)


def s4d_conv(nc, c, name, kz, W, u_all, y_all):
    with Phase(nc, name) as ph:
        CH = 8
        top = [ph.sb(f"top{i}", [P, CH, SEQ]) for i in range(2)]
        yb = [ph.bank(f"y{i}") for i in range(2)]
        loaded = [ph.sem(f"loaded{i}") for i in range(2)]
        y_done, y_ready = ph.sem("y_done"), ph.sem("y_ready")
        block = ph.block()
        STEPS = D // CH

        @block.sync
        def _(sp):
            def load(i, u):
                s = 2 * i + u
                if not isinstance(s, int) or s >= 2:
                    sp.wait_ge(y_done, s - 1)
                src = kz[bass.ds(CH * s, CH), 0:1]
                src = bass.AP(tensor=src.tensor, offset=src.offset, ap=[[1, P], [W, CH], [1, SEQ]])
                sp.dma_start(top[u][:, :, :], src).then_inc(loaded[u], 16)

            each(sp, STEPS, 2, lambda i, u, s: load(i, u))

        @block.tensor
        def _(pe):
            def body(i, u, s):
                pe.wait_ge(loaded[u], 16 * (i + 1))
                if not first(s) and not (isinstance(s, int) and s < 2):
                    pe.wait_ge(y_ready, s - 1)
                for j in range(CH):
                    o = yb[u][:, TILES * j:TILES * (j + 1)]
                    ch = u_all[:, bass.ds(CH * s + j, 1), :].rearrange("p a t -> p (a t)")
                    nc.tensor.matmul(o, top[u][:, j, 0:P], ch, start=True, stop=False)
                    half = u_all[:, bass.ds(CH * s + j, 1), 0:TILES:2].rearrange("p a t -> p (a t)")
                    m = nc.tensor.matmul(yb[u][:, TILES * j + 1:TILES * (j + 1):2], top[u][:, j, P:SEQ], half,
                                         start=False, stop=True)
                m.then_inc(y_done, 1)

            each(pe, STEPS, 2, body)

        @block.scalar
        def _(a):
            def body(i, u, s):
                hold(a, c.mark_a, y_done, s + 1)
                nc.scalar.activation(y_all[:, :, bass.ds(CH * s, CH)],
                                     yb[u][:, 0:CH * TILES].rearrange("p (c t) -> p t c", c=CH),
                                     ACT.Gelu).then_inc(y_ready, 1)

            each(a, STEPS, 2, body)


def s4d_output(nc, c, name, w, y_all):
    with Phase(nc, name) as ph:
        wg, wo = ph.sb("wg", [P, 2 * D]), ph.sb("wo", [P, D])
        bg, bo = ph.sb("bg", [P, 2]), ph.sb("bo", [1, D])
        sg, vT = ph.sb("sg", [P, GT]), ph.sb("vT", [P, GT])
        fr = Front(ph, c, y_all, norm=False)
        zb, ob = [ph.bank(f"z{i}") for i in range(2)], ph.bank("o")
        weights, z_done, sg_ready, v_ready, o_done, o_free = (
            ph.sem(s) for s in ("weights", "z_done", "sg_ready", "v_ready", "o_done", "o_free"))
        block = ph.block()

        @block.sync
        def _(sp):
            for dst, src in ((wg, "glu_W"), (wo, "out_W"), (bg, "glu_b"), (bo, "out_b")):
                sp.dma_start(dst[:], w["L1_attn_" + src]).then_inc(weights, 16)
            sp.wait_ge(weights, 64)

        @block.vector
        def _(v):
            v.sem_inc(o_free, 1)
            v.wait_ge(weights, 64)

            def body(i, u, k):
                v.wait_ge(sg_ready, k + 1)
                nc.vector.scalar_tensor_tensor(out=vT[:, :], in0=zb[0][:, :], scalar=bg[:, 0:1], in1=sg[:, :],
                                               op0=ALU.add, op1=ALU.mult).then_inc(v_ready, 1)
                v.wait_ge(o_done, k + 1)
                xt = tiles4(c.x, k)
                nc.vector.tensor_tensor(xt, xt, ob[:, :].rearrange("p (t d) -> p t d", t=TPG), ALU.add
                                        ).then_inc(o_free, 1)

            ahead(v, GROUPS, 2, lambda i, u, k: fr.dve(v, k, u), body)

        @block.scalar
        def _(a):
            def body(i, u, k):
                a.wait_ge(z_done, k + 1)
                nc.scalar.activation(sg[:, :], zb[1][:, :], ACT.Sigmoid, bias=bg[:, 1:2]).then_inc(sg_ready, 1)

            ahead(a, GROUPS, 2, lambda i, u, k: fr.act(a, k, u), body)

        @block.tensor
        def _(pe):
            pe.wait_ge(weights, 64)

            def body(i, u, k):
                pe.wait_ge(fr.xnT_ready, k + 1)
                for j in range(2):
                    m = nc.tensor.matmul(zb[j][:, :], wg[:, j * D:(j + 1) * D], fr.xnT[u][:, :], start=True, stop=True)
                m.then_inc(z_done, 1)
                pe.wait_ge(v_ready, k + 1)
                pe.wait_ge(o_free, k + 1)
                for t in range(TPG):
                    o = ob[:, t * D:(t + 1) * D]
                    nc.tensor.matmul(o, c.ones[0:1, :], bo[:, :], start=True, stop=False)
                    m = nc.tensor.matmul(o, vT[:, t * P:(t + 1) * P], wo[:, :], start=False, stop=True)
                m.then_inc(o_done, 1)

            ahead(pe, GROUPS, 2, lambda i, u, k: fr.pe(pe, k, u), body)


def mamba(nc, c, name, w):
    with ExitStack() as ctx:
        y_all = ctx.enter_context(nc.sbuf_tensor(name + "_y", [P, TILES, D], F32))
        mamba_rows(nc, c, name + "n", y_all)
        mamba_mix(nc, c, name + "m", w, y_all)


def mamba_rows(nc, c, name, y_all):
    with Phase(nc, name) as ph:
        st, mv = ph.sb("st", [P, TILES, 6]), ph.sb("mv", [P, TILES, 2])
        rs = Rsqrt(ph, c, "ln", TILES)
        stats, moments, rows, added = ph.sem("stats"), ph.sem("moments"), ph.sem("rows"), ph.sem("added")
        block = ph.block()

        @block.gpsimd
        def _(g):
            rs.pool(g, 0)

        @block.vector
        def _(v):
            with v.Fori(0, TILES) as t:
                nc.vector.bn_stats(st[:, bass.ds(t, 1), :], c.x[:, bass.ds(t, 1), :]).then_inc(stats, 1)
            v.wait_ge(stats, TILES)
            for t in range(TILES):
                nc.vector.bn_aggr(mv[:, t, :], st[:, t, :]).then_inc(moments, 1)
            v.wait_ge(moments, TILES)
            rs.dve(v, mv[:, :, 1], 0, 1.0, LN_EPS)
            v.wait_ge(rs.solved, 1)
            for t in range(TILES):
                nc.vector.tensor_scalar(y_all[:, t, :], c.x[:, t, :], mv[:, t, 0:1], rs.y[:, t:t + 1], ALU.subtract,
                                        ALU.mult).then_inc(rows, 1)
            v.wait_ge(rows, TILES)
            nc.vector.tensor_tensor(c.x[:, :, :], c.x[:, :, :], y_all[:, :, :], ALU.add).then_inc(added, 1)
            v.wait_ge(added, 1)


def mamba_mix(nc, c, name, w, y_all):
    with Phase(nc, name) as ph:
        CC, N, RK = 2, 16, 8
        RB = RK + 2 * N
        SPG = GT // SEQ
        EDGE = 1e30
        win, xpw, dtw, wo = ph.sb("win", [P, 512]), ph.sb("xpw", [P, CC, RB]), ph.sb("dtw", [RK, 256]), ph.sb(
            "wo", [P, CC, D])
        lnw, lnb, cw, cb = ph.sb("lnw", [P, 1]), ph.sb("lnb", [P, 1]), ph.sb("cw", [P, CC, 4]), ph.sb("cb", [P, CC])
        dtb, al, dd = ph.sb("dtb", [P, CC]), ph.sb("al", [P, CC, N]), ph.sb("dd", [P, CC])
        sel = ph.sb("sel", [RB, 2 * N, P])
        xpad = [ph.sb(f"xpad{i}", [P, SPG, SEQ + 3]) for i in range(CC)]
        cv, zs, xs, dl, du, yT = ([ph.sb(f"{n}{i}", [P, GT]) for i in range(CC)] for n in
                                  ("cv", "zs", "xs", "dl", "du", "yT"))
        va, ve = ([ph.sb(f"{n}{i}", [P, GT]) for i in range(CC)] for n in ("va", "ve"))
        dbc = ph.sb("dbc", [RB, GT])
        dA, db, hh, hc = ([ph.sb(f"{n}{i}", [P, GT]) for i in range(2)] for n in ("dA", "db", "hh", "hc"))
        fr = Front(ph, c, y_all, scale=lnw[:, 0:1], bias=lnb[:, 0:1])
        mb = ph.bank("misc")
        bb, cbk = [ph.bank(f"b{i}") for i in range(2)], [ph.bank(f"c{i}") for i in range(2)]
        yb = [ph.bank(f"y{i}") for i in range(CC)]
        (weights, made, ready, xz_done, xz_read, padded, conv, xs_ready, dbc_done, dbc_ready, dl_done, va_ready,
         soft, dl_ready, du_ready, edge, b_done, dA_ready, db_ready, h_ready, hc_ready, y_done, yy, y_ready, o_done,
         o_free) = (ph.sem(s) for s in (
             "weights", "made", "ready", "xz_done", "xz_read", "padded", "conv", "xs_ready", "dbc_done", "dbc_ready",
             "dl_done", "va_ready", "soft", "dl_ready", "du_ready", "edge", "b_done", "dA_ready", "db_ready",
             "h_ready", "hc_ready", "y_done", "yy", "y_ready", "o_done", "o_free"))
        summed = ph.sem("summed")
        block = ph.block()

        @block.sync
        def _(sp):
            for dst, src in ((win, "in_proj_w"), (xpw, "x_proj_w"), (dtw, "dt_proj_w"), (wo, "out_proj_w"),
                             (lnw, "ln_w"), (lnb, "ln_b"), (cw, "conv_w"), (cb, "conv_b"), (dtb, "dt_proj_b"),
                             (al, "A_log"), (dd, "D")):
                sp.dma_start(dst[:], w["L3_attn_" + src]).then_inc(weights, 16)
            sp.wait_ge(weights, 176)

        @block.gpsimd
        def _(g):
            nc.gpsimd.memset(sel[:, :, :], 0.0).then_inc(made, 1)
            for i in range(CC):
                nc.gpsimd.memset(xpad[i][:, :, 0:3], 0.0).then_inc(made, 1)
            g.wait_ge(made, 3)
            nc.gpsimd.affine_select(out=sel[:, :, :], in_=sel[:, :, :], compare_op=ALU.not_equal, fill=1.0, base=-RK,
                                    pattern=[[-1, 2 * N], [0, P]], channel_multiplier=1).then_inc(made, 1)
            ahead(g, GROUPS, 2, lambda i, u, k: fr.pool(g, k), lambda i, u, k: None)

        @block.scalar
        def _(a):
            a.wait_ge(weights, 176)
            nc.scalar.activation(al[:, :, :], al[:, :, :], ACT.Exp).then_inc(ready, 1)

            def body(i, u, k):
                for j in range(4):
                    a.wait_ge(xz_done, 4 * k + j + 1)
                    if j < CC:
                        m = nc.scalar.activation(xpad[j][:, :, 3:], mb[:, :].rearrange("p (s l) -> p s l", s=SPG),
                                                 ACT.Copy)
                    else:
                        m = nc.scalar.activation(zs[j - CC][:, :], mb[:, :], ACT.Silu)
                    m.then_inc(xz_read, 1)
                for j in range(CC):
                    a.wait_ge(conv, 8 * k + 4 * j + 4)
                    nc.scalar.activation(xs[j][:, :], cv[j][:, :], ACT.Silu, bias=cb[:, j:j + 1]).then_inc(xs_ready, 1)
                a.wait_ge(dbc_done, k + 1)
                nc.scalar.activation(dbc[:, :], mb[0:RB, :], ACT.Copy).then_inc(dbc_ready, 1)
                for j in range(CC):
                    n = CC * k + j
                    a.wait_ge(va_ready, 2 * n + 2)
                    nc.scalar.activation(ve[j][:, :], ve[j][:, :], ACT.Exp, scale=-1.0).then_inc(soft, 1)
                    a.wait_ge(soft, 2 * n + 1)
                    nc.scalar.activation(ve[j][:, :], ve[j][:, :], ACT.Ln, bias=1.0).then_inc(soft, 1)
                a.wait_ge(edge, CC * (k + 1))
                for s in range(N):
                    for j in range(CC):
                        n = CC * (N * k + s) + j
                        if s or not first(k):
                            a.wait_ge(h_ready, n - 1)
                        nc.scalar.activation(dA[j][:, :], dl[j][:, :], ACT.Exp, scale=al[:, j, s:s + 1]
                                             ).then_inc(dA_ready, 1)

            ahead(a, GROUPS, 2, lambda i, u, k: fr.act(a, k, u), body)

        @block.vector
        def _(v):
            V = nc.vector
            v.wait_ge(ready, 1)
            V.tensor_scalar(al[:, :, :], al[:, :, :], -1.0, None, ALU.mult).then_inc(ready, 1)
            v.wait_ge(made, 4)
            v.wait_ge(ready, 2)
            v.sem_inc(o_free, 1)

            def body(i, u, k):
                for j in range(CC):
                    v.wait_ge(xz_read, 4 * k + j + 1)
                    c3 = cv[j][:, :].rearrange("p (s l) -> p s l", s=SPG)
                    for q in range(4):
                        tap = xpad[j][:, :, q:q + SEQ]
                        if q == 0:
                            V.tensor_scalar(c3, tap, cw[:, j, 0:1], None, ALU.mult).then_inc(conv, 1)
                        else:
                            v.wait_ge(conv, 8 * k + 4 * j + q)
                            V.scalar_tensor_tensor(out=c3, in0=tap, scalar=cw[:, j, q:q + 1], in1=c3, op0=ALU.mult,
                                                   op1=ALU.add).then_inc(conv, 1)
                for j in range(CC):
                    n = CC * k + j
                    v.wait_ge(dl_done, n + 1)
                    V.tensor_scalar(va[j][:, :], mb[:, :], dtb[:, j:j + 1], None, ALU.add).then_inc(va_ready, 1)
                    v.wait_ge(va_ready, 2 * n + 1)
                    V.scalar_tensor_tensor(out=ve[j][:, :], in0=va[j][:, :], scalar=-1.0, in1=va[j][:, :],
                                           op0=ALU.mult, op1=ALU.max).then_inc(va_ready, 1)
                    v.wait_ge(soft, 2 * n + 2)
                    V.scalar_tensor_tensor(out=dl[j][:, :], in0=va[j][:, :], scalar=0.0, in1=ve[j][:, :],
                                           op0=ALU.max, op1=ALU.add).then_inc(dl_ready, 1)
                    v.wait_ge(dl_ready, n + 1)
                    V.tensor_tensor(du[j][:, :], dl[j][:, :], xs[j][:, :], ALU.mult).then_inc(du_ready, 1)
                    v.wait_ge(du_ready, n + 1)
                    V.memset(dl[j][:, SEQ:SEQ + 1], EDGE).then_inc(edge, 1)
                for s in range(N):
                    for j in range(CC):
                        n = CC * (N * k + s) + j
                        v.wait_ge(b_done, N * k + s + 1)
                        V.tensor_tensor(db[j][:, :], du[j][:, :], bb[s % 2][:, :], ALU.mult).then_inc(db_ready, 1)
                    for j in range(CC):
                        n = CC * (N * k + s) + j
                        v.wait_ge(db_ready, n + 1)
                        v.wait_ge(dA_ready, n + 1)
                        V.tensor_tensor_scan(hh[j][:, :], dA[j][:, :], db[j][:, :], 0.0, ALU.mult, ALU.add
                                             ).then_inc(h_ready, 1)
                    for j in range(CC):
                        n = CC * (N * k + s) + j
                        v.wait_ge(h_ready, n + 1)
                        if s or not first(k):
                            v.wait_ge(summed, n - 1)
                        V.tensor_tensor(hc[j][:, :], hh[j][:, :], cbk[s % 2][:, :], ALU.mult).then_inc(hc_ready, 1)
                for j in range(CC):
                    n = CC * k + j
                    v.wait_ge(summed, N * CC * (k + 1))
                    V.scalar_tensor_tensor(out=yT[j][:, :], in0=xs[j][:, :], scalar=dd[:, j:j + 1], in1=yb[j][:, :],
                                           op0=ALU.mult, op1=ALU.add).then_inc(yy, 1)
                    v.wait_ge(yy, n + 1)
                    V.tensor_tensor(yT[j][:, :], yT[j][:, :], zs[j][:, :], ALU.mult).then_inc(y_ready, 1)
                v.wait_ge(o_done, k + 1)
                xt = tiles4(c.x, k)
                V.tensor_tensor(xt, xt, mb[:, :].rearrange("p (t d) -> p t d", t=TPG), ALU.add).then_inc(o_free, 1)

            ahead(v, GROUPS, 2, lambda i, u, k: fr.dve(v, k, u), body)

        @block.tensor
        def _(pe):
            pe.wait_ge(weights, 176)
            pe.wait_ge(made, 4)

            def body(i, u, k):
                pe.wait_ge(fr.xnT_ready, k + 1)
                pe.wait_ge(o_free, k + 1)
                for j in range(4):
                    if j or not first(k):
                        pe.wait_ge(xz_read, 4 * k + j)
                    nc.tensor.matmul(mb[:, :], win[:, j * P:(j + 1) * P], fr.xnT[u][:, :], start=True, stop=True
                                     ).then_inc(xz_done, 1)
                pe.wait_ge(xs_ready, CC * (k + 1))
                pe.wait_ge(xz_read, 4 * k + 4)
                for j in range(CC):
                    m = nc.tensor.matmul(mb[0:RB, :], xpw[:, j, :], xs[j][:, :], start=(j == 0), stop=(j == CC - 1))
                m.then_inc(dbc_done, 1)
                pe.wait_ge(dbc_ready, k + 1)
                for j in range(CC):
                    n = CC * k + j
                    if j:
                        pe.wait_ge(va_ready, 2 * n - 1)
                    nc.tensor.matmul(mb[:, :], dtw[:, j * P:(j + 1) * P], dbc[0:RK, :], start=True, stop=True
                                     ).then_inc(dl_done, 1)

                def spread(s):
                    n = N * k + s
                    if s >= 2 or not first(k):
                        pe.wait_ge(hc_ready, CC * n - CC)
                    nc.tensor.matmul(bb[s % 2][:, :], sel[:, s, :], dbc[:, :], start=True, stop=True)
                    nc.tensor.matmul(cbk[s % 2][:, :], sel[:, N + s, :], dbc[:, :], start=True, stop=True
                                     ).then_inc(b_done, 1)

                spread(0)
                for s in range(N):
                    if s + 1 < N:
                        spread(s + 1)
                    for j in range(CC):
                        pe.wait_ge(hc_ready, CC * (N * k + s) + j + 1)
                        nc.tensor.matmul(yb[j][:, :], c.ident[:, :], hc[j][:, :], start=(s == 0), stop=(s == N - 1)
                                         ).then_inc(summed, 1)
                pe.wait_ge(y_ready, CC * (k + 1))
                for t in range(TPG):
                    for j in range(CC):
                        m = nc.tensor.matmul(mb[:, t * D:(t + 1) * D], yT[j][:, t * P:(t + 1) * P], wo[:, j, :],
                                             start=(j == 0), stop=(j == CC - 1))
                m.then_inc(o_done, 1)

            ahead(pe, GROUPS, 2, lambda i, u, k: fr.pe(pe, k, u), body)


def store(nc, c, out):
    with Phase(nc, "store") as ph:
        stored = ph.sem("stored")
        block = ph.block()

        @block.sync
        def _(sp):
            sp.dma_start(out.rearrange("(t p) d -> p t d", p=P), c.x[:, :, :]).then_inc(stored, 16)
            sp.wait_ge(stored, 16)


def stages(nc, c, w):
    return [
        lambda: moe64(nc, c, "l0f1", w),
        lambda: block_attention(nc, c, "l0a", w),
        lambda: moe64(nc, c, "l0f2", w),
        lambda: lowrank_ffn(nc, c, "l1f1", w),
        lambda: s4d(nc, c, "l1a", w),
        lambda: lowrank_ffn(nc, c, "l1f2", w),
        lambda: ternary_ffn(nc, c, "l2f1", w),
        lambda: window_attention(nc, c, "l2a", w),
        lambda: ternary_ffn(nc, c, "l2f2", w),
        lambda: gqa_moe(nc, c, "l3f1", w),
        lambda: mamba(nc, c, "l3a", w),
        lambda: gqa_moe(nc, c, "l3f2", w),
    ]


def program(nc, w, out, which=range(12)):
    with ExitStack() as ctx:
        c = Consts()

        def sb(name, shape, dt=F32):
            return ctx.enter_context(nc.sbuf_tensor(name, shape, dt))

        c.x = sb("x_state", [P, TILES, D])
        c.ident, c.mirror, c.ones, c.zero, c.below = (
            sb(n, [P, P]) for n in ("ident", "mirror", "ones", "zero", "below"))
        c.mark_v, c.mark_g, c.mark_a, c.mark_p = (
            ctx.enter_context(nc.semaphore(f"mark_{n}")) for n in ("vector", "gpsimd", "scalar", "tensor"))
        c.ident_b = sb("ident_b", [P, P], BF16)
        c.below_b, c.ones_b = sb("below_b", [P, P], BF16), sb("ones_b", [P, P], BF16)
        c.token_id, c.expert_id = sb("token_id", [P, TILES]), sb("expert_id", [P, 64])
        c.blank = sb("blank", [P, D + 64 + 1])
        c.mixtures, c.to_clear = {}, []
        for s, name, E in ((0, "l0f1", 64), (2, "l0f2", 64), (9, "l3f1", 8), (11, "l3f2", 8)):
            if s in which:
                c.mixtures[name] = Mixture(nc, ctx, name, E)
                c.to_clear.append(c.mixtures[name])
        setup(nc, c, w)
        todo = stages(nc, c, w)
        for s in which:
            todo[s]()
        store(nc, c, out)


def layouts(a):
    import numpy as np

    def t(m):
        return m.T

    def cols(v):
        return v.reshape(-1, P).T

    def row(v):
        return v.reshape(1, -1)

    def chunks(m):
        return m.reshape(-1, P, m.shape[-1]).transpose(1, 0, 2)

    def same(m):
        return m

    def four(m):
        m = m.reshape(m.shape[:-1] + (4, 1, 8))
        return np.broadcast_to(m, m.shape[:-2] + (4, 8)).reshape(m.shape[:-3] + (P,))

    plan = {
        "L0_attn_Wq": same, "L0_attn_Wk": same, "L0_attn_Wv": same, "L0_attn_Wo": same,
        "L0_attn_bq": cols, "L0_attn_bk": cols, "L0_attn_bv": row, "L0_attn_bo": row,
        "L0_ffn_wg": t, "L0_ffn_shared_w1": t, "L0_ffn_shared_w2": lambda m: chunks(m.T),
        "L0_ffn_expert_w1": lambda m: m.transpose(0, 2, 1),
        "L0_ffn_expert_w2": lambda m: m.transpose(0, 2, 1).reshape(64, 3, P, D).transpose(0, 2, 1, 3),
        "L1_attn_in_W": t, "L1_attn_in_b": row, "L1_attn_log_dt": cols, "L1_attn_C": lambda m: m.transpose(0, 2, 1),
        "L1_attn_log_A_real": same, "L1_attn_A_imag": same, "L1_attn_D_skip": cols,
        "L1_attn_glu_W": t, "L1_attn_glu_b": cols, "L1_attn_out_W": t, "L1_attn_out_b": row,
        "L1_ffn_U1": same, "L1_ffn_V1": same, "L1_ffn_b1": cols, "L1_ffn_U2": chunks, "L1_ffn_V2": same,
        "L1_ffn_b2": row,
        "L2_attn_Wq": t, "L2_attn_Wk": t, "L2_attn_Wv": t, "L2_attn_Wo": t, "L2_attn_global_token_indices": row,
        "L2_ffn_W1": t, "L2_ffn_b1": cols, "L2_ffn_W2": lambda m: chunks(m.T), "L2_ffn_b2": row,
        "L3_attn_ln_w": cols, "L3_attn_ln_b": cols, "L3_attn_in_proj_w": t,
        "L3_attn_conv_w": lambda m: m.reshape(2, P, 4).transpose(1, 0, 2), "L3_attn_conv_b": cols,
        "L3_attn_x_proj_w": lambda m: chunks(m.T), "L3_attn_dt_proj_w": t, "L3_attn_dt_proj_b": cols,
        "L3_attn_A_log": chunks, "L3_attn_D": cols, "L3_attn_out_proj_w": lambda m: chunks(m.T),
        "L3_ffn_qw": same, "L3_ffn_qb": cols, "L3_ffn_kw": four, "L3_ffn_kb": lambda v: cols(four(v)), "L3_ffn_vw": four,
        "L3_ffn_vb": lambda v: row(four(v)), "L3_ffn_ow": same, "L3_ffn_ob": row, "L3_ffn_gate_w": same, "L3_ffn_w1": same,
        "L3_ffn_w2": lambda m: m.reshape(8, 2, P, D).transpose(0, 2, 1, 3),
        "L3_ffn_norm1_w": row, "L3_ffn_norm2_w": row,
    }
    out = {n: np.ascontiguousarray(f(np.asarray(a[n]))) for n, f in plan.items()}
    out["x"] = np.ascontiguousarray(np.asarray(a["L0_attn_src"]).reshape(TOKENS, D))
    return out


def kernel(**inputs):
    import numpy as np
    import concourse.bacc as bacc
    from concourse.bass_utils import run_bass_kernel_spmd

    nc = bacc.Bacc("TRN2", target_bir_lowering=False, num_devices=1)
    arrays, w = {}, {}
    for name, a in layouts(inputs).items():
        arrays[f"in_{name}"] = a
        w[name] = nc.dram_tensor(f"in_{name}", a.shape, mybir.dt.from_np(a.dtype), kind="ExternalInput").ap()
    out = nc.dram_tensor("out", (TOKENS, D), F32, kind="ExternalOutput").ap()
    program(nc, w, out)
    r = run_bass_kernel_spmd(nc, [arrays], core_ids=[0])
    return r.results[0]["out"].reshape(16, 256, D)
```

```python
from contextlib import ExitStack

import concourse.bass as bass
from concourse import mybir

F32 = mybir.dt.float32
BF16 = mybir.dt.bfloat16
U32 = mybir.dt.uint32
I32 = mybir.dt.int32
ALU = mybir.AluOpType
ACT = mybir.ActivationFunctionType
AX_X = mybir.AxisListType.X

P = 128
D = 128
TOKENS = 4096
SEQ = 256
TILES = TOKENS // P
TPG = 4
GROUPS = TILES // TPG
GT = TPG * P
LN_EPS = 1e-5
RMS_EPS = 1e-6
SUB = 80
DUMPS = 4
SLOTS = 10240
TABLES = 2
FAR = 65536.0


class Phase:

    def __init__(self, nc, name):
        self.nc, self.name, self.ctx, self.sems = nc, name, ExitStack(), []

    def __enter__(self):
        return self

    def __exit__(self, *e):
        self.ctx.__exit__(*e)
        self.nc.clear_and_free_semaphores(self.sems)
        self.nc.all_engine_barrier()

    def sb(self, name, shape, dt=F32):
        return self.ctx.enter_context(self.nc.sbuf_tensor(f"{self.name}_{name}", shape, dt))

    def bank(self, name, dt=F32):
        return self.ctx.enter_context(self.nc.psum_tensor(f"{self.name}_{name}", [P, 512], dt))

    def sem(self, name):
        self.sems.append(self.nc.alloc_semaphore(f"{self.name}_{name}"))
        return self.sems[-1]

    def block(self):
        return self.ctx.enter_context(self.nc.Block())


def ahead(eng, n, unroll, front, body):
    front(0, 0, 0)

    def steps(i, last):
        for u in range(unroll):
            if u + 1 < unroll:
                front(i, u + 1, unroll * i + u + 1)
            elif not last:
                front(i + 1, 0, unroll * i + unroll)
            body(i, u, unroll * i + u)

    steps(0, False)
    with eng.Fori(1, n // unroll - 1) as i:
        steps(i, False)
    steps(n // unroll - 1, True)


def stream(eng, n, unroll, step):
    def steps(i, last):
        for u in range(unroll):
            def at(d, u=u):
                if u + d < unroll:
                    return i, u + d, unroll * i + u + d
                return None if last else (i + 1, u + d - unroll, unroll * i + u + d)
            step(at)

    steps(0, False)
    with eng.Fori(1, n // unroll - 1) as i:
        steps(i, False)
    steps(n // unroll - 1, True)


def each(eng, n, unroll, body):
    for u in range(unroll):
        body(0, u, u)
    with eng.Fori(1, n // unroll) as i:
        for u in range(unroll):
            body(i, u, unroll * i + u)


def tiles4(x, g):
    return x[:, bass.ds(TPG * g, TPG), :]


def hold(eng, mark, sem, value):
    eng.wait_ge(sem, value)
    eng.sem_inc(mark, 1)


def first(k):
    return isinstance(k, int) and k == 0


class Rsqrt:

    def __init__(self, ph, c, name, n):
        self.nc, self.mark = ph.nc, c.mark_g
        self.v, self.y, self.t = (ph.sb(f"{name}_{s}", [P, n]) for s in "vyt")
        self.seeding, self.seeded, self.newton, self.solved = (
            ph.sem(f"{name}_{s}") for s in ("seeding", "seeded", "newton", "solved"))

    def dve(self, v, src, k, scale, eps):
        nc = self.nc
        nc.vector.tensor_scalar(self.v[:, :], src, scale, eps, ALU.mult, ALU.add).then_inc(self.seeding, 1)
        v.wait_ge(self.seeding, 2 * k + 1)
        nc.vector.tensor_scalar(self.t[:, :].bitcast(I32), self.v[:, :].bitcast(I32), 1, None,
                                ALU.logical_shift_right).then_inc(self.seeding, 1)
        v.wait_ge(self.seeding, 2 * k + 2)
        nc.vector.tensor_scalar(self.y[:, :].bitcast(I32), self.t[:, :].bitcast(I32), -1.0, float(0x5F3759DF),
                                ALU.mult, ALU.add).then_inc(self.seeded, 1)

    def pool(self, g, k):
        nc, v, y, t = self.nc, self.v[:, :], self.y[:, :], self.t[:, :]
        g.wait_ge(self.seeded, k + 1)
        for i in range(3):
            n = 11 * k + 4 * i
            if i:
                g.wait_ge(self.newton, n)
            nc.gpsimd.tensor_tensor(t, y, y, ALU.mult).then_inc(self.newton, 1)
            g.wait_ge(self.newton, n + 1)
            nc.gpsimd.tensor_tensor(t, t, v, ALU.mult).then_inc(self.newton, 1)
            hold(g, self.mark, self.newton, n + 2)
            nc.gpsimd.tensor_scalar(t, t, -0.5, 1.5, ALU.mult, ALU.add).then_inc(self.newton, 1)
            g.wait_ge(self.newton, n + 3)
            nc.gpsimd.tensor_tensor(y, y, t, ALU.mult).then_inc(self.newton if i < 2 else self.solved, 1)


def weave(eng, n, unroll, group):
    def steps(i, last):
        for u in range(unroll):
            k = unroll * i + u
            nxt = (i, u + 1, k + 1) if u + 1 < unroll else None if last else (i + 1, 0, k + 1)
            group((i, u, k), nxt)

    steps(0, False)
    with eng.Fori(1, n // unroll - 1) as i:
        steps(i, False)
    steps(n // unroll - 1, True)


class Front:

    def __init__(self, ph, c, x, rows=None, perm=None, norm=True, scale=None, bias=None, bank=None, at_once=False):
        nc = ph.nc
        self.n = TILES if at_once else TPG
        self.at_once = at_once
        self.nc, self.c, self.x, self.norm = nc, c, x, norm
        self.perm = perm if perm is not None else c.ident
        self.scale, self.bias = scale, bias
        self.xn = rows if rows is not None else [ph.sb(f"xn{i}", [P, TPG, D]) for i in range(2)]
        self.xnT = [ph.sb(f"xnT{i}", [P, GT]) for i in range(2)]
        self.bank = bank if bank is not None else ph.bank("front")
        if norm:
            self.st = ph.sb("st", [P, self.n, 6])
            self.mv = ph.sb("mv", [P, self.n, 2])
            self.rsqrt = Rsqrt(ph, c, "ln", self.n)
            self.rs = self.rsqrt.y
        self.stats = ph.sem("stats")
        self.moments = ph.sem("moments")
        self.rows_ready = ph.sem("rows_ready")
        self.turned = ph.sem("turned")
        self.xnT_ready = ph.sem("xnT_ready")

    def dve(self, v, k, p, free=None):
        if self.norm:
            if not self.at_once:
                self.dve_stats(v, k)
            self.dve_rows(v, k, p, free)
            return
        if not first(k):
            hold(v, self.c.mark_v, self.turned, k)
        if free:
            free()
        self.nc.vector.tensor_copy(self.xn[p][:, :, 0:D], tiles4(self.x, k)).then_inc(self.rows_ready, TPG)

    def dve_stats(self, v, k):
        nc = self.nc
        n = self.n
        for t in range(n):
            nc.vector.bn_stats(self.st[:, t:t + 1, :], self.x[:, bass.ds(n * k + t, 1), :]).then_inc(self.stats, 1)
        hold(v, self.c.mark_v, self.stats, n * (k + 1))
        for t in range(n):
            nc.vector.bn_aggr(self.mv[:, t, :], self.st[:, t, :]).then_inc(self.moments, 1)
        v.wait_ge(self.moments, n * (k + 1))
        self.rsqrt.dve(v, self.mv[:, :, 1], k, 1.0, LN_EPS)

    def dve_rows(self, v, k, p, free=None):
        nc = self.nc
        if not first(k):
            v.wait_ge(self.turned, k)
        if not self.at_once:
            v.wait_ge(self.rsqrt.solved, k + 1)
        elif first(k):
            v.wait_ge(self.rsqrt.solved, 1)
        if free:
            free()
        for t in range(TPG):
            s = bass.ds(TPG * k + t, 1) if self.at_once else slice(t, t + 1)
            nc.vector.tensor_scalar(self.xn[p][:, t:t + 1, 0:D], self.x[:, bass.ds(TPG * k + t, 1), :],
                                    self.mv[:, s, 0:1].rearrange("p t o -> p (t o)"), self.rs[:, s], ALU.subtract,
                                    ALU.mult).then_inc(self.rows_ready, 1)

    def dve_start(self, v):
        if self.norm and self.at_once:
            self.dve_stats(v, 0)

    def pool_start(self, g):
        if self.norm and self.at_once:
            self.rsqrt.pool(g, 0)

    def pool(self, g, k):
        if self.norm and not self.at_once:
            self.rsqrt.pool(g, k)

    def pe(self, pe, k, p):
        pe.wait_ge(self.rows_ready, TPG * (k + 1))
        if not first(k):
            pe.wait_ge(self.xnT_ready, k)
        for t in range(TPG):
            m = self.nc.tensor.transpose(self.bank[:, t * P:(t + 1) * P], self.xn[p][:, t, 0:D], self.perm[:, :])
        m.then_inc(self.turned, 1)

    def act(self, a, k, p):
        a.wait_ge(self.turned, k + 1)
        if self.scale is None:
            self.nc.scalar.activation(self.xnT[p][:, :], self.bank[:, :], ACT.Copy).then_inc(self.xnT_ready, 1)
        else:
            self.nc.scalar.activation(self.xnT[p][:, :], self.bank[:, :], ACT.Identity, bias=self.bias,
                                      scale=self.scale).then_inc(self.xnT_ready, 1)


class Consts:
    pass


def setup(nc, c, w):
    with Phase(nc, "setup") as ph:
        loaded, made, out = ph.sem("loaded"), ph.sem("made"), ph.sem("converted")
        ti = ph.sb("ti", [P, TILES], I32)
        ei = ph.sb("ei", [P, 64], I32)
        di = ph.sb("di", [P, DUMPS], I32)
        blank_made = ph.sem("blank_made")
        block = ph.block()

        @block.sync
        def _(sp):
            sp.dma_start(c.x[:, :, :], w["x"].rearrange("(t p) d -> p t d", p=P)).then_inc(loaded, 16)
            sp.wait_ge(loaded, 16)

        @block.scalar
        def _(a):
            a.wait_ge(blank_made, 2)
            a.wait_ge(made, 5)
            clear_next(c, a)

        @block.gpsimd
        def _(g):
            n = 0
            for t, val in ((c.ident, 0.0), (c.mirror, 0.0), (c.ones, 1.0), (c.zero, 0.0), (c.below, 1.0)):
                nc.gpsimd.memset(t[:, :], val).then_inc(made, 1)
                n += 1
            g.wait_ge(made, n)
            for t, pat, mul, base, op in ((c.ident, -1, 1, 0, ALU.not_equal), (c.mirror, 1, 1, -(P - 1), ALU.not_equal)):
                nc.gpsimd.affine_select(out=t[:, :], in_=t[:, :], compare_op=op, fill=1.0, base=base,
                                        pattern=[[pat, P]], channel_multiplier=mul).then_inc(made, 1)
                n += 1
            nc.gpsimd.affine_select(out=c.below[:, :], in_=c.below[:, :], compare_op=ALU.is_gt, fill=0.0, base=0,
                                    pattern=[[1, P]], channel_multiplier=-1).then_inc(made, 1)
            nc.gpsimd.iota(ti[:, :], pattern=[[P, TILES]], base=0, channel_multiplier=1).then_inc(made, 1)
            nc.gpsimd.iota(ei[:, :], pattern=[[1, 64]], base=0, channel_multiplier=0).then_inc(made, 1)
            nc.gpsimd.iota(di[:, :], pattern=[[SUB, DUMPS]], base=TOKENS, channel_multiplier=1).then_inc(made, 1)

        @block.vector
        def _(v):
            nc.vector.memset(c.blank[:, :, :], 0.0).then_inc(blank_made, 1)
            v.wait_ge(made, 11)
            v.wait_ge(blank_made, 1)
            nc.vector.tensor_copy(c.token_id[:, :], ti[:, :]).then_inc(out, 1)
            nc.vector.tensor_copy(c.expert_id[:, :], ei[:, :]).then_inc(out, 1)
            nc.vector.tensor_copy(c.blank[:, :, -1:], di[:, :].unsqueeze(2)).then_inc(blank_made, 1)
            nc.vector.tensor_copy(c.below_b[:, :], c.below[:, :]).then_inc(out, 1)
            nc.vector.tensor_copy(c.ones_b[:, :], c.ones[:, :]).then_inc(out, 1)


def add_output(nc, c, v, ob, o_done, o_free, k):
    v.wait_ge(o_done, k + 1)
    nc.vector.scalar_tensor_tensor(
        out=tiles4(c.x, k), in0=ob[:, :].rearrange("p (t d) -> p t d", t=TPG), scalar=0.5,
        in1=tiles4(c.x, k), op0=ALU.mult, op1=ALU.add).then_inc(o_free, 1)


def front_two_ahead(fr, g):
    fr.pool(g, 0)
    fr.pool(g, 1)
    stream(g, GROUPS, 2, lambda at: fr.pool(g, at(2)[2]) if at(2) else None)


def lowrank_ffn(nc, c, name, w):
    with Phase(nc, name) as ph:
        R, F = 32, 512
        u1, v1 = ph.sb("u1", [P, R]), ph.sb("v1", [R, F])
        u2, v2 = ph.sb("u2", [P, 4, R]), ph.sb("v2", [R, D])
        b1, b2 = ph.sb("b1", [P, 4]), ph.sb("b2", [1, D])
        pT, hT = [ph.sb(f"pT{i}", [R, GT]) for i in range(2)], [ph.sb(f"hT{i}", [P, 4, GT]) for i in range(2)]
        qT = ph.sb("qT", [R, GT])
        fr = Front(ph, c, c.x)
        pb, qb, ob = ph.bank("p"), ph.bank("q"), ph.bank("o")
        hb = [ph.bank(f"h{i}") for i in range(4)]
        weights, p_done, pT_ready, h_done, gelu_done, q_done, qT_ready, o_done, o_free = (
            ph.sem(s) for s in ("weights", "p_done", "pT_ready", "h_done", "gelu_done", "q_done", "qT_ready",
                                "o_done", "o_free"))
        block = ph.block()

        @block.sync
        def _(sp):
            for dst, src in ((u1, "L1_ffn_U1"), (v1, "L1_ffn_V1"), (u2, "L1_ffn_U2"), (v2, "L1_ffn_V2"),
                             (b1, "L1_ffn_b1"), (b2, "L1_ffn_b2")):
                sp.dma_start(dst[:], w[src]).then_inc(weights, 16)
            sp.wait_ge(weights, 96)

        @block.gpsimd
        def _(g):
            front_two_ahead(fr, g)

        @block.vector
        def _(v):
            fr.dve(v, 0, 0)
            fr.dve(v, 1, 1)

            def step(at):
                if at(2):
                    fr.dve(v, at(2)[2], at(2)[1])
                if not first(at(0)[2]):
                    add_output(nc, c, v, ob, o_done, o_free, at(0)[2] - 1)

            stream(v, GROUPS, 2, step)
            add_output(nc, c, v, ob, o_done, o_free, GROUPS - 1)

        @block.scalar
        def _(a):
            a.wait_ge(weights, 96)

            def gelu(k, p, fs):
                for f in fs:
                    a.wait_ge(h_done, 4 * k + f + 1)
                    nc.scalar.activation(hT[p][:, f, :], hb[f][:, :], ACT.Gelu_apprx_tanh,
                                         bias=b1[:, f:f + 1]).then_inc(gelu_done, 1)

            def copy_p(k, p):
                a.wait_ge(p_done, k + 1)
                nc.scalar.activation(pT[p][:, :], pb[0:R, :], ACT.Copy).then_inc(pT_ready, 1)

            def step(at):
                if at(1):
                    gelu(at(1)[2], at(1)[1], (0, 1))
                if at(2):
                    fr.act(a, at(2)[2], at(2)[1])
                if at(1):
                    gelu(at(1)[2], at(1)[1], (2, 3))
                a.wait_ge(q_done, at(0)[2] + 1)
                nc.scalar.activation(qT[:, :], qb[0:R, :], ACT.Copy).then_inc(qT_ready, 1)
                if at(2):
                    copy_p(at(2)[2], at(2)[1])

            fr.act(a, 0, 0)
            copy_p(0, 0)
            fr.act(a, 1, 1)
            gelu(0, 0, range(4))
            copy_p(1, 1)
            stream(a, GROUPS, 2, step)

        @block.tensor
        def _(pe):
            pe.wait_ge(weights, 96)

            def times_u1(k, p):
                pe.wait_ge(fr.xnT_ready, k + 1)
                nc.tensor.matmul(pb[0:R, :], u1[:, :], fr.xnT[p][:, :], start=True, stop=True).then_inc(p_done, 1)

            def hidden(k, p, fs):
                pe.wait_ge(pT_ready, k + 1)
                for f in fs:
                    if not first(k):
                        pe.wait_ge(gelu_done, 4 * k - 3 + f)
                    nc.tensor.matmul(hb[f][:, :], v1[:, f * P:(f + 1) * P], pT[p][:, :], start=True,
                                     stop=True).then_inc(h_done, 1)

            def times_u2(k, p, fs):
                for f in fs:
                    pe.wait_ge(gelu_done, 4 * k + f + 1)
                    m = nc.tensor.matmul(qb[0:R, :], u2[:, f, :], hT[p][:, f, :], start=(f == 0), stop=(f == 3))
                if 3 in fs:
                    m.then_inc(q_done, 1)

            def output(k):
                pe.wait_ge(qT_ready, k + 1)
                if not first(k):
                    pe.wait_ge(o_free, k)
                for t in range(TPG):
                    o = ob[:, t * D:(t + 1) * D]
                    nc.tensor.matmul(o, c.ones[0:1, :], b2[:, :], start=True, stop=False)
                    m = nc.tensor.matmul(o, qT[:, t * P:(t + 1) * P], v2[:, :], start=False, stop=True)
                m.then_inc(o_done, 1)

            def step(at):
                i, u, k = at(0)
                if not first(k):
                    output(k - 1)
                if at(1):
                    hidden(at(1)[2], at(1)[1], (0, 1))
                times_u2(k, u, (0, 1))
                if at(2):
                    fr.pe(pe, at(2)[2], at(2)[1])
                if at(1):
                    hidden(at(1)[2], at(1)[1], (2, 3))
                times_u2(k, u, (2, 3))
                if at(2):
                    times_u1(at(2)[2], at(2)[1])

            fr.pe(pe, 0, 0)
            times_u1(0, 0)
            fr.pe(pe, 1, 1)
            hidden(0, 0, range(4))
            times_u1(1, 1)
            stream(pe, GROUPS, 2, step)
            output(GROUPS - 1)


def ternary_ffn(nc, c, name, w):
    with Phase(nc, name) as ph:
        w1, w2 = ph.sb("w1", [P, 512]), ph.sb("w2", [P, 4, D])
        b1, b2 = ph.sb("b1", [P, 4]), ph.sb("b2", [1, D])
        tmp, part = ph.sb("tmp", [P, 512]), ph.sb("part", [P, 2])
        scale = ph.sb("scale", [P, 2])
        hT = [ph.sb(f"hT{i}", [P, 4, GT]) for i in range(2)]
        fr = Front(ph, c, c.x)
        ob = ph.bank("o")
        hb = [ph.bank(f"h{i}") for i in range(4)]
        weights, tern, sums, h_done, gelu_done, o_done, o_free = (
            ph.sem(s) for s in ("weights", "tern", "sums", "h_done", "gelu_done", "o_done", "o_free"))
        block = ph.block()
        MAGIC = 1.5 * 2.0 ** 23
        TERN = 2 * 8

        @block.sync
        def _(sp):
            for dst, src in ((w1, "L2_ffn_W1"), (w2, "L2_ffn_W2"), (b1, "L2_ffn_b1"), (b2, "L2_ffn_b2")):
                sp.dma_start(dst[:], w[src]).then_inc(weights, 16)
            sp.wait_ge(weights, 64)

        @block.gpsimd
        def _(g):
            front_two_ahead(fr, g)

        @block.vector
        def _(v):
            v.wait_ge(weights, 64)
            n = 0
            mats = (w1[:, :], w2[:, :, :].rearrange("p c d -> p (c d)"))

            def step(ins):
                ins.then_inc(tern, 1)

            for j, m in enumerate(mats):
                step(nc.vector.tensor_reduce(part[:, j:j + 1], m, AX_X, ALU.add, apply_absolute_value=True))
            v.wait_ge(sums, 1)
            step(nc.vector.tensor_scalar(scale[:, :], ob[:, 0:2], 1.0 / (512 * D), 1e-8, ALU.mult, ALU.max))
            v.wait_ge(tern, 3)
            step(nc.vector.reciprocal(part[:, :], scale[:, :]))
            n = 4
            for j, m in enumerate(mats):
                v.wait_ge(tern, n)
                step(nc.vector.tensor_scalar(tmp[:, :], m, part[:, j:j + 1], 1.0, ALU.mult, ALU.min))
                v.wait_ge(tern, n + 1)
                step(nc.vector.tensor_scalar(tmp[:, :], tmp[:, :], -1.0, MAGIC, ALU.max, ALU.add))
                v.wait_ge(tern, n + 2)
                step(nc.vector.scalar_tensor_tensor(out=tmp[:, :], in0=tmp[:, :], scalar=-MAGIC, in1=m, op0=ALU.add,
                                                    op1=ALU.subtract))
                v.wait_ge(tern, n + 3)
                step(nc.vector.tensor_tensor(m, m, tmp[:, :], ALU.add))
                n += 4
            fr.dve(v, 0, 0)
            fr.dve(v, 1, 1)

            def group(at):
                if at(2):
                    fr.dve(v, at(2)[2], at(2)[1])
                if not first(at(0)[2]):
                    add_output(nc, c, v, ob, o_done, o_free, at(0)[2] - 1)

            stream(v, GROUPS, 2, group)
            add_output(nc, c, v, ob, o_done, o_free, GROUPS - 1)

        @block.scalar
        def _(a):
            def gelu(k, p, fs):
                for f in fs:
                    a.wait_ge(h_done, 4 * k + f + 1)
                    nc.scalar.activation(hT[p][:, f, :], hb[f][:, :], ACT.Gelu,
                                         bias=b1[:, f:f + 1]).then_inc(gelu_done, 1)

            def group(at):
                if at(1):
                    gelu(at(1)[2], at(1)[1], (0, 1))
                if at(2):
                    fr.act(a, at(2)[2], at(2)[1])
                if at(1):
                    gelu(at(1)[2], at(1)[1], (2, 3))

            a.wait_ge(weights, 64)
            fr.act(a, 0, 0)
            fr.act(a, 1, 1)
            gelu(0, 0, range(4))
            stream(a, GROUPS, 2, group)

        @block.tensor
        def _(pe):
            pe.wait_ge(tern, 2)
            nc.tensor.matmul(ob[:, 0:2], c.ones[:, :], part[:, :], start=True, stop=True).then_inc(sums, 1)
            pe.wait_ge(tern, 12)

            def hidden(k, p, fs):
                pe.wait_ge(fr.xnT_ready, k + 1)
                for f in fs:
                    if not first(k):
                        pe.wait_ge(gelu_done, 4 * k - 3 + f)
                    nc.tensor.matmul(hb[f][:, :], w1[:, f * P:(f + 1) * P], fr.xnT[p][:, :], start=True,
                                     stop=True).then_inc(h_done, 1)

            def output(k, p, ts):
                if 0 in ts:
                    pe.wait_ge(gelu_done, 4 * k + 4)
                    if not first(k):
                        pe.wait_ge(o_free, k)
                for t in ts:
                    o = ob[:, t * D:(t + 1) * D]
                    nc.tensor.matmul(o, c.ones[0:1, :], b2[:, :], start=True, stop=False)
                    for f in range(4):
                        m = nc.tensor.matmul(o, hT[p][:, f, t * P:(t + 1) * P], w2[:, f, :], start=False,
                                             stop=(f == 3))
                if TPG - 1 in ts:
                    m.then_inc(o_done, 1)

            def group(at):
                i, u, k = at(0)
                if at(1):
                    hidden(at(1)[2], at(1)[1], (0, 1))
                output(k, u, (0, 1))
                if at(2):
                    fr.pe(pe, at(2)[2], at(2)[1])
                if at(1):
                    hidden(at(1)[2], at(1)[1], (2, 3))
                output(k, u, (2, 3))

            fr.pe(pe, 0, 0)
            fr.pe(pe, 1, 1)
            hidden(0, 0, range(4))
            stream(pe, GROUPS, 2, group)


def head_masks(nc, ph, g, made, target, width):
    n = target.shape[-1]
    nc.gpsimd.memset(target, 1.0).then_inc(made, 1)
    g.wait_ge(made, 1)
    nc.gpsimd.affine_select(out=target, in_=target, compare_op=ALU.is_ge, fill=0.0, base=0,
                            pattern=[[-width, n]], channel_multiplier=1).then_inc(made, 1)
    g.wait_ge(made, 2)
    nc.gpsimd.affine_select(out=target, in_=target, compare_op=ALU.is_gt, fill=0.0, base=width,
                            pattern=[[width, n]], channel_multiplier=-1).then_inc(made, 1)


def block_attention(nc, c, name, w):
    with Phase(nc, name) as ph:
        H, DK, B = 8, 16, 64

        def pair(n, shape):
            return [ph.sb(f"{n}{i}", shape) for i in range(2)]

        wq, wk, wv, wo = (ph.sb(s, [P, D]) for s in ("wq", "wk", "wv", "wo"))
        bq, bk = ph.sb("bq", [P, 1]), ph.sb("bk", [P, 1])
        bv, bo = ph.sb("bv", [1, D]), ph.sb("bo", [1, D])
        bqs = ph.sb("bqs", [P, 1])
        hm = ph.sb("hm", [P, H])
        sm = ph.sb("sm", [P, 2, DK])
        qT, kT, kexp = pair("qT", [P, GT]), ph.sb("kT", [P, GT]), pair("kexp", [P, H, GT])
        vbd = pair("vbd", [P, 8, 4, 32])
        mx, sc, pr, pT = pair("mx", [P, H]), pair("sc", [P, 512]), pair("pr", [P, 512]), pair("pT", [P, 512])
        rz, oT = pair("rz", [P, P]), pair("oT", [P, P])
        ba, bb = ph.bank("a"), ph.bank("b")
        fr = Front(ph, c, c.x, bank=ba, at_once=True)
        sb_, tb, ob = ([ph.bank(f"{n}{i}") for i in range(2)] for n in ("s", "t", "o"))
        (weights, made, ready, q_done, k_done, v_done, qT_ready, kT_ready, kexp_v, kexp_g, vbd_ready) = (
            ph.sem(s) for s in ("weights", "made", "ready", "q_done", "k_done", "v_done", "qT_ready", "kT_ready",
                                "kexp_v", "kexp_g", "vbd_ready"))
        s_done, mx_ready, sc_ready, pr_ready, t_done, pT_ready, oz_done, rz_ready, oT_ready, o_done, o_free = (
            ph.sem(s) for s in ("s_done", "mx_ready", "sc_ready", "pr_ready", "t_done", "pT_ready", "oz_done",
                                "rz_ready", "oT_ready", "o_done", "o_free"))
        block = ph.block()

        def tile(at, t):
            g = at(t // TPG)
            return g and (g[1], g[2], t % TPG, TPG * at(0)[2] + t)

        def tiles(at, job, t):
            if tile(at, t):
                job(*tile(at, t))

        def old(n):
            return not isinstance(n, int) or n >= 2

        @block.sync
        def _(sp):
            for dst, src in ((wq, "Wq"), (wk, "Wk"), (wv, "Wv"), (wo, "Wo"), (bq, "bq"), (bk, "bk"), (bv, "bv"),
                             (bo, "bo")):
                sp.dma_start(dst[:], w["L0_attn_" + src]).then_inc(weights, 16)
            sp.wait_ge(weights, 128)

        @block.gpsimd
        def _(g):
            fr.pool_start(g)
            head_masks(nc, ph, g, made, hm[:, :], DK)
            nc.gpsimd.memset(sm[:, :, :], 0.0).then_inc(made, 1)
            g.wait_ge(made, 4)
            for s in range(2):
                nc.gpsimd.memset(sm[B * s:B * s + B, s, :], 1.0).then_inc(made, 1)
            g.wait_ge(made, 6)

            def keys(u, k):
                g.wait_ge(kT_ready, k + 1)
                for h in range(H // 2, H):
                    nc.gpsimd.tensor_tensor(kexp[u][:, h, :], kT[:, :], hm[:, h:h + 1].to_broadcast([P, GT]),
                                            ALU.mult).then_inc(kexp_g, 1)

            keys(0, 0)
            stream(g, GROUPS, 2, lambda at: keys(at(1)[1], at(1)[2]) if at(1) else None)

        @block.vector
        def _(v):
            V = nc.vector
            v.wait_ge(weights, 128)
            V.tensor_scalar(bqs[:, :], bq[:, :], DK ** -0.5, None, ALU.mult).then_inc(ready, 1)
            fr.dve_start(v)
            v.wait_ge(made, 6)

            def keys(u, k):
                v.wait_ge(kT_ready, k + 1)
                for h in range(H // 2):
                    V.tensor_scalar(kexp[u][:, h, :], kT[:, :], hm[:, h:h + 1], None, ALU.mult).then_inc(kexp_v, 1)

            def values(u, k, half):
                v.wait_ge(v_done, 2 * k + half + 1)
                src = (bb, ba)[half]
                for j in range(4):
                    V.tensor_tensor(
                        vbd[u][:, 4 * half + j, :, :], src[:, j * P:(j + 1) * P].rearrange("p (h d) -> p h d", d=32),
                        sm[:, :, :].rearrange("p s d -> p (s d)").unsqueeze(1).to_broadcast([P, 4, 32]),
                        ALU.mult).then_inc(vbd_ready, 1)

            def soft(u, k, t, n):
                v.wait_ge(s_done, n + 1)
                s3 = sb_[t % 2][:, :].rearrange("p (h q) -> p h q", h=H)
                V.tensor_reduce(mx[t % 2][:, :], s3, AX_X, ALU.max).then_inc(mx_ready, 1)
                v.wait_ge(mx_ready, n + 1)
                if old(n):
                    v.wait_ge(pr_ready, n - 1)
                V.tensor_tensor(sc[t % 2][:, :].rearrange("p (h q) -> p h q", h=H), s3,
                                mx[t % 2][:, :].unsqueeze(2).to_broadcast([P, H, B]), ALU.subtract).then_inc(sc_ready, 1)

            def divide(u, k, t, n):
                v.wait_ge(oz_done, n + 1)
                V.reciprocal(rz[t % 2][:, :], ob[t % 2][:, P:2 * P]).then_inc(rz_ready, 1)
                v.wait_ge(rz_ready, n + 1)
                V.tensor_tensor(oT[t % 2][:, :], ob[t % 2][:, 0:P], rz[t % 2][:, :], ALU.mult).then_inc(oT_ready, 1)

            def group(at):
                for t in range(TPG):
                    tiles(at, soft, t + 2)
                    divide(*tile(at, t))
                    n = TPG * at(0)[2] + t
                    if not first(n):
                        add_tile(n - 1, (t - 1) % 2)
                    if at(1) and t == 0:
                        keys(at(1)[1], at(1)[2])
                    if at(1) and t in (1, 2):
                        values(at(1)[1], at(1)[2], t - 1)
                    if at(2) and t == 1:
                        fr.dve(v, at(2)[2], at(2)[1])

            def add_tile(n, p):
                v.wait_ge(o_done, n + 1)
                xt = c.x[:, bass.ds(n, 1), :]
                V.tensor_tensor(xt, ob[p][:, 2 * P:3 * P].unsqueeze(1), xt, ALU.add).then_inc(o_free, 1)

            fr.dve(v, 0, 0)
            keys(0, 0)
            values(0, 0, 0)
            values(0, 0, 1)
            fr.dve(v, 1, 1)
            soft(0, 0, 0, 0)
            soft(0, 0, 1, 1)
            stream(v, GROUPS, 2, group)
            add_tile(TILES - 1, 1)

        @block.scalar
        def _(a):
            A = nc.scalar
            a.wait_ge(ready, 1)

            def rows(u, k):
                fr.act(a, k, u)

            def queries_keys(u, k):
                a.wait_ge(q_done, k + 1)
                A.activation(qT[u][:, :], bb[:, :], ACT.Identity, bias=bqs[:, 0:1], scale=DK ** -0.5
                             ).then_inc(qT_ready, 1)
                a.wait_ge(k_done, k + 1)
                if not first(k):
                    a.wait_ge(kexp_v, H // 2 * k)
                    a.wait_ge(kexp_g, H // 2 * k)
                A.activation(kT[:, :], ba[:, :], ACT.Identity, bias=bk[:, 0:1]).then_inc(kT_ready, 1)

            def probs(u, k, t, n):
                a.wait_ge(sc_ready, n + 1)
                if old(n):
                    a.wait_ge(t_done, n - 1)
                A.activation(pr[t % 2][:, :], sc[t % 2][:, :], ACT.Exp).then_inc(pr_ready, 1)

            def copy(u, k, t, n):
                a.wait_ge(t_done, n + 1)
                if old(n):
                    a.wait_ge(oz_done, n - 1)
                A.activation(pT[t % 2][:, :], tb[t % 2][:, :], ACT.Copy).then_inc(pT_ready, 1)

            def group(at):
                for t in range(TPG):
                    tiles(at, copy, t + 1)
                    tiles(at, probs, t + 2)
                    if at(2) and t == 2:
                        rows(at(2)[1], at(2)[2])
                    if at(2) and t == 3:
                        queries_keys(at(2)[1], at(2)[2])

            rows(0, 0)
            queries_keys(0, 0)
            rows(1, 1)
            queries_keys(1, 1)
            probs(0, 0, 0, 0)
            copy(0, 0, 0, 0)
            probs(0, 0, 1, 1)
            stream(a, GROUPS, 2, group)

        @block.tensor
        def _(pe):
            T = nc.tensor
            pe.wait_ge(weights, 128)
            pe.wait_ge(made, 6)

            def turn_rows(u, k):
                if not first(k):
                    pe.wait_ge(vbd_ready, 8 * k)
                fr.pe(pe, k, u)

            def queries_keys(u, k):
                pe.wait_ge(fr.xnT_ready, k + 1)
                T.matmul(bb[:, :], wq[:, :], fr.xnT[u][:, :], start=True, stop=True).then_inc(q_done, 1)
                T.matmul(ba[:, :], wk[:, :], fr.xnT[u][:, :], start=True, stop=True).then_inc(k_done, 1)

            def values(u, k):
                for half in range(2):
                    pe.wait_ge((qT_ready, kT_ready)[half], k + 1)
                    for j in range(4):
                        tok = (4 * half + j) * B
                        for s in range(2):
                            o = (bb, ba)[half][s * B:(s + 1) * B, j * P:(j + 1) * P]
                            T.matmul(o, c.ones[0:1, 0:B], bv[:, :], start=True, stop=False)
                            m = T.matmul(o, fr.xnT[u][:, tok:tok + B], wv[:, :], start=False, stop=True)
                    m.then_inc(v_done, 1)

            def scores(u, k, t, n):
                if t == 0:
                    pe.wait_ge(kexp_v, H // 2 * (k + 1))
                    pe.wait_ge(kexp_g, H // 2 * (k + 1))
                if old(n):
                    pe.wait_ge(sc_ready, n - 1)
                for b in range(2):
                    tok = slice(t * P + b * B, t * P + b * B + B)
                    m = T.matmul(sb_[t % 2][b * B:(b + 1) * B, :].rearrange("p (h q) -> p h q", h=H),
                                 qT[u][:, tok], kexp[u][:, :, tok], start=True, stop=True)
                m.then_inc(s_done, 1)

            def turn(u, k, t, n):
                pe.wait_ge(pr_ready, n + 1)
                if old(n):
                    pe.wait_ge(pT_ready, n - 1)
                for j in range(4):
                    m = T.transpose(tb[t % 2][:, j * P:(j + 1) * P], pr[t % 2][:, j * P:(j + 1) * P], c.ident[:, :])
                m.then_inc(t_done, 1)

            def heads(u, k, t, n):
                pe.wait_ge(pT_ready, n + 1)
                if t == 0:
                    pe.wait_ge(vbd_ready, 8 * (k + 1))
                if old(n):
                    pe.wait_ge(o_free, n - 1)
                for b in range(2):
                    for off in (0, P):
                        for j in range(4):
                            lhsT = vbd[u][:, 2 * t + b, j, :] if off == 0 else sm[:, :, :].rearrange("p s d -> p (s d)")
                            m = T.matmul(ob[t % 2][32 * j:32 * j + 32, off + b * B:off + (b + 1) * B], lhsT,
                                         pT[t % 2][:, j * P + b * B:j * P + (b + 1) * B],
                                         start=True, stop=True, tile_position=(0, 32 * j))
                m.then_inc(oz_done, 1)

            def project(n, p):
                o = ob[p][:, 2 * P:3 * P]
                pe.wait_ge(oT_ready, n + 1)
                T.matmul(o, c.ones[0:1, :], bo[:, :], start=True, stop=False)
                T.matmul(o, oT[p][:, :], wo[:, :], start=False, stop=True).then_inc(o_done, 1)

            def group(at):
                for t in range(TPG):
                    tiles(at, scores, t + 2)
                    tiles(at, turn, t + 1)
                    heads(*tile(at, t))
                    n = TPG * at(0)[2] + t
                    if not first(n):
                        project(n - 1, (t - 1) % 2)
                    if at(1) and t == 0:
                        values(at(1)[1], at(1)[2])
                    if at(2) and t == 2:
                        turn_rows(at(2)[1], at(2)[2])
                    if at(2) and t == 3:
                        queries_keys(at(2)[1], at(2)[2])

            turn_rows(0, 0)
            queries_keys(0, 0)
            values(0, 0)
            turn_rows(1, 1)
            queries_keys(1, 1)
            scores(0, 0, 0, 0)
            scores(0, 0, 1, 1)
            turn(0, 0, 0, 0)
            stream(pe, GROUPS, 2, group)
            project(TILES - 1, 1)


class FullAttention:

    H, DK = 16, 8
    CH = 8
    STEPS = TPG * 8
    ORDER = [4 * (i % 4) + i // 4 for i in range(16)]
    BANK = [0, 1, 2, 0, 1, 2, 0, 1]

    def __init__(self, ph, c, wq, wk, wv, wo, bq=None, bk=None, bv=None, bo=None, mask=None):
        self.nc, self.c, self.ph = ph.nc, c, ph
        self.wq, self.wk, self.wv, self.wo, self.bq, self.bk, self.bv, self.bo = wq, wk, wv, wo, bq, bk, bv, bo
        self.mask = mask
        self.hm = ph.sb("hm", [P, self.H])
        self.vm = ph.sb("vm", [P, 4, 4, 8])
        self.kT = ph.sb("kT", [P, GT])
        self.qT = [ph.sb(f"qT{i}", [P, GT]) for i in range(2)]
        self.kexp = [ph.sb(f"kexp{i}", [P, self.H, GT]) for i in range(2)]
        self.vbd = [ph.sb(f"vbd{i}", [P, TPG, self.H, 32]) for i in range(2)]
        self.mx, self.zs = ph.sb("mx", [P, 2, self.H]), ph.sb("zs", [P, 2, self.H])
        self.pr = [ph.sb(f"pr{i}", [P, 512]) for i in range(4)]
        self.pT = [ph.sb(f"pT{i}", [P, 512]) for i in range(2)]
        self.rz, self.zT, self.oT = ph.sb("rz", [P, P]), ph.sb("zT", [P, P]), ph.sb("oT", [P, P])
        self.pb = ph.bank("proj")
        self.fr = Front(ph, c, c.x, bank=self.pb)
        self.sb_ = [ph.bank(f"s{i}") for i in range(3)]
        self.tb = [ph.bank(f"t{i}") for i in range(2)]
        self.ob = [ph.bank(f"o{i}") for i in range(2)]
        self.made, self.q_done, self.k_done, self.v_done, self.qT_ready, self.kT_ready = (
            ph.sem(s) for s in ("made", "q_done", "k_done", "v_done", "qT_ready", "kT_ready"))
        self.kexp_ready, self.vbd_ready, self.s_done, self.mx_ready, self.pr_ready, self.t_done = (
            ph.sem(s) for s in ("kexp_ready", "vbd_ready", "s_done", "mx_ready", "pr_ready", "t_done"))
        self.pT_ready, self.rz_ready, self.oz_done, self.oT_ready, self.o_done, self.o_free = (
            ph.sem(s) for s in ("pT_ready", "rz_ready", "oz_done", "oT_ready", "o_done", "o_free"))
        self.zT_ready = ph.sem("zT_ready")

    MADE = 8

    def pool_setup(self, g):
        nc = self.nc
        head_masks(nc, self.ph, g, self.made, self.hm[:, :], self.DK)
        nc.gpsimd.memset(self.vm[:, :, :, :], 0.0).then_inc(self.made, 1)
        g.wait_ge(self.made, 4)
        for i in range(4):
            nc.gpsimd.memset(self.vm[:, i, i, :], 1.0).then_inc(self.made, 1)

    def later(self, s, now, nxt):
        if s < self.STEPS:
            return now[1], now[2], s // self.CH, s % self.CH
        return None if nxt is None else (nxt[1], nxt[2], 0, s - self.STEPS)

    def before(self, t, now):
        u, k = now[1], now[2]
        if t:
            return u, k, t - 1, TPG * k + t - 1
        return None if first(k) else (1 - u, k - 1, TPG - 1, TPG * k - 1)


    def dve_start(self, v, between=None):
        self.fr.dve(v, 0, 0)
        if between:
            between()
        for t in range(TPG):
            self.dve_values(v, 0, 0, t)
        self.dve_maxima(v, 0, 0, 0, 0)
        self.dve_maxima(v, 0, 0, 0, 1)

    def dve_maxima(self, v, u, k, t, q):
        v.wait_ge(self.s_done, self.CH * (TPG * k + t) + q + 1)
        self.nc.vector.tensor_reduce(self.mx[:, t % 2, 2 * q:2 * q + 2],
                                     self.sb_[self.BANK[q]][:, :].rearrange("p (h s) -> p h s", h=2), AX_X, ALU.max,
                                     negate=True).then_inc(self.mx_ready, 1)

    def dve_values(self, v, u, k, t):
        if t == 0:
            v.wait_ge(self.v_done, k + 1)
        for j in range(4):
            self.nc.vector.tensor_tensor(
                self.vbd[u][:, t, 4 * j:4 * j + 4, :],
                self.pb[:, t * P + 32 * j:t * P + 32 * j + 32].unsqueeze(1).to_broadcast([P, 4, 32]),
                self.vm[:, :, :, :].rearrange("p i a b -> p i (a b)"), ALU.mult).then_inc(self.vbd_ready, 1)

    def dve_inverse(self, v, tile):
        u, k, t, n = tile
        v.wait_ge(self.pr_ready, self.CH * (n + 1))
        self.nc.vector.reciprocal(
            self.rz[:, :].rearrange("p (a b d) -> p b a d", a=4, b=4),
            self.zs[:, t % 2, :].rearrange("p (b a) -> p b a", b=4).unsqueeze(3).to_broadcast([P, 4, 4, 8])
            ).then_inc(self.rz_ready, 1)

    def dve_divide(self, v, tile):
        u, k, t, n = tile
        v.wait_ge(self.oz_done, n + 1)
        self.nc.vector.tensor_copy(self.zT[:, :], self.ob[t % 2][:, P:2 * P]).then_inc(self.zT_ready, 1)
        v.wait_ge(self.zT_ready, n + 1)
        self.nc.vector.tensor_tensor(self.oT[:, :], self.ob[t % 2][:, 0:P], self.zT[:, :],
                                     ALU.mult).then_inc(self.oT_ready, 1)

    def dve_finish(self, v, tile, finish):
        v.wait_ge(self.o_done, tile[3] + 1)
        finish(tile, self.ob[tile[2] % 2][:, 2 * P:3 * P])

    def dve(self, v, now, nxt, finish, between=None):
        for s in range(self.STEPS):
            t, q = s // self.CH, s % self.CH
            n = self.CH * TPG * now[2] + s
            ahead2 = self.later(s + 2, now, nxt)
            if ahead2:
                self.dve_maxima(v, *ahead2)
            v.wait_ge(self.t_done, n + 1)
            self.nc.vector.tensor_copy(self.pT[q % 2][:, :], self.tb[q % 2][:, :]).then_inc(self.pT_ready, 1)
            tile = self.before(t, now)
            if tile and q == 0:
                self.dve_inverse(v, tile)
            if tile and q == 2:
                self.dve_divide(v, tile)
            if tile and q == 5:
                self.dve_finish(v, tile, finish)
            if nxt and s == 10:
                self.fr.dve_stats(v, nxt[2])
            if nxt and s == 14:
                self.fr.dve_rows(v, nxt[2], nxt[1])
            if nxt and 23 <= s < 27:
                self.dve_values(v, nxt[1], nxt[2], s - 23)
            if between:
                between(s)

    def last_tile(self):
        return 1, GROUPS - 1, TPG - 1, TILES - 1

    def dve_end(self, v, finish):
        tile = self.last_tile()
        self.dve_inverse(v, tile)
        self.dve_divide(v, tile)
        self.dve_finish(v, tile, finish)


    def act_queries(self, a, u, k):
        nc, s = self.nc, self.DK ** -0.5
        a.wait_ge(self.q_done, k + 1)
        if self.bq is None:
            nc.scalar.activation(self.qT[u][:, :], self.pb[:, :], ACT.Copy, scale=s).then_inc(self.qT_ready, 1)
        else:
            nc.scalar.activation(self.qT[u][:, :], self.pb[:, :], ACT.Identity, bias=self.bq[:, 0:1],
                                 scale=s).then_inc(self.qT_ready, 1)

    def act_keys(self, a, u, k):
        nc = self.nc
        a.wait_ge(self.k_done, k + 1)
        if self.bk is None:
            nc.scalar.activation(self.kT[:, :], self.pb[:, :], ACT.Copy).then_inc(self.kT_ready, 1)
        else:
            nc.scalar.activation(self.kT[:, :], self.pb[:, :], ACT.Identity,
                                 bias=self.bk[:, 0:1]).then_inc(self.kT_ready, 1)

    def act_head_keys(self, a, u, k, i):
        if i == 0:
            a.wait_ge(self.kT_ready, k + 1)
        h = self.ORDER[i]
        self.nc.scalar.activation(self.kexp[u][:, i, :], self.kT[:, :], ACT.Copy,
                                  scale=self.hm[:, h:h + 1]).then_inc(self.kexp_ready, 1)

    def act_start(self, a):
        a.wait_ge(self.made, self.MADE)
        self.fr.act(a, 0, 0)
        self.act_queries(a, 0, 0)
        self.act_keys(a, 0, 0)
        for i in range(self.H):
            self.act_head_keys(a, 0, 0, i)

    def act(self, a, now, nxt, between=None):
        for s in range(self.STEPS):
            t, q = s // self.CH, s % self.CH
            a.wait_ge(self.mx_ready, self.CH * TPG * now[2] + s + 1)
            for h in range(2):
                m = self.nc.scalar.activation(self.pr[q % 4][:, 256 * h:256 * h + 256],
                                              self.sb_[self.BANK[q]][:, 256 * h:256 * h + 256], ACT.Exp,
                                              bias=self.mx[:, t % 2, 2 * q + h:2 * q + h + 1],
                                              accum_out=self.zs[:, t % 2, 2 * q + h:2 * q + h + 1])
            m.then_inc(self.pr_ready, 1)
            if nxt:
                _, u, k = nxt
                if s == 17:
                    self.fr.act(a, k, u)
                if s == 19:
                    self.act_queries(a, u, k)
                if s == 21:
                    self.act_keys(a, u, k)
                if 22 <= s < 30:
                    self.act_head_keys(a, u, k, 2 * (s - 22))
                    self.act_head_keys(a, u, k, 2 * (s - 22) + 1)
            if between:
                between(s)


    def pe_rows(self, pe, u, k):
        if not first(k):
            pe.wait_ge(self.vbd_ready, 16 * k)
        self.fr.pe(pe, k, u)

    def pe_queries(self, pe, u, k):
        pe.wait_ge(self.fr.xnT_ready, k + 1)
        self.nc.tensor.matmul(self.pb[:, :], self.wq[:, :], self.fr.xnT[u][:, :], start=True,
                              stop=True).then_inc(self.q_done, 1)

    def pe_keys(self, pe, u, k):
        pe.wait_ge(self.qT_ready, k + 1)
        self.nc.tensor.matmul(self.pb[:, :], self.wk[:, :], self.fr.xnT[u][:, :], start=True,
                              stop=True).then_inc(self.k_done, 1)

    def pe_values(self, pe, u, k):
        pe.wait_ge(self.kT_ready, k + 1)
        for t in range(TPG):
            o = self.pb[:, t * P:(t + 1) * P]
            if self.bv is not None:
                self.nc.tensor.matmul(o, self.c.ones[0:1, :], self.bv[:, :], start=True, stop=False)
            m = self.nc.tensor.matmul(o, self.fr.xnT[u][:, t * P:(t + 1) * P], self.wv[:, :], start=self.bv is None,
                                      stop=True)
        m.then_inc(self.v_done, 1)

    def pe_scores(self, pe, u, k, t, q):
        n = self.CH * (TPG * k + t) + q
        if (t, q) == (0, 0):
            pe.wait_ge(self.kexp_ready, self.H * (k + 1))
        if q == 0 and not (first(k) and t == 0):
            pe.wait_ge(self.pr_ready, n - 1)
        if q == 1 and not (first(k) and t == 0):
            pe.wait_ge(self.pr_ready, n - 1)
        b, o = t // 2, self.sb_[self.BANK[q]][:, :].rearrange("p (h s) -> p h s", h=2)
        m = self.nc.tensor.matmul(o, self.qT[u][:, t * P:(t + 1) * P],
                                  self.kexp[u][:, 2 * q:2 * q + 2, SEQ * b:SEQ * b + SEQ], start=True,
                                  stop=self.mask is None)
        if self.mask is not None:
            m = self.nc.tensor.matmul(o, self.c.ident_b[:, :],
                                      self.mask[:, t % 2, :].unsqueeze(1).to_broadcast([P, 2, SEQ]), start=False,
                                      stop=True)
        m.then_inc(self.s_done, 1)

    def pe_heads(self, pe, u, k, t, q):
        tile = TPG * k + t
        if q == 0 and not (first(k) and t < 2):
            pe.wait_ge(self.o_free, tile - 1)
        pe.wait_ge(self.pT_ready, self.CH * tile + q + 1)
        for half in range(2):
            for j in range(2):
                h = self.ORDER[2 * q + j]
                quad, i = h // 4, h % 4
                self.nc.tensor.matmul(self.ob[t % 2][32 * quad:32 * quad + 32, 0:P],
                                      self.vbd[u][:, 2 * (t // 2) + half, h, :],
                                      self.pT[q % 2][:, 256 * j + P * half:256 * j + P * half + P],
                                      start=(i == 0 and half == 0), stop=(i == 3 and half == 1),
                                      tile_position=(0, 32 * quad), skip_group_check=True)

    def pe_sums(self, pe, tile):
        u, k, t, n = tile
        pe.wait_ge(self.rz_ready, n + 1)
        self.nc.tensor.transpose(self.ob[t % 2][:, P:2 * P], self.rz[:, :], self.c.ident[:, :]).then_inc(self.oz_done, 1)

    def pe_project(self, pe, tile):
        u, k, t, n = tile
        o = self.ob[t % 2][:, 2 * P:3 * P]
        pe.wait_ge(self.oT_ready, n + 1)
        if self.bo is not None:
            self.nc.tensor.matmul(o, self.c.ones[0:1, :], self.bo[:, :], start=True, stop=False)
        self.nc.tensor.matmul(o, self.oT[:, :], self.wo[:, :], start=self.bo is None, stop=True).then_inc(self.o_done, 1)

    def pe_start(self, pe, before_scores=None):
        self.pe_rows(pe, 0, 0)
        self.pe_queries(pe, 0, 0)
        self.pe_keys(pe, 0, 0)
        self.pe_values(pe, 0, 0)
        if before_scores:
            before_scores()
        self.pe_scores(pe, 0, 0, 0, 0)
        self.pe_scores(pe, 0, 0, 0, 1)

    def pe(self, pe, now, nxt):
        for s in range(self.STEPS):
            t, q = s // self.CH, s % self.CH
            ahead2 = self.later(s + 2, now, nxt)
            if ahead2:
                self.pe_scores(pe, *ahead2)
            pe.wait_ge(self.pr_ready, self.CH * TPG * now[2] + s + 1)
            for j in range(4):
                m = self.nc.tensor.transpose(self.tb[q % 2][:, j * P:(j + 1) * P], self.pr[q % 4][:, j * P:(j + 1) * P],
                                             self.c.ident[:, :])
            m.then_inc(self.t_done, 1)
            if s == 1:
                pe.wait_ge(self.vbd_ready, 16 * (now[2] + 1))
            tile = self.before(t, now)
            if s:
                self.pe_heads(pe, now[1], now[2], (s - 1) // self.CH, (s - 1) % self.CH)
            elif tile:
                self.pe_heads(pe, tile[0], tile[1], tile[2], self.CH - 1)
            if tile and q == 1:
                self.pe_sums(pe, tile)
            if tile and q == 4:
                self.pe_project(pe, tile)
            if nxt:
                _, u, k = nxt
                if s == 16:
                    self.pe_rows(pe, u, k)
                if s == 18:
                    self.pe_queries(pe, u, k)
                if s == 20:
                    self.pe_keys(pe, u, k)
                if s == 22:
                    self.pe_values(pe, u, k)

    def pe_end(self, pe):
        tile = self.last_tile()
        self.pe_heads(pe, tile[0], tile[1], tile[2], self.CH - 1)
        self.pe_sums(pe, tile)
        self.pe_project(pe, tile)


def window_attention(nc, c, name, w):
    with Phase(nc, name) as ph:
        HALF, NG = 32, 16
        wq, wk, wv, wo = (ph.sb(s, [P, D]) for s in ("wq", "wk", "wv", "wo"))
        gi, gf, gneg = ph.sb("gi", [P, NG], I32), ph.sb("gf", [P, NG]), ph.sb("gneg", [P, NG])
        posi, pos = ph.sb("posi", [P, 2], I32), ph.sb("pos", [P, 2])
        cposi, cpos = ph.sb("cposi", [P, SEQ], I32), ph.sb("cpos", [P, SEQ])
        hit, hit_q, hit_k = ph.sb("hit", [P, NG, SEQ]), ph.sb("hit_q", [P, 2]), ph.sb("hit_k", [P, SEQ])
        near, far, mask = ph.sb("near", [P, 2, SEQ]), ph.sb("far", [P, 2, SEQ]), ph.sb("mask", [P, 2, SEQ], BF16)
        at = FullAttention(ph, c, wq, wk, wv, wo, mask=mask)
        fr = at.fr
        weights, placed, step = ph.sem("weights"), ph.sem("placed"), ph.sem("step")
        block = ph.block()

        @block.sync
        def _(sp):
            for dst, src in ((wq, "Wq"), (wk, "Wk"), (wv, "Wv"), (wo, "Wo")):
                sp.dma_start(dst[:], w["L2_attn_" + src]).then_inc(weights, 16)
            sp.dma_start(gi[:, :], w["L2_attn_global_token_indices"][0, :].partition_broadcast(P)).then_inc(weights, 16)
            sp.wait_ge(weights, 80)

        @block.gpsimd
        def _(g):
            nc.gpsimd.iota(posi[:, :], pattern=[[P, 2]], base=0, channel_multiplier=1).then_inc(placed, 1)
            nc.gpsimd.iota(cposi[:, :], pattern=[[1, SEQ]], base=0, channel_multiplier=0).then_inc(placed, 1)
            at.pool_setup(g)
            ahead(g, GROUPS, 2, lambda i, u, k: fr.pool(g, k), lambda i, u, k: None)

        @block.vector
        def _(v):
            done = [0]

            def link(ins):
                done[0] += 1
                ins.then_inc(step, 1)
                v.wait_ge(step, done[0])

            def make_mask():
                v.wait_ge(weights, 80)
                v.wait_ge(placed, 2)
                link(nc.vector.tensor_copy(c.ident_b[:, :], c.ident[:, :]))
                link(nc.vector.tensor_copy(pos[:, :], posi[:, :]))
                link(nc.vector.tensor_copy(cpos[:, :], cposi[:, :]))
                link(nc.vector.tensor_copy(gf[:, :], gi[:, :]))
                link(nc.vector.tensor_scalar(gneg[:, :], gf[:, :], 0.0, float(SEQ), ALU.is_lt, ALU.mult))
                link(nc.vector.tensor_tensor(gf[:, :], gf[:, :], gneg[:, :], ALU.add))
                link(nc.vector.tensor_tensor(hit[:, :, :], cpos[:, :].unsqueeze(1).to_broadcast([P, NG, SEQ]),
                                             gf[:, :].unsqueeze(2).to_broadcast([P, NG, SEQ]), ALU.is_equal))
                link(nc.vector.tensor_reduce(hit_k[:, :], hit[:, :, :].rearrange("p g s -> p s g"), AX_X, ALU.max))
                for t in range(2):
                    link(nc.vector.tensor_scalar(gneg[:, :], gf[:, :], pos[:, t:t + 1], None, ALU.is_equal))
                    link(nc.vector.tensor_reduce(hit_q[:, t:t + 1], gneg[:, :], AX_X, ALU.max))
                    d = near[:, t, :]
                    link(nc.vector.tensor_scalar(d, cpos[:, :], pos[:, t:t + 1], None, ALU.subtract))
                    link(nc.vector.tensor_scalar(far[:, t, :], d, -1.0, None, ALU.mult))
                    link(nc.vector.tensor_tensor(d, d, far[:, t, :], ALU.max))
                    link(nc.vector.tensor_scalar(d, d, float(HALF), hit_q[:, t:t + 1], ALU.is_le, ALU.max))
                    link(nc.vector.tensor_tensor(d, d, hit_k[:, :], ALU.max))
                    link(nc.vector.tensor_scalar(mask[:, t, :], d, -1.0, 1e30, ALU.add, ALU.mult))

            v.wait_ge(at.made, at.MADE)

            def finish(tile, o):
                xt = c.x[:, bass.ds(tile[3], 1), :]
                nc.vector.tensor_tensor(xt, o.unsqueeze(1), xt, ALU.add).then_inc(at.o_free, 1)

            at.dve_start(v, make_mask)
            weave(v, GROUPS, 2, lambda now, nxt: at.dve(v, now, nxt, finish))
            at.dve_end(v, finish)

        @block.scalar
        def _(a):
            at.act_start(a)
            weave(a, GROUPS, 2, lambda now, nxt: at.act(a, now, nxt))

        @block.tensor
        def _(pe):
            pe.wait_ge(weights, 80)
            at.pe_start(pe, lambda: pe.wait_ge(step, 8 + 2 * 8))
            weave(pe, GROUPS, 2, lambda now, nxt: at.pe(pe, now, nxt))
            at.pe_end(pe)


class Mixture:

    def __init__(self, nc, ctx, name, E):
        self.R = D + E + 1
        self.rows = nc.dram_tensor(f"{name}_rows", (SLOTS, self.R), F32, kind="Internal").ap()
        self.tables = [nc.dram_tensor(f"{name}_table{i}", (TOKENS + DUMPS * SUB, D), F32, kind="Internal").ap()
                       for i in range(TABLES)]
        self.cleared = ctx.enter_context(nc.semaphore(f"{name}_cleared"))

    CLEARED = 16 * (DUMPS + 2 * TABLES)


def clear_next(c, sp):
    if not c.to_clear:
        return
    m = c.to_clear.pop(0)
    for a in range(DUMPS):
        sp.dma_start(m.rows.rearrange("(n a p) r -> p a n r", a=DUMPS, p=SUB)[:, a, :, :],
                     c.blank[0:SUB, a:a + 1, -m.R:].to_broadcast([SUB, SLOTS // SUB // DUMPS, m.R])
                     ).then_inc(m.cleared, 16)
    for t in m.tables:
        sp.dma_start(t[0:TOKENS, :].rearrange("(n p) d -> p n d", p=P),
                     c.zero[:, :].unsqueeze(1).to_broadcast([P, TILES, D])).then_inc(m.cleared, 16)
        sp.dma_start(t[TOKENS:, :].rearrange("(a p) d -> p a d", p=SUB),
                     c.zero[0:SUB, :].unsqueeze(1).to_broadcast([SUB, DUMPS, D])).then_inc(m.cleared, 16)


class Shared:

    F = 3

    def __init__(self, ph, c, w1, w2):
        self.nc, self.c, self.w1, self.w2 = ph.nc, c, w1, w2
        self.hb = [[ph.bank(f"h{j}{i}") for i in range(2)] for j in range(2)]
        self.ob = ph.bank("o")
        self.sT, self.gT = ph.sb("sT", [P, 2, GT]), ph.sb("gT", [P, self.F, GT])
        self.h_done, self.silu_ready, self.gT_ready, self.o_done, self.o_free = (
            ph.sem(s) for s in ("h_done", "silu_ready", "gT_ready", "o_done", "o_free"))

    def pe_hidden(self, pe, k, xT, f):
        n = self.F * k + f
        pe.wait_ge(self.gT_ready, n + 1)
        for j in range(2):
            m = self.nc.tensor.matmul(self.hb[j][f % 2][:, :], self.w1[:, (self.F * j + f) * P:(self.F * j + f + 1) * P],
                                      xT[:, :], start=True, stop=True)
        m.then_inc(self.h_done, 1)

    def pe(self, pe, k, xT):
        for f in range(self.F):
            self.pe_hidden(pe, k, xT, f)
        pe.wait_ge(self.gT_ready, self.F * (k + 1) + 2)
        pe.wait_ge(self.o_free, k + 1)
        for t in range(TPG):
            for f in range(self.F):
                m = self.nc.tensor.matmul(self.ob[:, t * D:(t + 1) * D], self.gT[:, f, t * P:(t + 1) * P],
                                          self.w2[:, f, :], start=(f == 0), stop=(f == self.F - 1))
        m.then_inc(self.o_done, 1)

    def act(self, a, k):
        for f in range(self.F):
            n = self.F * k + f
            a.wait_ge(self.h_done, n + 1)
            a.wait_ge(self.gT_ready, n + 1)
            self.nc.scalar.activation(self.sT[:, f % 2, :], self.hb[1][f % 2][:, :],
                                      ACT.Silu).then_inc(self.silu_ready, 1)

    def dve_init(self, v):
        v.sem_inc(self.gT_ready, 2)
        v.sem_inc(self.o_free, 1)

    def dve_gate(self, v, k, f):
        v.wait_ge(self.silu_ready, self.F * k + f + 1)
        self.nc.vector.tensor_tensor(self.gT[:, f, :], self.hb[0][f % 2][:, :], self.sT[:, f % 2, :],
                                     ALU.mult).then_inc(self.gT_ready, 1)

    def dve_add(self, v, k):
        v.wait_ge(self.o_done, k + 1)
        xt = tiles4(self.c.x, k)
        self.nc.vector.scalar_tensor_tensor(out=xt, in0=self.ob[:, :].rearrange("p (t d) -> p t d", t=TPG), scalar=0.5,
                                            in1=xt, op0=ALU.mult, op1=ALU.add).then_inc(self.o_free, 1)


def route(nc, c, name, w, source, m, gate, E, K, CAP, kind, shared=None):
    with Phase(nc, name) as ph:
        R = D + E + 1
        wg = ph.sb("wg", [P, E])
        row = [ph.sb(f"row{i}", [P, TPG, R]) for i in range(2)]
        rows = m.rows
        idx = [ph.sb(f"idx{i}", [P, TPG, K], U32) for i in range(2)]
        first_slot = ph.sb("first_slot", [P, E])
        lg, gates, slot, over = (ph.sb(s, [P, TPG, E]) for s in ("lg", "gates", "slot", "over"))
        top, topi, topf = ph.sb("top", [P, TPG, 8]), ph.sb("topi", [P, TPG, 8], U32), ph.sb("topf", [P, TPG * K])
        slotf, mx, total = ph.sb("slotf", [P, TPG * K]), ph.sb("mx", [P, TPG]), ph.sb("total", [P, TPG])
        hot, pick = ph.sb("hot", [P, TPG * K, E]), ph.sb("pick", [P, TPG * K, E])
        mask, cum = ph.sb("mask", [P, TPG, E], BF16), [ph.sb(f"cum{i}", [P, E], BF16) for i in range(2)]
        part = ph.sb("part", [P, E], BF16)
        if shared:
            sw1, sw2 = ph.sb("sw1", [P, 768]), ph.sb("sw2", [P, 3, D])
            sh = Shared(ph, c, sw1, sw2)
        fr = Front(ph, c, source, norm=(kind == "softmax"), at_once=True)
        lb, rb = ph.bank("logits"), ph.bank("rank")
        (weights, consts, row_ready, l_done, l_ready, e_ready, steps, masked, ranked, cum_ready, sent_ready) = (
            ph.sem(s) for s in ("weights", "consts", "row_ready", "l_done", "l_ready", "e_ready", "steps", "masked",
                                "ranked", "cum_ready", "sent_ready"))
        full, leastf, least_ready = [ph.sb(f"full{i}", [P, 1], I32) for i in range(2)], ph.sb("leastf", [P, 1]), ph.sem(
            "least_ready")
        sent, rows_free = ph.sem("sent"), ph.sem("rows_free")
        PER = 16 * TPG * K
        block = ph.block()
        loads = [(wg, gate)] + ([(sw1, "L0_ffn_shared_w1"), (sw2, "L0_ffn_shared_w2")] if shared else [])

        @block.sync
        def _(sp):
            for dst, src in loads:
                sp.dma_start(dst[:], w[src]).then_inc(weights, 16)
            sp.wait_ge(weights, 16 * len(loads))

        @block.gpsimd
        def _(g):
            g.sem_inc(rows_free, 2)
            fr.pool_start(g)

            def body(i, u, k):
                hold(g, c.mark_g, row_ready, k + 1)
                hold(g, c.mark_g, sent_ready, 2 * (k + 1))
                least = g.value_load(full[u][0:1, 0:1], min_val=0, max_val=TOKENS)
                with g.If(least < CAP):
                    for t in range(TPG):
                        for j in range(K):
                            g.indirect_dma_start(out=rows, out_offset=bass.IndirectOffsetOnAxis(
                                ap=idx[u][:, t, j:j + 1], axis=0), in_=row[u][:, t, :], in_offset=None,
                                bounds_check=SLOTS - 1, oob_is_err=False).then_inc(sent, 16)
                    hold(g, c.mark_g, sent, PER * (k + 1))
                g.sem_inc(rows_free, 1)

            g.wait_ge(m.cleared, m.CLEARED)
            ahead(g, GROUPS, 2, lambda i, u, k: fr.pool(g, k), body)

        @block.vector
        def _(v):
            nc.vector.tensor_scalar(first_slot[:, :], c.expert_id[:, 0:E], float(CAP), None, ALU.mult).then_inc(consts, 1)
            nc.vector.memset(cum[0][:, :], 0.0).then_inc(consts, 1)
            fr.dve_start(v)
            if shared:
                sh.dve_init(v)
            STEPS = 19 if kind == "softmax" else 16

            def front(i, u, k):
                if not isinstance(k, int) or k >= 2:
                    v.wait_ge(row_ready, k - 1)
                fr.dve(v, k, u)

            def body(i, u, k):
                done = [0]

                def link(*ins, wait=True):
                    for x in ins:
                        x.then_inc(steps, 1)
                    done[0] += 1 if len(ins) == 1 else 0
                    if wait:
                        v.wait_ge(steps, STEPS * k + done[0])

                v.wait_ge(l_done, k + 1)
                l3 = lb[:, 0:TPG * E].rearrange("p (t e) -> p t e", t=TPG)

                def spread(a):
                    return a.unsqueeze(2).to_broadcast([P, TPG, E])

                if kind == "softmax":
                    link(nc.vector.tensor_reduce(mx[:, :], l3, AX_X, ALU.max))
                    nc.vector.tensor_tensor(lg[:, :, :], l3, spread(mx[:, :]), ALU.subtract).then_inc(l_ready, 1)
                    v.wait_ge(e_ready, k + 1)
                    link(nc.vector.tensor_reduce(mx[:, :], lg[:, :, :], AX_X, ALU.add))
                    link(nc.vector.reciprocal(mx[:, :], mx[:, :]))
                    link(nc.vector.tensor_tensor(gates[:, :, :], lg[:, :, :], spread(mx[:, :]), ALU.mult), wait=False)
                else:
                    v.wait_ge(e_ready, k + 1)
                    link(nc.vector.tensor_copy(gates[:, :, :], lg[:, :, :]), wait=False)
                hold(v, c.mark_v, steps, STEPS * k + done[0])
                for t in range(TPG):
                    m = nc.vector.max(top[:, t, :], gates[:, t, :])
                link(m, wait=False)
                hold(v, c.mark_v, steps, STEPS * k + done[0])
                for t in range(TPG):
                    m = nc.vector.max_index(topi[:, t, :], top[:, t, :], gates[:, t, :])
                link(m)
                link(nc.vector.tensor_copy(topf[:, :].rearrange("p (t j) -> p t j", t=TPG), topi[:, :, 0:K]))
                link(nc.vector.tensor_tensor(hot[:, :, :],
                                             c.expert_id[:, 0:E].unsqueeze(1).to_broadcast([P, TPG * K, E]),
                                             topf[:, :].unsqueeze(2).to_broadcast([P, TPG * K, E]), ALU.is_equal))
                with nc.allow_low_precision("zeros and ones"):
                    nc.vector.tensor_reduce(mask[:, :, :], hot[:, :, :].rearrange("p (t j) e -> p t e j", t=TPG), AX_X,
                                            ALU.add).then_inc(masked, 1)
                v.wait_ge(masked, k + 1)
                with nc.allow_low_precision("counts up to 32"):
                    link(nc.vector.tensor_reduce(part[:, :], mask[:, :, :].rearrange("p t e -> p e t"), AX_X, ALU.add))
                    nc.vector.tensor_tensor(cum[1 - u][:, :], cum[u][:, :], part[:, :], ALU.add).then_inc(cum_ready, 1)
                if shared:
                    for f in range(2):
                        sh.dve_gate(v, k, f)
                link(nc.vector.tensor_reduce(total[:, :], top[:, :, 0:K], AX_X, ALU.add))
                if kind == "softmax":
                    link(nc.vector.tensor_scalar(total[:, :], total[:, :], 2.0 ** -23, None, ALU.max))
                else:
                    link(nc.vector.tensor_scalar(total[:, :], total[:, :], 1e-6, None, ALU.add))
                link(nc.vector.reciprocal(total[:, :], total[:, :]))
                v.wait_ge(rows_free, k + 1)
                link(nc.vector.tensor_tensor(row[u][:, :, D:D + E], gates[:, :, :], spread(total[:, :]), ALU.mult),
                     wait=False)
                nc.vector.tensor_copy(row[u][:, :, R - 1:R], c.token_id[:, bass.ds(TPG * k, TPG)].unsqueeze(2)
                                      ).then_inc(steps, 1)
                done[0] += 1
                v.wait_ge(ranked, k + 1)
                r3 = rb[:, 0:TPG * E].rearrange("p (t e) -> p t e", t=TPG)
                link(nc.vector.tensor_scalar(over[:, :, :], r3, float(CAP), FAR, ALU.is_ge, ALU.mult), wait=False)
                link(nc.vector.tensor_tensor(slot[:, :, :], r3,
                                             first_slot[:, :].unsqueeze(1).to_broadcast([P, TPG, E]), ALU.add))
                link(nc.vector.tensor_tensor(slot[:, :, :], slot[:, :, :], over[:, :, :], ALU.add))
                link(nc.vector.tensor_tensor(pick[:, :, :].rearrange("p (t j) e -> p t j e", t=TPG),
                                             hot[:, :, :].rearrange("p (t j) e -> p t j e", t=TPG),
                                             slot[:, :, :].unsqueeze(2).to_broadcast([P, TPG, K, E]), ALU.mult))
                link(nc.vector.tensor_reduce(slotf[:, :], pick[:, :, :], AX_X, ALU.add))
                assert done[0] == STEPS, done
                nc.vector.tensor_reduce(leastf[:, :], rb[:, 0:E], AX_X, ALU.min).then_inc(least_ready, 1)
                v.wait_ge(least_ready, k + 1)
                nc.vector.tensor_copy(full[u][:, :], leastf[:, :]).then_inc(sent_ready, 1)
                nc.vector.tensor_copy(idx[u][:, :, :].rearrange("p t j -> p (t j)"), slotf[:, :]).then_inc(sent_ready, 1)
                if shared:
                    sh.dve_gate(v, k, 2)
                    sh.dve_add(v, k)

            ahead(v, GROUPS, 2, front, body)

        @block.scalar
        def _(a):
            def body(i, u, k):
                if kind == "softmax":
                    a.wait_ge(l_ready, k + 1)
                    nc.scalar.activation(lg[:, :, :], lg[:, :, :], ACT.Exp).then_inc(e_ready, 1)
                else:
                    a.wait_ge(l_done, k + 1)
                    nc.scalar.activation(lg[:, :, :], lb[:, 0:TPG * E].rearrange("p (t e) -> p t e", t=TPG),
                                         ACT.Sigmoid).then_inc(e_ready, 1)
                a.wait_ge(rows_free, k + 1)
                nc.scalar.activation(row[u][:, :, 0:D], fr.xn[u][:, :, :], ACT.Copy).then_inc(row_ready, 1)
                if shared:
                    sh.act(a, k)

            ahead(a, GROUPS, 2, lambda i, u, k: fr.act(a, k, u), body)

        @block.tensor
        def _(pe):
            pe.wait_ge(weights, 16 * len(loads))
            pe.wait_ge(consts, 2)

            def body(i, u, k):
                pe.wait_ge(fr.xnT_ready, k + 1)
                if not first(k):
                    pe.wait_ge(e_ready, k)
                for t in range(TPG):
                    m = nc.tensor.matmul(lb[:, t * E:(t + 1) * E], fr.xnT[u][:, t * P:(t + 1) * P], wg[:, :],
                                         start=True, stop=True)
                m.then_inc(l_done, 1)
                if shared:
                    for f in range(2):
                        sh.pe_hidden(pe, k, fr.xnT[u], f)
                pe.wait_ge(masked, k + 1)
                if not first(k):
                    pe.wait_ge(cum_ready, k)
                    pe.wait_ge(sent_ready, 2 * k)
                for t in range(TPG):
                    o = rb[:, t * E:(t + 1) * E]
                    nc.tensor.matmul(o, c.ones_b[:, :], cum[u][:, :], start=True, stop=False)
                    for b in range(t):
                        nc.tensor.matmul(o, c.ones_b[:, :], mask[:, b, :], start=False, stop=False)
                    m = nc.tensor.matmul(o, c.below_b[:, :], mask[:, t, :], start=False, stop=True)
                m.then_inc(ranked, 1)
                if shared:
                    sh.pe_hidden(pe, k, fr.xnT[u], 2)
                    pe.wait_ge(sh.gT_ready, 3 * (k + 1) + 2)
                    pe.wait_ge(sh.o_free, k + 1)
                    for t in range(TPG):
                        for f in range(3):
                            m = nc.tensor.matmul(sh.ob[:, t * D:(t + 1) * D], sh.gT[:, f, t * P:(t + 1) * P],
                                                 sw2[:, f, :], start=(f == 0), stop=(f == 2))
                    m.then_inc(sh.o_done, 1)

            ahead(pe, GROUPS, 2, lambda i, u, k: fr.pe(pe, k, u), body)


def experts(nc, c, name, w, rows, tables, w1d, w2d, E, C1, KC, A, gated):
    with Phase(nc, name) as ph:
        R = D + E + 1
        S, U = A * SUB, 4
        units = SLOTS // S
        PER = units // E
        assert PER in (1, U)
        w1 = [ph.sb(f"w1_{i}", [P, C1 * P]) for i in range(U)]
        w2 = [ph.sb(f"w2_{i}", [P, KC, D]) for i in range(U)]
        row = [ph.sb(f"row{i}", [SUB, A, R]) for i in range(U)]
        xeT = [ph.sb(f"xeT{i}", [P, S]) for i in range(2)]
        sT = [ph.sb(f"sT{i}", [P, KC * S]) for i in range(2)]
        gT = [ph.sb(f"gT{i}", [P, KC * S]) for i in range(2)]
        y = [ph.sb(f"y{i}", [SUB, A, D]) for i in range(2)]
        idx = [ph.sb(f"idx{i}", [SUB, A], U32) for i in range(2)]
        xb = ph.bank("x")
        hb = [[ph.bank(f"h{i}{j}") for j in range(2)] for i in range(2)]
        ob = [ph.bank(f"o{i}") for i in range(2)]
        loaded = [ph.sem(f"loaded{i}") for i in range(U)]
        added = [ph.sem(f"added{i}") for i in range(2)]
        turned, xe_ready, h_done, s_ready, g_ready, o_done, y_ready, idx_ready = (
            ph.sem(s) for s in ("turned", "xe_ready", "h_done", "s_ready", "g_ready", "o_done", "y_ready", "idx_ready"))
        block = ph.block()

        def expert(i, u):
            return U * i + u if PER == 1 else i

        def use(i, u):
            return i + 1

        @block.sync
        def _(sp):
            def load(i, u):
                n, p = U * i + u, u % U
                if not isinstance(n, int) or n >= U:
                    sp.wait_ge(y_ready, n - U + 1)
                e = expert(i, u)
                for dst, src in ((row[p][:, :, :], rows[bass.ds(S * n, S), :].rearrange("(a p) r -> p a r", p=SUB)),
                                 (w1[p][:, :], w1d[bass.ds(e, 1), :, :].rearrange("a p f -> (a p) f")),
                                 (w2[p][:, :, :], w2d[bass.ds(e, 1), :, :, :].rearrange("a p c d -> (a p) c d"))):
                    sp.dma_start(dst, src).then_inc(loaded[p], 16)

            for u in range(U):
                load(0, u)
            with sp.Fori(1, units // U) as i:
                for u in range(U):
                    load(i, u)

        @block.tensor
        def _(pe):
            def turn(i, u, n):
                pe.wait_ge(loaded[u % U], 48 * use(i, u))
                if not first(n):
                    pe.wait_ge(xe_ready, n)
                for a in range(A):
                    m = nc.tensor.transpose(xb[:, a * SUB:(a + 1) * SUB], row[u % U][:, a, 0:D], c.ident[0:SUB, 0:SUB])
                m.then_inc(turned, 1)

            def hidden(i, u, n):
                p = u % 2
                pe.wait_ge(xe_ready, n + 1)
                for f in range(C1):
                    o = hb[p][f // 3][:, (f % 3) * S:(f % 3 + 1) * S] if gated else hb[p][f][:, 0:S]
                    m = nc.tensor.matmul(o, w1[u % U][:, f * P:(f + 1) * P], xeT[p][:, :], start=True, stop=True)
                m.then_inc(h_done, 1)

            def output(i, u, n):
                p = u % 2
                pe.wait_ge(g_ready, n + 1)
                if not isinstance(n, int) or n >= 2:
                    pe.wait_ge(y_ready, n - 1)
                for a in range(A):
                    for f in range(KC):
                        m = nc.tensor.matmul(ob[p][0:SUB, a * D:(a + 1) * D],
                                             gT[p][:, f * S + a * SUB:f * S + (a + 1) * SUB],
                                             w2[u % U][:, f, :], start=(f == 0), stop=(f == KC - 1))
                m.then_inc(o_done, 1)

            def step(at):
                if at(1):
                    hidden(*at(1))
                if at(2):
                    turn(*at(2))
                output(*at(0))

            turn(0, 0, 0)
            hidden(0, 0, 0)
            turn(0, 1, 1)
            stream(pe, units, U, step)

        @block.scalar
        def _(a_):
            def copy(i, u, n):
                a_.wait_ge(turned, n + 1)
                nc.scalar.activation(xeT[u % 2][:, :], xb[:, 0:S], ACT.Copy).then_inc(xe_ready, 1)

            def bend(i, u, n):
                p = u % 2
                a_.wait_ge(h_done, n + 1)
                if gated:
                    nc.scalar.activation(sT[p][:, :], hb[p][1][:, 0:KC * S], ACT.Silu).then_inc(s_ready, 1)
                else:
                    for f in range(KC):
                        m = nc.scalar.activation(gT[p][:, f * S:(f + 1) * S], hb[p][f][:, 0:S], ACT.Gelu)
                    m.then_inc(g_ready, 1)

            def step(at):
                bend(*at(0))
                if at(2):
                    copy(*at(2))

            copy(0, 0, 0)
            copy(0, 1, 1)
            stream(a_, units, U, step)

        @block.vector
        def _(v):
            def step(at):
                i, u, n = at(0)
                p = u % 2
                if gated:
                    v.wait_ge(s_ready, n + 1)
                    nc.vector.tensor_tensor(gT[p][:, :], hb[p][0][:, 0:KC * S], sT[p][:, :], ALU.mult).then_inc(g_ready, 1)
                if not isinstance(n, int) or n >= 2:
                    v.wait_ge(added[p], 16 * A * ((U // 2) * i + u // 2))
                v.wait_ge(loaded[u % U], 48 * use(i, u))
                nc.vector.tensor_copy(idx[p][:, :], row[u % U][:, :, R - 1]).then_inc(idx_ready, 1)
                v.wait_ge(o_done, n + 1)
                nc.vector.tensor_tensor(y[p][:, :, :], ob[p][0:SUB, 0:A * D].rearrange("p (a d) -> p a d", a=A),
                                        row[u % U][:, :, bass.ds(D + expert(i, u), 1)].to_broadcast([SUB, A, D]),
                                        ALU.mult).then_inc(y_ready, 1)

            stream(v, units, U, step)

        @block.gpsimd
        def _(g):
            def step(at):
                i, u, n = at(0)
                p = u % 2
                hold(g, c.mark_g, idx_ready, n + 1)
                hold(g, c.mark_g, y_ready, n + 1)
                for a in range(A):
                    g.indirect_dma_start(out=tables[p], out_offset=bass.IndirectOffsetOnAxis(
                        ap=idx[p][:, a:a + 1], axis=0), in_=y[p][:, a, :], in_offset=None,
                        bounds_check=TOKENS + DUMPS * SUB - 1, oob_is_err=True, compute_op=ALU.add).then_inc(added[p], 16)

            stream(g, units, U, step)
            for p in range(2):
                g.wait_ge(added[p], 16 * (units * A // 2))


def combine(nc, c, name, tables, source=None, norm=None, w=None):
    with Phase(nc, name) as ph:
        acc = [ph.sb(f"acc{i}", [P, TABLES, GT]) for i in range(2)]
        s01, out = [ph.sb(f"s01{i}", [P, GT]) for i in range(2)], ph.sb("out", [P, GT])
        loaded = [ph.sem(f"loaded{i}") for i in range(2)]
        steps, free, weights, squared, scaled, applied = (
            ph.sem(s) for s in ("steps", "free", "weights", "squared", "scaled", "applied"))
        if source is not None:
            nw = ph.sb("nw", [P, D])
            sq, ss = [ph.sb(f"sq{i}", [P, TPG, D]) for i in range(2)], [
                ph.sb(f"ss{i}", [P, TPG]) for i in range(2)]
            rms = [Rsqrt(ph, c, f"rms{i}", TPG) for i in range(2)]
        block = ph.block()

        @block.sync
        def _(sp):
            if source is not None:
                sp.dma_start(nw[:, :], w[norm][0, :].partition_broadcast(P)).then_inc(weights, 16)

            def load(i, u):
                k = 2 * i + u
                if not isinstance(k, int) or k >= 2:
                    sp.wait_ge(free, k - 1)
                for t in range(TABLES):
                    sp.dma_start(acc[u][:, t, :].rearrange("p (t d) -> p t d", t=TPG),
                                 tables[t][bass.ds(GT * k, GT), :].rearrange("(t p) d -> p t d", p=P)
                                 ).then_inc(loaded[u], 16)

            for u in range(2):
                load(0, u)
            with sp.Fori(1, GROUPS // 2) as i:
                for u in range(2):
                    load(i, u)

        @block.scalar
        def _(a):
            clear_next(c, a)

            def body(i, u, k):
                a.wait_ge(steps, k + 1)
                for t in range(TPG):
                    m = nc.scalar.activation(sq[u][:, t, :], s01[u][:, t * D:(t + 1) * D], ACT.Square,
                                             accum_out=ss[u][:, t:t + 1])
                m.then_inc(squared, 1)

            if source is not None:
                each(a, GROUPS, 2, body)

        if source is not None:
            @block.gpsimd
            def _(g):
                each(g, GROUPS, 2, lambda i, u, k: rms[u].pool(g, i))

        @block.vector
        def _(v):
            if source is not None:
                v.wait_ge(weights, 16)

            def sums(i, u, k):
                if not isinstance(k, int) or k >= 2:
                    v.wait_ge(applied if source is None else scaled, k - 1)
                v.wait_ge(loaded[u], 16 * TABLES * (i + 1))
                nc.vector.tensor_tensor(s01[u][:, :], acc[u][:, 0, :], acc[u][:, 1, :], ALU.add).then_inc(free, 1)
                v.wait_ge(free, k + 1)
                if source is not None:
                    s3 = s01[u][:, :].rearrange("p (t d) -> p t d", t=TPG)
                    nc.vector.tensor_tensor(s3, s3, tiles4(source, k), ALU.add).then_inc(steps, 1)

            def body(i, u, k):
                s3 = s01[u][:, :].rearrange("p (t d) -> p t d", t=TPG)
                xt = tiles4(c.x, k)
                if source is None:
                    nc.vector.scalar_tensor_tensor(out=xt, in0=s3, scalar=0.5, in1=xt, op0=ALU.mult, op1=ALU.add
                                                   ).then_inc(applied, 1)
                    return
                v.wait_ge(rms[u].solved, i + 1)
                out3 = out[:, :].rearrange("p (t d) -> p t d", t=TPG)
                if not first(k):
                    v.wait_ge(applied, k)
                for t in range(TPG):
                    m = nc.vector.scalar_tensor_tensor(out=out3[:, t, :], in0=s3[:, t, :], scalar=rms[u].y[:, t:t + 1],
                                                       in1=nw[:, :], op0=ALU.mult, op1=ALU.mult)
                m.then_inc(scaled, 1)
                v.wait_ge(scaled, k + 1)
                nc.vector.scalar_tensor_tensor(out=xt, in0=out3, scalar=0.5, in1=xt, op0=ALU.mult, op1=ALU.add
                                               ).then_inc(applied, 1)

            def root(i, u, k):
                if source is not None:
                    v.wait_ge(squared, k + 1)
                    rms[u].dve(v, ss[u][:, :], i, 1.0 / D, RMS_EPS)

            def step(at):
                if at(1):
                    root(*at(1))
                body(*at(0))
                if at(2):
                    sums(*at(2))

            sums(0, 0, 0)
            sums(0, 1, 1)
            root(0, 0, 0)
            stream(v, GROUPS, 2, step)


def moe64(nc, c, name, w):
    m = c.mixtures[name]
    route(nc, c, name + "r", w, c.x, m, "L0_ffn_wg", 64, 8, 160, "softmax", shared=True)
    experts(nc, c, name + "e", w, m.rows, m.tables, w["L0_ffn_expert_w1"], w["L0_ffn_expert_w2"], 64, 6, 3, 2, True)
    combine(nc, c, name + "c", m.tables)


def gqa_moe(nc, c, name, w):
    m = c.mixtures[name]
    with ExitStack() as ctx:
        src = ctx.enter_context(nc.sbuf_tensor(name + "_src", [P, TILES, D], F32))
        grouped_attention(nc, c, name + "a", w, src)
        route(nc, c, name + "r", w, src, m, "L3_ffn_gate_w", 8, 2, 1280, "sigmoid")
        experts(nc, c, name + "e", w, m.rows, m.tables, w["L3_ffn_w1"], w["L3_ffn_w2"], 8, 2, 2, 4, False)
        combine(nc, c, name + "c", m.tables, source=src, norm="L3_ffn_norm2_w", w=w)


def grouped_attention(nc, c, name, w, src):
    with Phase(nc, name) as ph:
        wq, wk, wv, wo = (ph.sb(s, [P, D]) for s in ("wq", "wk", "wv", "wo"))
        bq, bqs, bk = ph.sb("bq", [P, 1]), ph.sb("bqs", [P, 1]), ph.sb("bk", [P, 1])
        bv, bo, nw = ph.sb("bv", [1, D]), ph.sb("bo", [1, D]), ph.sb("nw", [P, D])
        at = FullAttention(ph, c, wq, wk, wv, wo, bq=bqs, bk=bk, bv=bv, bo=bo)
        fr = at.fr
        sg = [ph.sb(f"sg{i}", [P, TPG, D]) for i in range(2)]
        sq, ss = ph.sb("sq", [P, TPG, D]), ph.sb("ss", [P, TPG])
        rms = Rsqrt(ph, c, "rms", TPG)
        weights, ready, sg_ready, squared = ph.sem("weights"), ph.sem("ready"), ph.sem("sg_ready"), ph.sem("squared")
        block = ph.block()

        @block.sync
        def _(sp):
            for dst, s in ((wq, "qw"), (wk, "kw"), (wv, "vw"), (wo, "ow"), (bq, "qb"), (bk, "kb"), (bv, "vb"),
                           (bo, "ob")):
                sp.dma_start(dst[:], w["L3_ffn_" + s]).then_inc(weights, 16)
            sp.dma_start(nw[:, :], w["L3_ffn_norm1_w"][0, :].partition_broadcast(P)).then_inc(weights, 16)
            sp.wait_ge(weights, 144)

        @block.gpsimd
        def _(g):
            at.pool_setup(g)
            fr.pool(g, 0)

            def group(now, nxt):
                if not first(now[2]):
                    rms.pool(g, now[2] - 1)
                if nxt:
                    fr.pool(g, nxt[2])

            weave(g, GROUPS, 2, group)
            rms.pool(g, GROUPS - 1)

        @block.vector
        def _(v):
            v.wait_ge(weights, 144)
            nc.vector.tensor_scalar(bqs[:, :], bq[:, :], at.DK ** -0.5, None, ALU.mult).then_inc(ready, 1)
            v.wait_ge(at.made, at.MADE)
            at.dve_start(v)

            def finish(tile, o):
                u, k, t, n = tile
                nc.vector.tensor_tensor(sg[u][:, t, :], o, fr.xn[u][:, t, :], ALU.add).then_inc(at.o_free, 1)

            def root(k):
                v.wait_ge(squared, k + 1)
                rms.dve(v, ss[:, :], k, 1.0 / D, RMS_EPS)

            def scale(u, k):
                v.wait_ge(rms.solved, k + 1)
                for t in range(TPG):
                    nc.vector.scalar_tensor_tensor(out=src[:, bass.ds(TPG * k + t, 1), :], in0=sg[u][:, t:t + 1, :],
                                                   scalar=rms.y[:, t:t + 1], in1=nw[:, :].unsqueeze(1),
                                                   op0=ALU.mult, op1=ALU.mult)

            def group(now, nxt):
                def between(s):
                    if not first(now[2]):
                        if s == 8:
                            root(now[2] - 1)
                        if s == 12:
                            scale(1 - now[1], now[2] - 1)

                at.dve(v, now, nxt, finish, between)

            weave(v, GROUPS, 2, group)
            at.dve_end(v, finish)
            root(GROUPS - 1)
            scale(1, GROUPS - 1)

        @block.scalar
        def _(a):
            a.wait_ge(ready, 1)
            at.act_start(a)

            def squares(u, k):
                a.wait_ge(at.o_free, TPG * (k + 1))
                for t in range(TPG):
                    m = nc.scalar.activation(sq[:, t, :], sg[u][:, t, :], ACT.Square, accum_out=ss[:, t:t + 1])
                m.then_inc(squared, 1)

            def group(now, nxt):
                at.act(a, now, nxt,
                       lambda s: squares(1 - now[1], now[2] - 1) if s == 7 and not first(now[2]) else None)

            weave(a, GROUPS, 2, group)
            squares(1, GROUPS - 1)

        @block.tensor
        def _(pe):
            pe.wait_ge(weights, 144)
            at.pe_start(pe)
            weave(pe, GROUPS, 2, lambda now, nxt: at.pe(pe, now, nxt))
            at.pe_end(pe)


def s4d(nc, c, name, w):
    W = 383
    kz = nc.dram_tensor(f"{name}_kernel", (D, W), F32, kind="Internal").ap()
    s4d_kernel(nc, c, name + "k", w, kz)
    with ExitStack() as ctx:
        u_all = ctx.enter_context(nc.sbuf_tensor(name + "_u", [P, D, TILES], F32))
        y_all = ctx.enter_context(nc.sbuf_tensor(name + "_y", [P, TILES, D], F32))
        s4d_input(nc, c, name + "i", w, u_all)
        s4d_conv(nc, c, name + "t", kz, W, u_all, y_all)
        s4d_output(nc, c, name + "o", w, y_all)


def s4d_kernel(nc, c, name, w, kz):
    with Phase(nc, name) as ph:
        N, M = 32, 32
        PI = 3.141592653589793
        C1 = 6.28125
        C2 = 4058 * 2.0 ** -21
        C3 = 2 * PI - C1 - C2
        MAGIC = 1.5 * 2.0 ** 23
        ldt, cc_, lar, ai, dsk = (ph.sb(n, s) for n, s in (
            ("ldt", [P, 1]), ("cc", [P, 2, N]), ("lar", [P, N]), ("ai", [P, N]), ("dsk", [P, 1])))
        mi, mf = ph.sb("mi", [P, M], I32), ph.sb("mf", [P, M])
        dt, ar = ph.sb("dt", [P, 1]), ph.sb("ar", [P, N])
        dr, di = ph.sb("dr", [P, N]), ph.sb("di", [P, N])
        argr, argi, turns, mag, sn, cs = (ph.sb(n, [P, N, M]) for n in ("argr", "argi", "turns", "mag", "sn", "cs"))
        nr, ni, tr, ti, den, t0, cr, ci = (ph.sb(n, [P, N]) for n in ("nr", "ni", "tr", "ti", "den", "t0", "cr", "ci"))
        pr, pi, pt = (ph.sb(n, [P, N, 16]) for n in ("pr", "pi", "pt"))
        big, big2 = ph.sb("big", [P, N, 256]), ph.sb("big2", [P, N, 256])
        kk = ph.sb("kk", [P, W_KZ])
        loaded, placed, step, to_act, from_act, stored = (
            ph.sem(s) for s in ("loaded", "placed", "step", "to_act", "from_act", "stored"))
        block = ph.block()

        @block.sync
        def _(sp):
            for dst, src in ((ldt, "log_dt"), (cc_, "C"), (lar, "log_A_real"), (ai, "A_imag"), (dsk, "D_skip")):
                sp.dma_start(dst[:], w["L1_attn_" + src]).then_inc(loaded, 16)
            sp.wait_ge(to_act, 4)
            sp.dma_start(kz, kk[:, :]).then_inc(stored, 16)
            sp.wait_ge(stored, 16)

        @block.gpsimd
        def _(g):
            nc.gpsimd.iota(mi[:, 0:16], pattern=[[1, 16]], base=0, channel_multiplier=0).then_inc(placed, 1)
            nc.gpsimd.iota(mi[:, 16:32], pattern=[[16, 16]], base=0, channel_multiplier=0).then_inc(placed, 1)

        @block.scalar
        def _(a):
            a.wait_ge(loaded, 80)
            nc.scalar.activation(dt[:, :], ldt[:, :], ACT.Exp).then_inc(from_act, 1)
            nc.scalar.activation(ar[:, :], lar[:, :], ACT.Exp).then_inc(from_act, 1)
            a.wait_ge(to_act, 1)
            nc.scalar.activation(mag[:, :, :], argr[:, :, :], ACT.Exp).then_inc(from_act, 1)
            a.wait_ge(to_act, 2)
            nc.scalar.activation(sn[:, :, :], argi[:, :, :], ACT.Sin).then_inc(from_act, 1)
            a.wait_ge(to_act, 3)
            nc.scalar.activation(cs[:, :, :], turns[:, :, :], ACT.Sin).then_inc(from_act, 1)

        @block.vector
        def _(v):
            done = [0]

            def link(ins):
                done[0] += 1
                ins.then_inc(step, 1)
                v.wait_ge(step, done[0])

            V = nc.vector

            def tt(o, a, b, op):
                link(V.tensor_tensor(o, a, b, op))

            v.wait_ge(placed, 2)
            link(V.tensor_copy(mf[:, :], mi[:, :]))
            link(V.memset(kk[:, 0:127], 0.0))
            v.wait_ge(from_act, 2)
            link(V.tensor_scalar(ar[:, :], ar[:, :], -1.0, None, ALU.mult))
            link(V.tensor_scalar(dr[:, :], ar[:, :], dt[:, 0:1], None, ALU.mult))
            link(V.tensor_scalar(di[:, :], ai[:, :], dt[:, 0:1], None, ALU.mult))
            mb = mf[:, :].unsqueeze(1).to_broadcast([P, N, M])
            V.tensor_tensor(argr[:, :, :], dr[:, :].unsqueeze(2).to_broadcast([P, N, M]), mb, ALU.mult).then_inc(to_act, 1)
            tt(argi[:, :, :], di[:, :].unsqueeze(2).to_broadcast([P, N, M]), mb, ALU.mult)
            link(V.tensor_scalar(turns[:, :, :], argi[:, :, :], 1.0 / (2 * PI), MAGIC, ALU.mult, ALU.add))
            link(V.tensor_scalar(turns[:, :, :], turns[:, :, :], -MAGIC, None, ALU.add))
            for part in (C1, C2, C3):
                link(V.scalar_tensor_tensor(out=argi[:, :, :], in0=turns[:, :, :], scalar=-part, in1=argi[:, :, :],
                                            op0=ALU.mult, op1=ALU.add))
            V.tensor_scalar(argi[:, :, :], argi[:, :, :], 3.1415925, -3.1415925, ALU.min, ALU.max).then_inc(to_act, 1)
            v.wait_ge(to_act, 2)
            link(V.scalar_tensor_tensor(out=turns[:, :, :], in0=argi[:, :, :], scalar=-1.0, in1=argi[:, :, :],
                                        op0=ALU.mult, op1=ALU.min))
            V.tensor_scalar(turns[:, :, :], turns[:, :, :], PI / 2, None, ALU.add).then_inc(to_act, 1)
            v.wait_ge(from_act, 5)
            tt(sn[:, :, :], sn[:, :, :], mag[:, :, :], ALU.mult)
            tt(cs[:, :, :], cs[:, :, :], mag[:, :, :], ALU.mult)
            link(V.tensor_scalar(nr[:, :], cs[:, :, 1], -1.0, None, ALU.add))
            link(V.tensor_copy(ni[:, :], sn[:, :, 1]))
            c_r, c_i = cc_[:, 0, :], cc_[:, 1, :]
            tt(tr[:, :], c_r, nr[:, :], ALU.mult)
            tt(t0[:, :], c_i, ni[:, :], ALU.mult)
            tt(tr[:, :], tr[:, :], t0[:, :], ALU.subtract)
            tt(ti[:, :], c_r, ni[:, :], ALU.mult)
            tt(t0[:, :], c_i, nr[:, :], ALU.mult)
            tt(ti[:, :], ti[:, :], t0[:, :], ALU.add)
            tt(den[:, :], ar[:, :], ar[:, :], ALU.mult)
            tt(t0[:, :], ai[:, :], ai[:, :], ALU.mult)
            tt(den[:, :], den[:, :], t0[:, :], ALU.add)
            link(V.reciprocal(den[:, :], den[:, :]))
            tt(cr[:, :], tr[:, :], ar[:, :], ALU.mult)
            tt(t0[:, :], ti[:, :], ai[:, :], ALU.mult)
            tt(cr[:, :], cr[:, :], t0[:, :], ALU.add)
            tt(ci[:, :], ti[:, :], ar[:, :], ALU.mult)
            tt(t0[:, :], tr[:, :], ai[:, :], ALU.mult)
            tt(ci[:, :], ci[:, :], t0[:, :], ALU.subtract)
            tt(cr[:, :], cr[:, :], den[:, :], ALU.mult)
            tt(ci[:, :], ci[:, :], den[:, :], ALU.mult)
            def b16(a):
                return a.unsqueeze(2).to_broadcast([P, N, 16])

            er, ei = cs[:, :, 16:32], sn[:, :, 16:32]
            tt(pr[:, :, :], er, b16(cr[:, :]), ALU.mult)
            tt(pt[:, :, :], ei, b16(ci[:, :]), ALU.mult)
            tt(pr[:, :, :], pr[:, :, :], pt[:, :, :], ALU.subtract)
            tt(pi[:, :, :], er, b16(ci[:, :]), ALU.mult)
            tt(pt[:, :, :], ei, b16(cr[:, :]), ALU.mult)
            tt(pi[:, :, :], pi[:, :, :], pt[:, :, :], ALU.add)

            def outer(o, p_, q_):
                tt(o[:, :, :].rearrange("p n (a b) -> p n a b", a=16),
                   p_[:, :, :].unsqueeze(3).to_broadcast([P, N, 16, 16]),
                   q_[:, :, 0:16].unsqueeze(2).to_broadcast([P, N, 16, 16]), ALU.mult)

            outer(big, pr, cs)
            outer(big2, pi, sn)
            tt(big[:, :, :], big[:, :, :], big2[:, :, :], ALU.subtract)
            link(V.tensor_reduce(kk[:, 127:W_KZ], big[:, :, :].rearrange("p n l -> p l n"), AX_X, ALU.add))
            link(V.tensor_scalar(kk[:, 127:W_KZ], kk[:, 127:W_KZ], 2.0, None, ALU.mult))
            V.tensor_tensor(kk[:, 127:128], kk[:, 127:128], dsk[:, :], ALU.add).then_inc(to_act, 1)


W_KZ = 383


def s4d_input(nc, c, name, w, u_all):
    with Phase(nc, name) as ph:
        win, bin_ = ph.sb("win", [P, D]), ph.sb("bin", [1, D])
        fr = Front(ph, c, c.x, perm=c.mirror, at_once=True)
        ub = ph.bank("u")
        weights, u_done, u_ready, x_ready = (ph.sem(s) for s in ("weights", "u_done", "u_ready", "x_ready"))
        block = ph.block()

        @block.sync
        def _(sp):
            sp.dma_start(win[:, :], w["L1_attn_in_W"]).then_inc(weights, 16)
            sp.dma_start(bin_[:, :], w["L1_attn_in_b"]).then_inc(weights, 16)
            sp.wait_ge(weights, 32)

        @block.gpsimd
        def _(g):
            fr.pool_start(g)

        @block.vector
        def _(v):
            fr.dve_start(v)

            def body(i, u, k):
                v.wait_ge(fr.rows_ready, TPG * (k + 1))
                xt = tiles4(c.x, k)
                nc.vector.tensor_tensor(xt, xt, fr.xn[u][:, :, :], ALU.add).then_inc(x_ready, 1)
                v.wait_ge(x_ready, k + 1)

            ahead(v, GROUPS, 2, lambda i, u, k: fr.dve(v, k, u), body)

        @block.scalar
        def _(a):
            def body(i, u, k):
                hold(a, c.mark_a, u_done, k + 1)
                nc.scalar.activation(u_all[:, :, bass.ds(TPG * k, TPG)],
                                     ub[:, :].rearrange("p (t d) -> p d t", t=TPG), ACT.Copy).then_inc(u_ready, 1)

            ahead(a, GROUPS, 2, lambda i, u, k: fr.act(a, k, u), body)

        @block.tensor
        def _(pe):
            pe.wait_ge(weights, 32)

            def body(i, u, k):
                pe.wait_ge(fr.xnT_ready, k + 1)
                if not first(k):
                    pe.wait_ge(u_ready, k)
                for t in range(TPG):
                    o = ub[:, t * D:(t + 1) * D]
                    nc.tensor.matmul(o, c.ones[0:1, :], bin_[:, :], start=True, stop=False)
                    m = nc.tensor.matmul(o, fr.xnT[u][:, t * P:(t + 1) * P], win[:, :], start=False, stop=True)
                m.then_inc(u_done, 1)

            ahead(pe, GROUPS, 2, lambda i, u, k: fr.pe(pe, k, u), body)


def s4d_conv(nc, c, name, kz, W, u_all, y_all):
    with Phase(nc, name) as ph:
        CH = 8
        top = [ph.sb(f"top{i}", [P, CH, SEQ]) for i in range(2)]
        yb = [ph.bank(f"y{i}") for i in range(2)]
        loaded = [ph.sem(f"loaded{i}") for i in range(2)]
        y_done, y_ready = ph.sem("y_done"), ph.sem("y_ready")
        block = ph.block()
        STEPS = D // CH

        @block.sync
        def _(sp):
            def load(i, u):
                s = 2 * i + u
                if not isinstance(s, int) or s >= 2:
                    sp.wait_ge(y_done, s - 1)
                src = kz[bass.ds(CH * s, CH), 0:1]
                src = bass.AP(tensor=src.tensor, offset=src.offset, ap=[[1, P], [W, CH], [1, SEQ]])
                sp.dma_start(top[u][:, :, :], src).then_inc(loaded[u], 16)

            each(sp, STEPS, 2, lambda i, u, s: load(i, u))

        @block.tensor
        def _(pe):
            def body(i, u, s):
                pe.wait_ge(loaded[u], 16 * (i + 1))
                if not first(s) and not (isinstance(s, int) and s < 2):
                    pe.wait_ge(y_ready, s - 1)
                for j in range(CH):
                    o = yb[u][:, TILES * j:TILES * (j + 1)]
                    ch = u_all[:, bass.ds(CH * s + j, 1), :].rearrange("p a t -> p (a t)")
                    nc.tensor.matmul(o, top[u][:, j, 0:P], ch, start=True, stop=False)
                    half = u_all[:, bass.ds(CH * s + j, 1), 0:TILES:2].rearrange("p a t -> p (a t)")
                    m = nc.tensor.matmul(yb[u][:, TILES * j + 1:TILES * (j + 1):2], top[u][:, j, P:SEQ], half,
                                         start=False, stop=True)
                m.then_inc(y_done, 1)

            each(pe, STEPS, 2, body)

        @block.scalar
        def _(a):
            def body(i, u, s):
                hold(a, c.mark_a, y_done, s + 1)
                nc.scalar.activation(y_all[:, :, bass.ds(CH * s, CH)],
                                     yb[u][:, 0:CH * TILES].rearrange("p (c t) -> p t c", c=CH),
                                     ACT.Gelu).then_inc(y_ready, 1)

            each(a, STEPS, 2, body)


def s4d_output(nc, c, name, w, y_all):
    with Phase(nc, name) as ph:
        wg, wo = ph.sb("wg", [P, 2 * D]), ph.sb("wo", [P, D])
        bg, bo = ph.sb("bg", [P, 2]), ph.sb("bo", [1, D])
        sg, vT = ([ph.sb(f"{n}{i}", [P, GT]) for i in range(2)] for n in ("sg", "vT"))
        fr = Front(ph, c, y_all, norm=False)
        zb, ob = [[ph.bank(f"z{i}{j}") for j in range(2)] for i in range(2)], [ph.bank(f"o{i}") for i in range(2)]
        weights, z_done, sg_ready, v_ready, o_done, o_free = (
            ph.sem(s) for s in ("weights", "z_done", "sg_ready", "v_ready", "o_done", "o_free"))
        block = ph.block()

        @block.sync
        def _(sp):
            for dst, src in ((wg, "glu_W"), (wo, "out_W"), (bg, "glu_b"), (bo, "out_b")):
                sp.dma_start(dst[:], w["L1_attn_" + src]).then_inc(weights, 16)
            sp.wait_ge(weights, 64)

        @block.vector
        def _(v):
            v.wait_ge(weights, 64)

            def gate(i, u, k):
                v.wait_ge(sg_ready, k + 1)
                nc.vector.scalar_tensor_tensor(out=vT[u][:, :], in0=zb[u][0][:, :], scalar=bg[:, 0:1], in1=sg[u][:, :],
                                               op0=ALU.add, op1=ALU.mult).then_inc(v_ready, 1)

            def add(i, u, k):
                v.wait_ge(o_done, k + 1)
                xt = tiles4(c.x, k)
                nc.vector.tensor_tensor(xt, xt, ob[u][:, :].rearrange("p (t d) -> p t d", t=TPG), ALU.add
                                        ).then_inc(o_free, 1)

            def step(at):
                if at(2):
                    fr.dve(v, at(2)[2], at(2)[1])
                if at(1):
                    gate(*at(1))
                add(*at(0))

            fr.dve(v, 0, 0)
            fr.dve(v, 1, 1)
            gate(0, 0, 0)
            stream(v, GROUPS, 2, step)

        @block.scalar
        def _(a):
            def gates(i, u, k):
                a.wait_ge(z_done, k + 1)
                nc.scalar.activation(sg[u][:, :], zb[u][1][:, :], ACT.Sigmoid, bias=bg[:, 1:2]).then_inc(sg_ready, 1)

            def step(at):
                if at(1):
                    gates(*at(1))
                if at(2):
                    fr.act(a, at(2)[2], at(2)[1])

            a.wait_ge(weights, 64)
            fr.act(a, 0, 0)
            gates(0, 0, 0)
            fr.act(a, 1, 1)
            stream(a, GROUPS, 2, step)

        @block.tensor
        def _(pe):
            pe.wait_ge(weights, 64)

            def halves(i, u, k):
                pe.wait_ge(fr.xnT_ready, k + 1)
                if not isinstance(k, int) or k >= 2:
                    pe.wait_ge(v_ready, k - 1)
                for j in range(2):
                    m = nc.tensor.matmul(zb[u][j][:, :], wg[:, j * D:(j + 1) * D], fr.xnT[u][:, :], start=True, stop=True)
                m.then_inc(z_done, 1)

            def output(i, u, k):
                pe.wait_ge(v_ready, k + 1)
                if not isinstance(k, int) or k >= 2:
                    pe.wait_ge(o_free, k - 1)
                for t in range(TPG):
                    o = ob[u][:, t * D:(t + 1) * D]
                    nc.tensor.matmul(o, c.ones[0:1, :], bo[:, :], start=True, stop=False)
                    m = nc.tensor.matmul(o, vT[u][:, t * P:(t + 1) * P], wo[:, :], start=False, stop=True)
                m.then_inc(o_done, 1)

            def step(at):
                if at(1):
                    halves(*at(1))
                if at(2):
                    fr.pe(pe, at(2)[2], at(2)[1])
                output(*at(0))

            fr.pe(pe, 0, 0)
            halves(0, 0, 0)
            fr.pe(pe, 1, 1)
            stream(pe, GROUPS, 2, step)


def mamba(nc, c, name, w):
    with ExitStack() as ctx:
        y_all = ctx.enter_context(nc.sbuf_tensor(name + "_y", [P, TILES, D], F32))
        mamba_rows(nc, c, name + "n", y_all)
        mamba_mix(nc, c, name + "m", w, y_all)


def mamba_rows(nc, c, name, y_all):
    with Phase(nc, name) as ph:
        st, mv = ph.sb("st", [P, TILES, 6]), ph.sb("mv", [P, TILES, 2])
        rs = Rsqrt(ph, c, "ln", TILES)
        stats, moments, rows, added = ph.sem("stats"), ph.sem("moments"), ph.sem("rows"), ph.sem("added")
        block = ph.block()

        @block.gpsimd
        def _(g):
            rs.pool(g, 0)

        @block.vector
        def _(v):
            for t in range(TILES):
                nc.vector.bn_stats(st[:, t, :], c.x[:, t, :]).then_inc(stats, 1)
            hold(v, c.mark_v, stats, TILES)
            for t in range(TILES):
                nc.vector.bn_aggr(mv[:, t, :], st[:, t, :]).then_inc(moments, 1)
            v.wait_ge(moments, TILES)
            rs.dve(v, mv[:, :, 1], 0, 1.0, LN_EPS)
            v.wait_ge(rs.solved, 1)
            for t in range(TILES):
                nc.vector.tensor_scalar(y_all[:, t, :], c.x[:, t, :], mv[:, t, 0:1], rs.y[:, t:t + 1], ALU.subtract,
                                        ALU.mult).then_inc(rows, 1)
            v.wait_ge(rows, TILES)
            nc.vector.tensor_tensor(c.x[:, :, :], c.x[:, :, :], y_all[:, :, :], ALU.add).then_inc(added, 1)
            v.wait_ge(added, 1)


def mamba_mix(nc, c, name, w, y_all):
    with Phase(nc, name) as ph:
        CC, N, RK = 2, 16, 8
        SPG = GT // SEQ
        EDGE = 1e30

        def rows_of(n, shape=None, dt=F32):
            return [ph.sb(f"{n}{i}", shape or [P, GT], dt) for i in range(2)]

        win, xpw, dtw, wo = ph.sb("win", [P, 512]), ph.sb("xpw", [P, CC, P]), ph.sb("dtw", [RK, 256]), ph.sb(
            "wo", [P, CC, D])
        lnw, lnb, cw, cb = ph.sb("lnw", [P, 1]), ph.sb("lnb", [P, 1]), ph.sb("cw", [P, CC, 4]), ph.sb("cb", [P, CC])
        dtb, al, dd = ph.sb("dtb", [P, CC]), ph.sb("al", [P, CC, N]), ph.sb("dd", [P, CC])
        self_, sel = ph.sb("self", [P, 2 * N, P]), ph.sb("sel", [P, 2 * N, P], BF16)
        xpad = rows_of("xpad", [P, SPG, SEQ + 3])
        cv, ra, ve, yT = rows_of("cv"), rows_of("ra"), rows_of("ve"), rows_of("yT")
        zs, xs, dl, du = ([rows_of(f"{n}{j}") for j in range(CC)] for n in ("zs", "xs", "dl", "du"))
        dA, db, hh, hc = ([rows_of(f"{n}{j}") for j in range(CC)] for n in ("dA", "db", "hh", "hc"))
        bs = rows_of("bs")
        dbc, rest, parts = ph.sb("dbc", [P, GT]), ph.sb("rest", [P, GT]), rows_of("parts", None, BF16)
        mb, ob = ph.bank("misc"), ph.bank("out")
        banks = (mb, ob)
        fr = Front(ph, c, y_all, scale=lnw[:, 0:1], bias=lnb[:, 0:1], bank=mb, at_once=True)
        bb, cbk = [ph.bank(f"b{i}") for i in range(2)], [ph.bank(f"c{i}") for i in range(2)]
        yb = [ph.bank(f"y{i}") for i in range(CC)]
        (weights, made, ready, xz_done, xz_read, conv, silu_z, xs_ready, dbc_done, dbc_ready, dt_done, dt_read) = (
            ph.sem(s) for s in ("weights", "made", "ready", "xz_done", "xz_read", "conv", "silu_z", "xs_ready",
                                "dbc_done", "dbc_ready", "dt_done", "dt_read"))
        (exped, soft, split, parts_ready, dl_ready, du_ready, edge, b_done, bs_ready, dA_ready, db0_ready,
         db1_ready) = (ph.sem(s) for s in ("exped", "soft", "split", "parts_ready", "dl_ready", "du_ready", "edge",
                                           "b_done", "bs_ready", "dA_ready", "db0_ready", "db1_ready"))
        h_ready, hc_ready, summed, yy, y_ready, o_done, o_free = (
            ph.sem(s) for s in ("h_ready", "hc_ready", "summed", "yy", "y_ready", "o_done", "o_free"))
        rest_ready, c_done = ph.sem("rest_ready"), ph.sem("c_done")
        block = ph.block()

        def after(s, now, nxt):
            n = N * now[2] + s + 1
            if s + 1 < N:
                return now[1], now[2], s + 1, n
            return None if nxt is None else (nxt[1], nxt[2], s + 1 - N, n)

        def early(n, depth):
            return isinstance(n, int) and n < depth

        @block.sync
        def _(sp):
            for dst, src in ((win, "in_proj_w"), (xpw, "x_proj_w"), (dtw, "dt_proj_w"), (wo, "out_proj_w"),
                             (lnw, "ln_w"), (lnb, "ln_b"), (cw, "conv_w"), (cb, "conv_b"), (dtb, "dt_proj_b"),
                             (al, "A_log"), (dd, "D")):
                sp.dma_start(dst[:], w["L3_attn_" + src]).then_inc(weights, 16)
            sp.wait_ge(weights, 176)

        @block.gpsimd
        def _(g):
            G = nc.gpsimd
            G.memset(self_[:, :, :], 0.0).then_inc(made, 1)
            for i in range(CC):
                G.memset(xpad[i][:, :, 0:3], 0.0).then_inc(made, 1)
            g.wait_ge(made, 3)
            for q in range(1, 4):
                G.affine_select(out=self_[:, :, :], in_=self_[:, :, :], compare_op=ALU.not_equal, fill=1.0,
                                base=-32 * q, pattern=[[-1, 2 * N], [0, P]], channel_multiplier=1).then_inc(made, 1)
                g.wait_ge(made, 3 + q)

            def split_rows(u, k, q):
                if q == 0:
                    hold(g, c.mark_g, dbc_ready, k + 1)
                    G.tensor_copy(parts[u][:, :], dbc[:, :]).then_inc(split, 1)
                    g.wait_ge(split, 2 * k + 1)
                    G.tensor_tensor(rest[:, :], dbc[:, :], parts[u][:, :], ALU.subtract).then_inc(rest_ready, 1)
                else:
                    g.wait_ge(split, 2 * k + 2)
                    G.tensor_tensor(rest[:, :], rest[:, :], parts[u][:, :], ALU.subtract).then_inc(rest_ready, 1)

            def step_sizes(u, k):
                for j in range(CC):
                    g.wait_ge(soft, CC * k + j + 1)
                    G.tensor_tensor(dl[j][u][:, :], ra[j][:, :], ve[j][:, :], ALU.add).then_inc(dl_ready, 1)
                for j in range(CC):
                    g.wait_ge(dl_ready, CC * k + j + 1)
                    G.tensor_tensor(du[j][u][:, :], dl[j][u][:, :], xs[j][u][:, :], ALU.mult).then_inc(du_ready, 1)
                for j in range(CC):
                    hold(g, c.mark_g, du_ready, CC * k + j + 1)
                    G.memset(dl[j][u][:, SEQ:SEQ + 1], EDGE).then_inc(edge, 1)

            def inputs(u, k, s, n):
                if not early(n, 2):
                    g.wait_ge(h_ready, 2 * n - 2)
                g.wait_ge(bs_ready, n + 1)
                G.tensor_tensor(db[1][s % 2][:, :], du[1][u][:, :], bs[s % 2][:, :], ALU.mult).then_inc(db1_ready, 1)

            def gate_output(u, k):
                for j in range(CC):
                    g.wait_ge(yy, CC * k + j + 1)
                    G.tensor_tensor(yT[j][:, :], yT[j][:, :], zs[j][u][:, :], ALU.mult).then_inc(y_ready, 1)

            def group(now, nxt):
                for s in range(N):
                    nx = after(s, now, nxt)
                    if nx:
                        inputs(*nx)
                    if s == 0 and not first(now[2]):
                        gate_output(1 - now[1], now[2] - 1)
                    if s in (10, 12) and nxt:
                        split_rows(nxt[1], nxt[2], (s - 10) // 2)
                    if s == 13 and nxt:
                        step_sizes(nxt[1], nxt[2])

            fr.pool_start(g)
            split_rows(0, 0, 0)
            split_rows(0, 0, 1)
            step_sizes(0, 0)
            inputs(0, 0, 0, 0)
            weave(g, GROUPS, 2, group)
            gate_output(1, GROUPS - 1)

        @block.scalar
        def _(a):
            A = nc.scalar
            a.wait_ge(weights, 176)
            A.activation(al[:, :, :], al[:, :, :], ACT.Exp).then_inc(ready, 1)
            a.wait_ge(made, 6)
            A.activation(sel[:, :, :], self_[:, :, :], ACT.Copy).then_inc(ready, 1)

            def read_xz(u, k, j):
                a.wait_ge(xz_done, 4 * k + j + 1)
                dst, src = ((xpad[j][:, :, 3:], banks[j % 2][:, :].rearrange("p (s l) -> p s l", s=SPG)) if j < CC else
                            (zs[j - CC][u][:, :], banks[j % 2][:, :]))
                A.activation(dst, src, ACT.Copy).then_inc(xz_read, 1)

            def silus(u, k):
                a.wait_ge(xz_read, 4 * k + 4)
                for j in range(CC):
                    A.activation(zs[j][u][:, :], zs[j][u][:, :], ACT.Silu).then_inc(silu_z, 1)
                for j in range(CC):
                    a.wait_ge(conv, 8 * k + 4 * j + 4)
                    A.activation(xs[j][u][:, :], cv[j][:, :], ACT.Silu, bias=cb[:, j:j + 1]).then_inc(xs_ready, 1)

            def read_dbc(u, k):
                a.wait_ge(dbc_done, k + 1)
                A.activation(dbc[:, :], mb[:, :], ACT.Copy).then_inc(dbc_ready, 1)

            def next_part(u, k, q):
                a.wait_ge(rest_ready, 2 * k + q)
                A.activation(parts[u][32 * q + 32:P, :], rest[32 * q + 32:P, :], ACT.Copy
                             ).then_inc(split if q == 1 else parts_ready, 1)

            def read_dt(u, k, j):
                a.wait_ge(dt_done, CC * k + j + 1)
                A.activation(ra[j][:, :], banks[j][:, :], ACT.Relu, bias=dtb[:, j:j + 1])
                A.activation(ve[j][:, :], banks[j][:, :], ACT.Abs, bias=dtb[:, j:j + 1]).then_inc(dt_read, 1)

            def softplus(u, k):
                for j in range(CC):
                    a.wait_ge(dt_read, CC * k + j + 1)
                    A.activation(ve[j][:, :], ve[j][:, :], ACT.Exp, scale=-1.0).then_inc(exped, 1)
                for j in range(CC):
                    a.wait_ge(exped, CC * k + j + 1)
                    A.activation(ve[j][:, :], ve[j][:, :], ACT.Ln, bias=1.0).then_inc(soft, 1)

            def decays(u, k, s, n):
                a.wait_ge(b_done, n + 1)
                if not early(n, 2):
                    a.wait_ge(h_ready, 2 * n - 2)
                A.activation(bs[s % 2][:, :], bb[s % 2][:, :], ACT.Copy).then_inc(bs_ready, 1)
                if s == 0:
                    a.wait_ge(edge, CC * (k + 1))
                for j in range(CC):
                    A.activation(dA[j][s % 2][:, :], dl[j][u][:, :], ACT.Exp, scale=al[:, j, s:s + 1]
                                 ).then_inc(dA_ready, 1)

            def group(now, nxt):
                for s in range(N):
                    nx = after(s, now, nxt)
                    if nx:
                        decays(*nx)
                    if nxt:
                        _, u, k = nxt
                        if s == 2:
                            fr.act(a, k, u)
                        if s in (5, 7):
                            read_xz(u, k, s - 5)
                            read_xz(u, k, s - 4)
                        if s == 8:
                            silus(u, k)
                        if s == 10:
                            read_dbc(u, k)
                        if s in (11, 13):
                            next_part(u, k, (s - 9) // 2)
                        if s == 12:
                            read_dt(u, k, 0)
                            read_dt(u, k, 1)
                            softplus(u, k)

            fr.act(a, 0, 0)
            for j in range(4):
                read_xz(0, 0, j)
            silus(0, 0)
            read_dbc(0, 0)
            for q in (1, 2):
                next_part(0, 0, q)
            for j in range(CC):
                read_dt(0, 0, j)
            softplus(0, 0)
            a.wait_ge(ready, 3)
            decays(0, 0, 0, 0)
            weave(a, GROUPS, 2, group)

        @block.vector
        def _(v):
            V = nc.vector
            v.wait_ge(ready, 2)
            V.tensor_scalar(al[:, :, :], al[:, :, :], -1.0, None, ALU.mult).then_inc(ready, 1)
            v.wait_ge(made, 3)

            def convolve(k, j):
                v.wait_ge(xz_read, 4 * k + j + 1)
                c3 = cv[j][:, :].rearrange("p (s l) -> p s l", s=SPG)
                for q in range(4):
                    tap = xpad[j][:, :, q:q + SEQ]
                    if q == 0:
                        V.tensor_scalar(c3, tap, cw[:, j, 0:1], None, ALU.mult).then_inc(conv, 1)
                    else:
                        v.wait_ge(conv, 8 * k + 4 * j + q)
                        V.scalar_tensor_tensor(out=c3, in0=tap, scalar=cw[:, j, q:q + 1], in1=c3, op0=ALU.mult,
                                               op1=ALU.add).then_inc(conv, 1)

            def inputs(u, k, s, n):
                if s == 0:
                    v.wait_ge(du_ready, CC * k + 1)
                if not early(n, 2):
                    v.wait_ge(h_ready, 2 * n - 3)
                v.wait_ge(bs_ready, n + 1)
                V.tensor_tensor(db[0][s % 2][:, :], du[0][u][:, :], bs[s % 2][:, :], ALU.mult).then_inc(db0_ready, 1)

            def scan(n, s, j):
                v.wait_ge(dA_ready, 2 * n + j + 1)
                v.wait_ge(db1_ready if j else db0_ready, n + 1)
                if not early(n, 2):
                    v.wait_ge(hc_ready, 2 * n - 3 + j)
                V.tensor_tensor_scan(hh[j][s % 2][:, :], dA[j][s % 2][:, :], db[j][s % 2][:, :], 0.0, ALU.mult, ALU.add
                                     ).then_inc(h_ready, 1)

            def outputs(n, s, j):
                v.wait_ge(h_ready, 2 * n + j + 1)
                v.wait_ge(c_done, n + 1)
                if not early(n, 2):
                    v.wait_ge(summed, 2 * n - 3 + j)
                V.tensor_tensor(hc[j][s % 2][:, :], hh[j][s % 2][:, :], cbk[s % 2][:, :], ALU.mult
                                ).then_inc(hc_ready, 1)

            def gather(u, k):
                v.wait_ge(summed, N * CC * (k + 1))
                for j in range(CC):
                    V.scalar_tensor_tensor(out=yT[j][:, :], in0=xs[j][u][:, :], scalar=dd[:, j:j + 1], in1=yb[j][:, :],
                                           op0=ALU.mult, op1=ALU.add).then_inc(yy, 1)

            def add(u, k):
                v.wait_ge(o_done, k + 1)
                xt = tiles4(c.x, k)
                V.tensor_tensor(xt, xt, ob[:, :].rearrange("p (t d) -> p t d", t=TPG), ALU.add).then_inc(o_free, 1)

            def group(now, nxt):
                for s in range(N):
                    n = N * now[2] + s
                    nx = after(s, now, nxt)
                    for j in range(CC):
                        scan(n, s, j)
                    if s == 0 and not first(now[2]):
                        gather(1 - now[1], now[2] - 1)
                    if nx:
                        inputs(*nx)
                    for j in range(CC):
                        outputs(n, s, j)
                    if s == 3 and not first(now[2]):
                        add(1 - now[1], now[2] - 1)
                    if nxt:
                        _, u, k = nxt
                        if s == 0:
                            fr.dve_rows(v, k, u)
                        if s in (5, 6):
                            convolve(k, s - 5)

            fr.dve_start(v)
            fr.dve(v, 0, 0)
            for j in range(CC):
                convolve(0, j)
            inputs(0, 0, 0, 0)
            weave(v, GROUPS, 2, group)
            gather(1, GROUPS - 1)
            add(1, GROUPS - 1)

        @block.tensor
        def _(pe):
            T = nc.tensor
            pe.wait_ge(weights, 176)
            pe.wait_ge(ready, 2)

            def turn(u, k):
                if not first(k):
                    pe.wait_ge(dt_read, CC * k)
                fr.pe(pe, k, u)

            def xz(u, k, j):
                if j >= CC:
                    pe.wait_ge(xz_read, 4 * k + j - 1)
                elif j == 0:
                    pe.wait_ge(fr.xnT_ready, k + 1)
                elif not early(k, 2):
                    pe.wait_ge(o_free, k - 1)
                T.matmul(banks[j % 2][:, :], win[:, j * P:(j + 1) * P], fr.xnT[u][:, :], start=True, stop=True
                         ).then_inc(xz_done, 1)

            def x_proj(u, k):
                pe.wait_ge(xs_ready, CC * (k + 1))
                for j in range(CC):
                    m = T.matmul(mb[:, :], xpw[:, j, :], xs[j][u][:, :], start=(j == 0), stop=(j == CC - 1))
                m.then_inc(dbc_done, 1)

            def dt(u, k, j):
                pe.wait_ge(dbc_ready, k + 1)
                T.matmul(banks[j][:, :], dtw[:, j * P:(j + 1) * P], dbc[0:RK, :], start=True, stop=True).then_inc(dt_done, 1)

            def spread(u, k, s, n):
                if s == 0:
                    pe.wait_ge(parts_ready, k + 1)
                if not early(n, 2):
                    pe.wait_ge(bs_ready, n - 1)
                T.matmul(bb[s % 2][:, :], sel[:, s, :], parts[u][:, :], start=True, stop=True).then_inc(b_done, 1)

            def spread_c(u, k, s, n):
                if not early(n, 2):
                    pe.wait_ge(hc_ready, CC * n - CC)
                T.matmul(cbk[s % 2][:, :], sel[:, N + s, :], parts[u][:, :], start=True, stop=True).then_inc(c_done, 1)

            def output(u, k):
                pe.wait_ge(y_ready, CC * (k + 1))
                if not first(k):
                    pe.wait_ge(o_free, k)
                for t in range(TPG):
                    for j in range(CC):
                        m = T.matmul(ob[:, t * D:(t + 1) * D], yT[j][:, t * P:(t + 1) * P], wo[:, j, :],
                                     start=(j == 0), stop=(j == CC - 1))
                m.then_inc(o_done, 1)

            def group(now, nxt):
                for s in range(N):
                    n = N * now[2] + s
                    nx, nx2 = after(s, now, nxt), after(s + 1, now, nxt)
                    if nx2:
                        spread(*nx2)
                    if nx:
                        spread_c(*nx)
                    for j in range(CC):
                        pe.wait_ge(hc_ready, CC * n + j + 1)
                        if s == 0 and not first(now[2]):
                            pe.wait_ge(yy, CC * now[2] - 1 + j)
                        T.matmul(yb[j][:, :], c.ident[:, :], hc[j][s % 2][:, :], start=(s == 0), stop=(s == N - 1)
                                 ).then_inc(summed, 1)
                    if s == 1 and not first(now[2]):
                        output(1 - now[1], now[2] - 1)
                    if nxt:
                        _, u, k = nxt
                        if s == 0:
                            turn(u, k)
                        if s in (3, 5):
                            xz(u, k, s - 3)
                            xz(u, k, s - 2)
                        if s == 8:
                            x_proj(u, k)
                        if s == 10:
                            dt(u, k, 0)
                            dt(u, k, 1)

            turn(0, 0)
            for j in range(4):
                xz(0, 0, j)
            x_proj(0, 0)
            for j in range(CC):
                dt(0, 0, j)
            spread(0, 0, 0, 0)
            spread_c(0, 0, 0, 0)
            spread(0, 0, 1, 1)
            weave(pe, GROUPS, 2, group)
            output(1, GROUPS - 1)


def store(nc, c, out):
    with Phase(nc, "store") as ph:
        stored = ph.sem("stored")
        block = ph.block()

        @block.sync
        def _(sp):
            sp.dma_start(out.rearrange("(t p) d -> p t d", p=P), c.x[:, :, :]).then_inc(stored, 16)
            sp.wait_ge(stored, 16)


def stages(nc, c, w):
    return [
        lambda: moe64(nc, c, "l0f1", w),
        lambda: block_attention(nc, c, "l0a", w),
        lambda: moe64(nc, c, "l0f2", w),
        lambda: lowrank_ffn(nc, c, "l1f1", w),
        lambda: s4d(nc, c, "l1a", w),
        lambda: lowrank_ffn(nc, c, "l1f2", w),
        lambda: ternary_ffn(nc, c, "l2f1", w),
        lambda: window_attention(nc, c, "l2a", w),
        lambda: ternary_ffn(nc, c, "l2f2", w),
        lambda: gqa_moe(nc, c, "l3f1", w),
        lambda: mamba(nc, c, "l3a", w),
        lambda: gqa_moe(nc, c, "l3f2", w),
    ]


def program(nc, w, out, which=range(12)):
    with ExitStack() as ctx:
        c = Consts()

        def sb(name, shape, dt=F32):
            return ctx.enter_context(nc.sbuf_tensor(name, shape, dt))

        c.x = sb("x_state", [P, TILES, D])
        c.ident, c.mirror, c.ones, c.zero, c.below = (
            sb(n, [P, P]) for n in ("ident", "mirror", "ones", "zero", "below"))
        c.mark_v, c.mark_g, c.mark_a, c.mark_p = (
            ctx.enter_context(nc.semaphore(f"mark_{n}")) for n in ("vector", "gpsimd", "scalar", "tensor"))
        c.ident_b = sb("ident_b", [P, P], BF16)
        c.below_b, c.ones_b = sb("below_b", [P, P], BF16), sb("ones_b", [P, P], BF16)
        c.token_id, c.expert_id = sb("token_id", [P, TILES]), sb("expert_id", [P, 64])
        c.blank = sb("blank", [P, DUMPS, D + 64 + 1])
        c.mixtures, c.to_clear = {}, []
        for s, name, E in ((0, "l0f1", 64), (2, "l0f2", 64), (9, "l3f1", 8), (11, "l3f2", 8)):
            if s in which:
                c.mixtures[name] = Mixture(nc, ctx, name, E)
                c.to_clear.append(c.mixtures[name])
        setup(nc, c, w)
        todo = stages(nc, c, w)
        for s in which:
            todo[s]()
        store(nc, c, out)


def layouts(a):
    import numpy as np

    def t(m):
        return m.T

    def cols(v):
        return v.reshape(-1, P).T

    def row(v):
        return v.reshape(1, -1)

    def chunks(m):
        return m.reshape(-1, P, m.shape[-1]).transpose(1, 0, 2)

    def same(m):
        return m

    def four(m):
        m = m.reshape(m.shape[:-1] + (4, 1, 8))
        return np.broadcast_to(m, m.shape[:-2] + (4, 8)).reshape(m.shape[:-3] + (P,))

    plan = {
        "L0_attn_Wq": same, "L0_attn_Wk": same, "L0_attn_Wv": same, "L0_attn_Wo": same,
        "L0_attn_bq": cols, "L0_attn_bk": cols, "L0_attn_bv": row, "L0_attn_bo": row,
        "L0_ffn_wg": t, "L0_ffn_shared_w1": t, "L0_ffn_shared_w2": lambda m: chunks(m.T),
        "L0_ffn_expert_w1": lambda m: m.transpose(0, 2, 1),
        "L0_ffn_expert_w2": lambda m: m.transpose(0, 2, 1).reshape(64, 3, P, D).transpose(0, 2, 1, 3),
        "L1_attn_in_W": t, "L1_attn_in_b": row, "L1_attn_log_dt": cols, "L1_attn_C": lambda m: m.transpose(0, 2, 1),
        "L1_attn_log_A_real": same, "L1_attn_A_imag": same, "L1_attn_D_skip": cols,
        "L1_attn_glu_W": t, "L1_attn_glu_b": cols, "L1_attn_out_W": t, "L1_attn_out_b": row,
        "L1_ffn_U1": same, "L1_ffn_V1": same, "L1_ffn_b1": cols, "L1_ffn_U2": chunks, "L1_ffn_V2": same,
        "L1_ffn_b2": row,
        "L2_attn_Wq": t, "L2_attn_Wk": t, "L2_attn_Wv": t, "L2_attn_Wo": t, "L2_attn_global_token_indices": row,
        "L2_ffn_W1": t, "L2_ffn_b1": cols, "L2_ffn_W2": lambda m: chunks(m.T), "L2_ffn_b2": row,
        "L3_attn_ln_w": cols, "L3_attn_ln_b": cols, "L3_attn_in_proj_w": t,
        "L3_attn_conv_w": lambda m: m.reshape(2, P, 4).transpose(1, 0, 2), "L3_attn_conv_b": cols,
        "L3_attn_x_proj_w": lambda m: chunks(np.concatenate([m[:32], m[8:], m[8:], m[8:]]).T), "L3_attn_dt_proj_w": t, "L3_attn_dt_proj_b": cols,
        "L3_attn_A_log": chunks, "L3_attn_D": cols, "L3_attn_out_proj_w": lambda m: chunks(m.T),
        "L3_ffn_qw": same, "L3_ffn_qb": cols, "L3_ffn_kw": four, "L3_ffn_kb": lambda v: cols(four(v)), "L3_ffn_vw": four,
        "L3_ffn_vb": lambda v: row(four(v)), "L3_ffn_ow": same, "L3_ffn_ob": row, "L3_ffn_gate_w": same, "L3_ffn_w1": same,
        "L3_ffn_w2": lambda m: m.reshape(8, 2, P, D).transpose(0, 2, 1, 3),
        "L3_ffn_norm1_w": row, "L3_ffn_norm2_w": row,
    }
    out = {n: np.ascontiguousarray(f(np.asarray(a[n]))) for n, f in plan.items()}
    out["x"] = np.ascontiguousarray(np.asarray(a["L0_attn_src"]).reshape(TOKENS, D))
    return out


def kernel(**inputs):
    import numpy as np
    import concourse.bacc as bacc
    from concourse.bass_utils import run_bass_kernel_spmd

    nc = bacc.Bacc("TRN2", target_bir_lowering=False, num_devices=1)
    arrays, w = {}, {}
    for name, a in layouts(inputs).items():
        arrays[f"in_{name}"] = a
        w[name] = nc.dram_tensor(f"in_{name}", a.shape, mybir.dt.from_np(a.dtype), kind="ExternalInput").ap()
    out = nc.dram_tensor("out", (TOKENS, D), F32, kind="ExternalOutput").ap()
    program(nc, w, out)
    r = run_bass_kernel_spmd(nc, [arrays], core_ids=[0])
    return r.results[0]["out"].reshape(16, 256, D)
```
